# Optimizing a Trainium2 kernel written in Bass

```python
import numpy as np
import jax
import jax.numpy as jnp

def _softmax(x, axis=-1):
    return jax.nn.softmax(x, axis=axis)

def _gelu(x):
    return jax.nn.gelu(x, approximate=True)

def _silu(x):
    return jax.nn.silu(x)

def _sigmoid(x):
    return jax.nn.sigmoid(x)

def _layernorm(x, axis=-1, eps=1e-05):
    m = jnp.mean(x, axis=axis, keepdims=True)
    v = jnp.var(x, axis=axis, keepdims=True)
    return (x - m) / jnp.sqrt(v + eps)

def _scatter_add(tgt, idx, src, axis=0):
    return tgt.at[idx].add(src)

def _segment_sum(src, seg, n):
    return jax.ops.segment_sum(src, seg, n)
kernel_name = 'mk_gnn_resnorm_d4_gnn_r8_9682b7'

def setup_inputs(seed: int=0):
    np.random.seed(seed)
    _w = jnp.asarray

    def _rec_inputs():
        import jax
        import jax.numpy as jnp
        _gk = jax.random.key(seed)
        x = -0.0003713 + 1 * jax.random.normal(jax.random.fold_in(_gk, 1), (12500, 128), jnp.float32)
        src = jax.random.randint(jax.random.fold_in(_gk, 2), (200000,), 0, 12500, jnp.int32)
        dst = jax.random.randint(jax.random.fold_in(_gk, 3), (200000,), 0, 12500, jnp.int32)
        _o = jnp.argsort(dst, stable=True)
        src = src[_o]
        dst = dst[_o]
        return (x, src, dst)
    x, src, dst = _rec_inputs()

    def _L0_gnn_setup():
        import jax, jax.numpy as jnp
        import numpy as np
        N = 12500
        E = 100000
        D = 128
        NEG_SLOPE = 0.2
        EPS = 1e-16

        def gatv2_layer(x, src, dst, Wl, bl, Wr, br, att, bias):
            n = x.shape[0]
            xl = x @ Wl + bl
            xr = x @ Wr + br
            xj = xl[src]
            e = jax.nn.leaky_relu(xj + xr[dst], NEG_SLOPE)
            logits = e @ att
            m = jax.ops.segment_max(logits, dst, num_segments=n)
            ex = jnp.exp(logits - m[dst])
            denom = jax.ops.segment_sum(ex, dst, num_segments=n)
            alpha = ex / (denom[dst] + EPS)
            out = jax.ops.segment_sum(alpha[:, None] * xj, dst, num_segments=n)
            return out + bias
        key = jax.random.key(seed)
        ks = jax.random.split(key, 16)
        s = 1.0 / np.sqrt(D)
        inp = {'x': jax.random.normal(ks[0], (N, D), dtype=jnp.float32), 'edge_index': jax.random.randint(ks[1], (2, E), 0, N, dtype=jnp.int32)}
        names = ['Wl1', 'Wr1', 'att1', 'Wl2', 'Wr2', 'att2']
        shapes = [(D, D), (D, D), (D,), (D, D), (D, D), (D,)]
        for i, (nme, shp) in enumerate(zip(names, shapes)):
            inp[nme] = jax.random.normal(ks[2 + i], shp, dtype=jnp.float32) * s
        for nme in ['bl1', 'br1', 'bias1', 'bl2', 'br2', 'bias2']:
            inp[nme] = jnp.zeros((D,), dtype=jnp.float32)
        return inp
    _L0_gnn_all = _L0_gnn_setup()
    _L0_gnn_in = {k: v for k, v in _L0_gnn_all.items() if k in ('Wl1', 'bl1', 'Wr1', 'br1', 'att1', 'bias1', 'Wl2', 'bl2', 'Wr2', 'br2', 'att2', 'bias2')}
    del _L0_gnn_all

    def _L1_gnn_setup():
        import jax, jax.numpy as jnp
        import numpy as np
        N_NODES = 6250
        N_EDGES = 100000
        EMBED_DIM = 128
        key = jax.random.key(seed)
        ks = jax.random.split(key, 6)
        std = 1.0 / np.sqrt(EMBED_DIM)
        emb = jax.random.normal(ks[0], (N_NODES, EMBED_DIM), dtype=jnp.float32)
        edges = jax.random.randint(ks[1], (2, N_EDGES), 0, N_NODES, dtype=jnp.int64)
        w_weight = jax.random.uniform(ks[2], (EMBED_DIM, EMBED_DIM), dtype=jnp.float32, minval=-std, maxval=std)
        w_bias = jnp.zeros((EMBED_DIM,), dtype=jnp.float32)
        a_weight = jax.random.normal(ks[3], (2 * EMBED_DIM,), dtype=jnp.float32) * 0.05
        a_bias = jnp.zeros((1,), dtype=jnp.float32)
        trans_weight = jax.random.normal(ks[4], (EMBED_DIM, 2 * EMBED_DIM), dtype=jnp.float32) * 0.05
        trans_bias = jnp.zeros((EMBED_DIM,), dtype=jnp.float32)
        ln_gamma = jnp.ones((EMBED_DIM,), dtype=jnp.float32)
        ln_beta = jnp.zeros((EMBED_DIM,), dtype=jnp.float32)
        return {'emb': emb, 'edges': edges, 'w_weight': w_weight, 'w_bias': w_bias, 'a_weight': a_weight, 'a_bias': a_bias, 'trans_weight': trans_weight, 'trans_bias': trans_bias, 'ln_gamma': ln_gamma, 'ln_beta': ln_beta}
    _L1_gnn_all = _L1_gnn_setup()
    _L1_gnn_in = {k: v for k, v in _L1_gnn_all.items() if k in ('w_weight', 'w_bias', 'a_weight', 'a_bias', 'trans_weight', 'trans_bias', 'ln_gamma', 'ln_beta')}
    del _L1_gnn_all

    def _L2_gnn_setup():
        import jax, jax.numpy as jnp
        import numpy as np
        N_NODES = 12500
        N_EDGES = 200000
        D = 128
        LEAKY_ALPHA = 0.2
        ELU_ALPHA = 1.0

        def _elu(x, alpha):
            return jnp.where(x > 0, x, alpha * (jnp.exp(jnp.minimum(x, 0.0)) - 1.0))
        key = jax.random.key(seed)
        ks = jax.random.split(key, 8)
        s = 0.05
        atom_features = jax.random.normal(ks[0], (N_NODES, D), dtype=jnp.float32)
        W1 = jax.random.normal(ks[1], (1, 2 * D), dtype=jnp.float32) * s
        b1 = jnp.zeros((1,), dtype=jnp.float32)
        W2 = jax.random.normal(ks[2], (D, D), dtype=jnp.float32) * s
        b2 = jnp.zeros((D,), dtype=jnp.float32)
        w_ih = jax.random.normal(ks[3], (3 * D, D), dtype=jnp.float32) * s
        w_hh = jax.random.normal(ks[4], (3 * D, D), dtype=jnp.float32) * s
        b_ih = jnp.zeros((3 * D,), dtype=jnp.float32)
        b_hh = jnp.zeros((3 * D,), dtype=jnp.float32)
        edge_index = jax.random.randint(ks[5], (2, N_EDGES), 0, N_NODES, dtype=jnp.int64)
        return {'atom_features': atom_features, 'W1': W1, 'b1': b1, 'W2': W2, 'b2': b2, 'w_ih': w_ih, 'w_hh': w_hh, 'b_ih': b_ih, 'b_hh': b_hh, 'edge_index': edge_index}
    _L2_gnn_all = _L2_gnn_setup()
    _L2_gnn_in = {k: v for k, v in _L2_gnn_all.items() if k in ('W1', 'b1', 'W2', 'b2', 'w_ih', 'w_hh', 'b_ih', 'b_hh')}
    del _L2_gnn_all

    def _L3_gnn_setup():
        import jax, jax.numpy as jnp
        import numpy as np
        N_NODES = 6250
        N_EDGES = 100000
        IN_DIM = 128
        OUT_DIM = 128
        NUM_HEADS = 8
        HEAD_DIM = OUT_DIM // NUM_HEADS
        LN_EPS = 1e-05
        key = jax.random.key(seed)
        ks = jax.random.split(key, 8)

        def xavier(k, shape, fan_in, fan_out):
            a = float(np.sqrt(6.0 / (fan_in + fan_out)))
            return jax.random.uniform(k, shape, jnp.float32, -a, a)
        x = jax.random.normal(ks[0], (N_NODES, IN_DIM), jnp.float32)
        edge_index = jax.random.randint(ks[1], (2, N_EDGES), 0, N_NODES, jnp.int32)
        W_src = xavier(ks[2], (IN_DIM, OUT_DIM), IN_DIM, OUT_DIM)
        W_dst = xavier(ks[3], (IN_DIM, OUT_DIM), IN_DIM, OUT_DIM)
        attn = xavier(ks[4], (NUM_HEADS, HEAD_DIM), HEAD_DIM, NUM_HEADS)
        W_out = xavier(ks[5], (OUT_DIM, OUT_DIM), OUT_DIM, OUT_DIM)
        b_out = jnp.zeros((OUT_DIM,), jnp.float32)
        gamma = jnp.ones((OUT_DIM,), jnp.float32)
        beta = jnp.zeros((OUT_DIM,), jnp.float32)
        return {'x': x, 'edge_index': edge_index, 'W_src': W_src, 'W_dst': W_dst, 'attn': attn, 'W_out': W_out, 'b_out': b_out, 'gamma': gamma, 'beta': beta}
    _L3_gnn_all = _L3_gnn_setup()
    _L3_gnn_in = {k: v for k, v in _L3_gnn_all.items() if k in ('W_src', 'W_dst', 'attn', 'W_out', 'b_out', 'gamma', 'beta')}
    del _L3_gnn_all
    return {'x': x, 'src': src, 'dst': dst, 'L0_gnn_Wl1': _L0_gnn_in['Wl1'], 'L0_gnn_bl1': _L0_gnn_in['bl1'], 'L0_gnn_Wr1': _L0_gnn_in['Wr1'], 'L0_gnn_br1': _L0_gnn_in['br1'], 'L0_gnn_att1': _L0_gnn_in['att1'], 'L0_gnn_bias1': _L0_gnn_in['bias1'], 'L0_gnn_Wl2': _L0_gnn_in['Wl2'], 'L0_gnn_bl2': _L0_gnn_in['bl2'], 'L0_gnn_Wr2': _L0_gnn_in['Wr2'], 'L0_gnn_br2': _L0_gnn_in['br2'], 'L0_gnn_att2': _L0_gnn_in['att2'], 'L0_gnn_bias2': _L0_gnn_in['bias2'], 'L1_gnn_w_weight': _L1_gnn_in['w_weight'], 'L1_gnn_w_bias': _L1_gnn_in['w_bias'], 'L1_gnn_a_weight': _L1_gnn_in['a_weight'], 'L1_gnn_a_bias': _L1_gnn_in['a_bias'], 'L1_gnn_trans_weight': _L1_gnn_in['trans_weight'], 'L1_gnn_trans_bias': _L1_gnn_in['trans_bias'], 'L1_gnn_ln_gamma': _L1_gnn_in['ln_gamma'], 'L1_gnn_ln_beta': _L1_gnn_in['ln_beta'], 'L2_gnn_W1': _L2_gnn_in['W1'], 'L2_gnn_b1': _L2_gnn_in['b1'], 'L2_gnn_W2': _L2_gnn_in['W2'], 'L2_gnn_b2': _L2_gnn_in['b2'], 'L2_gnn_w_ih': _L2_gnn_in['w_ih'], 'L2_gnn_w_hh': _L2_gnn_in['w_hh'], 'L2_gnn_b_ih': _L2_gnn_in['b_ih'], 'L2_gnn_b_hh': _L2_gnn_in['b_hh'], 'L3_gnn_W_src': _L3_gnn_in['W_src'], 'L3_gnn_W_dst': _L3_gnn_in['W_dst'], 'L3_gnn_attn': _L3_gnn_in['attn'], 'L3_gnn_W_out': _L3_gnn_in['W_out'], 'L3_gnn_b_out': _L3_gnn_in['b_out'], 'L3_gnn_gamma': _L3_gnn_in['gamma'], 'L3_gnn_beta': _L3_gnn_in['beta']}

def reference(x, src, dst, L0_gnn_Wl1, L0_gnn_bl1, L0_gnn_Wr1, L0_gnn_br1, L0_gnn_att1, L0_gnn_bias1, L0_gnn_Wl2, L0_gnn_bl2, L0_gnn_Wr2, L0_gnn_br2, L0_gnn_att2, L0_gnn_bias2, L1_gnn_w_weight, L1_gnn_w_bias, L1_gnn_a_weight, L1_gnn_a_bias, L1_gnn_trans_weight, L1_gnn_trans_bias, L1_gnn_ln_gamma, L1_gnn_ln_beta, L2_gnn_W1, L2_gnn_b1, L2_gnn_W2, L2_gnn_b2, L2_gnn_w_ih, L2_gnn_w_hh, L2_gnn_b_ih, L2_gnn_b_hh, L3_gnn_W_src, L3_gnn_W_dst, L3_gnn_attn, L3_gnn_W_out, L3_gnn_b_out, L3_gnn_gamma, L3_gnn_beta):
    import jax
    import jax.numpy as jnp

    def _L0_gnn_ref(x, edge_index, Wl1, bl1, Wr1, br1, att1, bias1, Wl2, bl2, Wr2, br2, att2, bias2):
        import jax, jax.numpy as jnp
        import numpy as np
        N = 12500
        E = 100000
        D = 128
        NEG_SLOPE = 0.2
        EPS = 1e-16

        def gatv2_layer(x, src, dst, Wl, bl, Wr, br, att, bias):
            n = x.shape[0]
            xl = x @ Wl + bl
            xr = x @ Wr + br
            xj = xl[src]
            e = jax.nn.leaky_relu(xj + xr[dst], NEG_SLOPE)
            logits = e @ att
            m = jax.ops.segment_max(logits, dst, num_segments=n)
            ex = jnp.exp(logits - m[dst])
            denom = jax.ops.segment_sum(ex, dst, num_segments=n)
            alpha = ex / (denom[dst] + EPS)
            out = jax.ops.segment_sum(alpha[:, None] * xj, dst, num_segments=n)
            return out + bias
        src = edge_index[0]
        dst = edge_index[1]
        h = gatv2_layer(x, src, dst, Wl1, bl1, Wr1, br1, att1, bias1)
        h = jax.nn.relu(h)
        out = gatv2_layer(h, src, dst, Wl2, bl2, Wr2, br2, att2, bias2)
        return out

    def _L1_gnn_ref(emb, edges, w_weight, w_bias, a_weight, a_bias, trans_weight, trans_bias, ln_gamma, ln_beta):
        import jax, jax.numpy as jnp
        import numpy as np
        N_NODES = 6250
        N_EDGES = 100000
        EMBED_DIM = 128
        bsz, d = emb.shape
        e_dst, e_src = (edges[0], edges[1])
        s = emb @ w_weight.T + w_bias
        a1, a2 = (a_weight[:d], a_weight[d:])
        p1 = s @ a1
        p2 = s @ a2
        score = p1[e_dst] + p2[e_src] + a_bias[0]
        attn = jnp.exp(jnp.where(score > 0, score, 0.2 * score))
        denom = jax.ops.segment_sum(attn, e_dst, num_segments=bsz)
        msg = attn[:, None] * emb[e_src]
        agg = jax.ops.segment_sum(msg, e_dst, num_segments=bsz)
        agg = agg / (denom[:, None] + 1e-20)
        h = jnp.concatenate([emb, agg], axis=-1) @ trans_weight.T + trans_bias
        mu = jnp.mean(h, axis=-1, keepdims=True)
        var = jnp.mean(jnp.square(h - mu), axis=-1, keepdims=True)
        h = (h - mu) * jax.lax.rsqrt(var + 1e-05) * ln_gamma + ln_beta
        return h

    def _L2_gnn_ref(atom_features, W1, b1, W2, b2, w_ih, w_hh, b_ih, b_hh, edge_index):
        import jax, jax.numpy as jnp
        import numpy as np
        N_NODES = 12500
        N_EDGES = 200000
        D = 128
        LEAKY_ALPHA = 0.2
        ELU_ALPHA = 1.0

        def _elu(x, alpha):
            return jnp.where(x > 0, x, alpha * (jnp.exp(jnp.minimum(x, 0.0)) - 1.0))
        N, d = atom_features.shape
        src = edge_index[0]
        dst = edge_index[1]
        nft = atom_features @ W2.T + b2
        w_d = W1[0, :d]
        w_s = W1[0, d:]
        logit = atom_features @ w_d
        logit_src = atom_features @ w_s
        score = logit[dst] + logit_src[src] + b1[0]
        score = jnp.where(score > 0, score, LEAKY_ALPHA * score)
        m = jax.ops.segment_max(score, dst, num_segments=N)
        m_safe = jnp.where(jnp.isfinite(m), m, 0.0)
        e = jnp.exp(score - m_safe[dst])
        denom = jax.ops.segment_sum(e, dst, num_segments=N)
        attn = e / denom[dst]
        msg = attn[:, None] * nft[src]
        transform = jax.ops.segment_sum(msg, dst, num_segments=N)
        context = _elu(transform, ELU_ALPHA)
        deg = jax.ops.segment_sum(jnp.ones_like(score), dst, num_segments=N)
        out_emb = jnp.where(deg[:, None] > 0, context, atom_features)
        gi = out_emb @ w_ih.T + b_ih
        gh = atom_features @ w_hh.T + b_hh
        gi_r, gi_z, gi_n = jnp.split(gi, 3, axis=-1)
        gh_r, gh_z, gh_n = jnp.split(gh, 3, axis=-1)
        r = jax.nn.sigmoid(gi_r + gh_r)
        z = jax.nn.sigmoid(gi_z + gh_z)
        n = jnp.tanh(gi_n + r * gh_n)
        h_new = (1.0 - z) * n + z * atom_features
        return h_new

    def _L3_gnn_ref(x, edge_index, W_src, W_dst, attn, W_out, b_out, gamma, beta):
        import jax, jax.numpy as jnp
        import numpy as np
        N_NODES = 6250
        N_EDGES = 100000
        IN_DIM = 128
        OUT_DIM = 128
        NUM_HEADS = 8
        HEAD_DIM = OUT_DIM // NUM_HEADS
        LN_EPS = 1e-05
        N = x.shape[0]
        H, D = attn.shape
        src, dst = (edge_index[0], edge_index[1])
        h_src = (x @ W_src).reshape(N, H, D)
        h_dst = (x @ W_dst).reshape(N, H, D)
        h_src_e = h_src[src]
        e = jax.nn.leaky_relu(h_src_e + h_dst[dst], 0.2)
        s = jnp.einsum('ehd,hd->eh', e, attn)
        m = jax.ops.segment_max(s, dst, num_segments=N)
        exp = jnp.exp(s - m[dst])
        denom = jax.ops.segment_sum(exp, dst, num_segments=N)
        alpha = exp / (denom[dst] + 1e-08)
        msg = (h_src_e * alpha[..., None]).reshape(-1, H * D)
        out = jax.ops.segment_sum(msg, dst, num_segments=N)
        out = out @ W_out + b_out
        out = out + x
        mu = jnp.mean(out, axis=-1, keepdims=True)
        var = jnp.var(out, axis=-1, keepdims=True)
        out = (out - mu) * jax.lax.rsqrt(var + LN_EPS) * gamma + beta
        return out
    edge_index = jnp.stack([src, dst])
    x = _layernorm(x + _L0_gnn_ref(x, edge_index, L0_gnn_Wl1, L0_gnn_bl1, L0_gnn_Wr1, L0_gnn_br1, L0_gnn_att1, L0_gnn_bias1, L0_gnn_Wl2, L0_gnn_bl2, L0_gnn_Wr2, L0_gnn_br2, L0_gnn_att2, L0_gnn_bias2), axis=-1)
    x = _layernorm(x + _L1_gnn_ref(x, edge_index, L1_gnn_w_weight, L1_gnn_w_bias, L1_gnn_a_weight, L1_gnn_a_bias, L1_gnn_trans_weight, L1_gnn_trans_bias, L1_gnn_ln_gamma, L1_gnn_ln_beta), axis=-1)
    x = _layernorm(x + _L2_gnn_ref(x, L2_gnn_W1, L2_gnn_b1, L2_gnn_W2, L2_gnn_b2, L2_gnn_w_ih, L2_gnn_w_hh, L2_gnn_b_ih, L2_gnn_b_hh, edge_index), axis=-1)
    x = _layernorm(x + _L3_gnn_ref(x, edge_index, L3_gnn_W_src, L3_gnn_W_dst, L3_gnn_attn, L3_gnn_W_out, L3_gnn_b_out, L3_gnn_gamma, L3_gnn_beta), axis=-1)
    return x

_drawn_inputs = setup_inputs


def setup_inputs(seed=0):
    import zlib

    import numpy as np

    out = dict(_drawn_inputs(seed))
    spreads = {'L0_gnn_bl1': (0.0, 0.1),
     'L0_gnn_br1': (0.0, 2.0),
     'L0_gnn_bias1': (0.0, 0.1),
     'L0_gnn_bl2': (0.0, 0.1),
     'L0_gnn_br2': (0.0, 2.0),
     'L0_gnn_bias2': (0.0, 0.1),
     'L1_gnn_w_bias': (0.0, 2.0),
     'L1_gnn_trans_bias': (0.0, 0.1),
     'L1_gnn_ln_gamma': (1.0, 0.2),
     'L1_gnn_ln_beta': (0.0, 0.1),
     'L2_gnn_b2': (0.0, 0.439),
     'L2_gnn_b_ih': (0.0, 0.1),
     'L2_gnn_b_hh': (0.0, 0.356),
     'L3_gnn_b_out': (0.0, 0.1),
     'L3_gnn_gamma': (1.0, 0.2),
     'L3_gnn_beta': (0.0, 0.1)}
    factors = {'L0_gnn_Wr1': 4.338,
     'L0_gnn_Wr2': 8.0,
     'L0_gnn_att2': 7.499,
     'L2_gnn_W1': 5.206,
     'L1_gnn_w_weight': 6.076}
    for name, (base, spread) in spreads.items():
        noise = np.random.default_rng([zlib.crc32(name.encode()), seed]).standard_normal(out[name].shape)
        drawn = base * np.exp(spread * noise) if base else spread * noise
        out[name] = jnp.asarray(drawn.astype(out[name].dtype))
    for name, factor in factors.items():
        out[name] = (out[name] * factor).astype(out[name].dtype)
    return out
```

```python
from contextlib import ExitStack

import concourse.bass as bass
from concourse import mybir

F32 = mybir.dt.float32
BF16 = mybir.dt.bfloat16
I32 = mybir.dt.int32
ALU = mybir.AluOpType
ACT = mybir.ActivationFunctionType
AX = mybir.AxisListType

P = 128
NEG = -1.0e30
SLOPE = 0.2
LN_EPS = 1e-5
G = 16
U = 4
CH = 4
NCH = G // CH
AW = 136
XW = 130
NSUM = 4
NBB = 7


def view(ap, free):
    return bass.AP(ap.tensor, ap.offset, [tuple(ap.ap[0])] + [tuple(f) for f in free])


class Done:

    def __init__(self, sem, value):
        self.sem, self.value = sem, value


class Program:
    ENGINES = ("pe", "act", "dve", "pool", "sp")
    DMA_RING = 8

    def __init__(self, nc, ctx):
        self.nc, self.ctx = nc, ctx
        self.queue = {e: [] for e in self.ENGINES}
        self.stage("start")
        self.ring = {e: [self.sem(f"{e}_dma{n}") for n in range(self.DMA_RING)] for e in ("sp", "pool")}
        self.ring_n = {e: 0 for e in ("sp", "pool")}
        self.anchor = self.sem("wait_anchor")

    def sem(self, name):
        return self.ctx.enter_context(self.nc.semaphore(name))

    def stage(self, name):
        self.name = name
        self.done_sem = {}
        self.count = {e: 0 for e in self.ENGINES}

    def engine_sem(self, e):
        if e not in self.done_sem:
            self.done_sem[e] = self.sem(f"{self.name}_{e}_done")
        return self.done_sem[e]

    def add(self, e, fn, after=()):
        sem = self.engine_sem(e)
        self.count[e] += 1
        waits = list(flat(after))

        def emit(eng, last):
            for w in waits:
                if last.get(id(w.sem), 0) < w.value:
                    eng.wait_ge(w.sem, w.value)
                    last[id(w.sem)] = w.value
            fn(eng).then_inc(sem, 1)

        self.queue[e].append(emit)
        return Done(sem, self.count[e])

    def dma(self, e, fn, after=()):
        n = self.ring_n[e]
        self.ring_n[e] += 1
        sem, turn = self.ring[e][n % self.DMA_RING], n // self.DMA_RING
        waits = list(flat(after)) + ([Done(sem, 16 * turn)] if turn else [])

        def emit(eng, last):
            for w in waits:
                if last.get(id(w.sem), 0) < w.value:
                    eng.wait_ge(w.sem, w.value)
                    last[id(w.sem)] = w.value
            fn(eng).then_inc(sem, 16)

        self.queue[e].append(emit)
        return Done(sem, 16 * (turn + 1))

    def play(self, e, eng):
        last = {}
        for emit in self.queue[e]:
            emit(eng, last)


def flat(x):
    if isinstance(x, (Done, tuple)) and not isinstance(x, list) and (isinstance(x, Done)):
        yield x
        return
    for y in x:
        if y is None:
            continue
        if isinstance(y, Done):
            yield y
        else:
            yield from flat(y)


class Op:

    def __init__(self, e, fn, after, lag, anchored):
        self.e, self.fn, self.after, self.lag, self.anchored = e, fn, after, lag, anchored
        self.counted = False


class SlotDma(Op):

    def __init__(self, e, fn, after, sems, base, gain):
        super().__init__(e, fn, after, 0, True)
        self.sems, self.base, self.gain = sems, base, gain


class Loop:

    PEELED = 2 * U

    def __init__(self, prog, n):
        self.prog, self.n, self.ops = prog, n, []
        assert n % U == 0 and n > self.PEELED

    def op(self, e, fn, after=(), lag=0, anchored=False):
        o = Op(e, fn, [(a, 0) if isinstance(a, Op) else a for a in after if a is not None], lag, anchored)
        self.ops.append(o)
        return o

    def slot_dma(self, e, fn, after, sems, base, gain):
        o = SlotDma(e, fn, [(a, 0) if isinstance(a, Op) else a for a in after], sems, base, gain)
        self.ops.append(o)
        return o

    def close(self):
        prog = self.prog
        for o in self.ops:
            for p, _ in o.after:
                if not isinstance(p, SlotDma):
                    p.counted = True
        per, first, tail = {}, {}, {}
        for o in self.ops:
            if isinstance(o, SlotDma) or not o.counted:
                continue
            per[o.e] = per.get(o.e, 0) + 1
            o.pos = per[o.e]
            if o.lag == 0:
                first[o.e] = first.get(o.e, 0) + 1
                o.pos_first = first[o.e]
            else:
                tail[o.e] = tail.get(o.e, 0) + 1
                o.pos_tail = tail[o.e]
        self.per, self.first, self.tail = per, first, tail
        self.sems = {e: prog.engine_sem(e) for e in per}
        for e in prog.ENGINES:
            prog.queue[e].append(lambda eng, last, e=e: self.play(e, eng, last))
        for e in per:
            prog.count[e] += first.get(e, 0) + per[e] * (self.n - 1) + tail.get(e, 0)

    def last(self, o):
        return Done(self.sems[o.e], self.first.get(o.e, 0) + self.per[o.e] * (self.n - 1) + o.pos_tail)

    def value(self, p, turn):
        if turn < 0 or (turn == 0 and p.lag == 1) or (turn == self.n and p.lag == 0):
            return None
        if turn == 0:
            return p.pos_first
        at = self.first.get(p.e, 0) + self.per[p.e] * (turn - 1)
        return at + (p.pos_tail if turn == self.n else p.pos)

    def play(self, e, eng, last):
        ops = [o for o in self.ops if o.e == e]
        if not ops:
            return
        prog = self.prog
        seen = {}

        def run(o, i, u, reg, j):
            for p, d in o.after:
                if isinstance(p, SlotDma):
                    sem = p.sems[(u - d) % U]
                    if reg is None:
                        if i - d < 0 or (i == self.n and d == 0):
                            continue
                        const, step = p.base + p.gain * ((i - d) // U + 1), 0
                    else:
                        const, step = p.base + p.gain * ((u - d) // U + 1), p.gain
                else:
                    sem = self.sems[p.e]
                    if reg is None:
                        const, step = self.value(p, i - d), 0
                        if const is None:
                            continue
                    else:
                        const = self.first.get(p.e, 0) + self.per[p.e] * (u - d - 1) + p.pos
                        step = self.per[p.e] * U
                key = id(sem)
                if key in seen and seen[key] >= const:
                    continue
                seen[key] = const
                if reg is None:
                    eng.wait_ge(sem, const)
                else:
                    eng.wait_ge(sem, j * step + const)
                    if o.anchored:
                        eng.sem_inc(prog.anchor, 1)
            ins = o.fn(eng, u, i)
            if isinstance(o, SlotDma):
                return
            if o.counted:
                ins.then_inc(self.sems[e], 1)

        for i in range(self.PEELED):
            for o in ops:
                if not (i == 0 and o.lag == 1):
                    run(o, i, i % U, None, None)
        seen.clear()
        with eng.Fori(self.PEELED // U, self.n // U) as j:
            for u in range(U):
                for o in ops:
                    run(o, j * U + u, u, True, j)
        seen.clear()
        for o in ops:
            if o.lag == 1:
                run(o, self.n, self.n % U, None, None)
        last.clear()


def build(nc, a, out):
    N = a["x"].shape[0]
    T = a["src"].shape[0]
    NB = -(-N // P)
    T_REAL = a["t_real"]
    SC = -(-(T_REAL + NB) // P)
    S = SC * P
    NG = S // G
    NEED_PAD = NB * P - N
    assert T == S and NG % U == 0 and NB % NBB == 0
    GC = P // G

    def dram(name, shape, dt=F32):
        return nc.dram_tensor(name, shape, dt).ap()

    ET = 5 * G
    edge_tab = dram("edge_tab", (NG, P, ET))
    onehot_tab = dram("onehot_tab", (3, S * P), BF16)
    source_tab = dram("source_tab", (4, S * P), BF16)
    step_tab = dram("step_tab", (S, 2 * P + 2))
    col_tab = dram("col_tab", (3 * SC, P))
    R1, R8 = 2 * G + 1 + G, 8 * (2 * G + 1) + G
    row_tab1 = dram("row_tab1", (NG, R1))
    row_tab8 = dram("row_tab8", (NG, R8))
    gather_a = dram("gather_a", (NB * P, P))
    gather_b = dram("gather_b", (NB * P, P))
    gather_c = dram("gather_c", (NB * P, P))
    scatter_s = [dram(f"scatter_s{k}", (NB * P + P, XW)) for k in range(NSUM)]
    gather_s2 = dram("gather_s2", (NB * P, P + 1))
    res = [dram(f"residual{n}", (NB * P, P)) for n in range(2)]

    with ExitStack() as ctx:
        prog = Program(nc, ctx)
        add, dma = prog.add, prog.dma

        def sb(name, shape, dt=F32):
            return ctx.enter_context(nc.sbuf_tensor(name, shape, dt))

        bank = [ctx.enter_context(nc.psum_tensor(f"bank{n}", [P, 512], F32)) for n in range(8)]

        ident = sb("ident", [P, P])
        iota = sb("iota", [P, P])
        ones = sb("ones", [P, P])
        oh_w = sb("oh_w", [5, P], BF16)
        minus_half = sb("minus_half", [P, NBB])
        agg = sb("agg", [P, NB, AW])
        dst_side = sb("dst_side", [P, max(NB, 64), P])
        dst_score = sb("dst_score", [P, NB])
        rows = sb("rows", [P, U, G, XW])
        lrelu = sb("lrelu", [P, 2, CH * P])
        oh_t = sb("oh_t", [P, 2, CH * P])
        oh_e = sb("oh_e", [P, 8, P])
        xw = sb("xw", [P, 2, CH * AW])
        edge_sb = sb("edge_sb", [P, U, ET])
        oh_ws = sb("oh_ws", [6, 2 * P], BF16)
        dump_row = sb("dump_row", [P, 1])
        oh_rows = sb("oh_rows", [5, U, G * P], BF16)
        step_sb = sb("step_sb", [P, U, 2 * P + 2])
        row_sb = sb("row_sb", [1, U, R8])
        param = sb("param", [P, 12 * P])
        att = sb("att", [P, P])
        logit = sb("logit", [P, P])
        masked = sb("masked", [P, P])
        seg_fwd = sb("seg_fwd", [P, P])
        seg_max = sb("seg_max", [P, P])
        run_max = sb("run_max", [P, P])
        shifted = sb("shifted", [P, P])
        weight = sb("weight", [P, 2, P])
        rescale = sb("rescale", [P, 2, P])
        decay_m = sb("decay_m", [P, P])
        carry = sb("carry", [1, 8 * (G + 1)])
        carry_in = sb("carry_in", [1, 8 * (G + 1)])
        cin_row = sb("cin_row", [1, P])
        cin = sb("cin", [P, 4])
        acc_tmp = sb("acc_tmp", [P, 2, AW])
        stats = sb("stats", [P, NBB, 6])
        moments = sb("moments", [P, NBB, 2])
        rstd = sb("rstd", [P, 2, NBB])
        recip = sb("recip", [P, 8 * NBB])
        col3 = sb("col3", [P, 3 * SC])

        s_tab = [prog.sem(f"tables_in_slot{u}") for u in range(U)]
        s_gat = [prog.sem(f"rows_in_slot{u}") for u in range(U)]
        tab_base = [0]
        gat_base = [0]

        prog.stage("prep")
        ld_id = dma("sp", lambda e: e.dma_start(ident[:, :], a["c_ident"]))
        ld_iota = dma("sp", lambda e: e.dma_start(iota[:, :], a["c_iota"]))
        ld_ohw = dma("sp", lambda e: e.dma_start(oh_w[:, :], a["c_ohw"]))
        ld_ohs = dma("sp", lambda e: e.dma_start(oh_ws[:, :], a["c_ohs"]))
        ld_dump = dma("sp", lambda e: e.dma_start(dump_row[:, :], a["c_dump"]))
        big1 = agg[:, :, :].rearrange("p a b -> p (a b)")
        big2 = dst_side[:, :, :].rearrange("p a b -> p (a b)")
        pool_rows = rows[:, :, :, :].rearrange("p a b c -> p (a b c)")
        step_no = col3[:, 0:SC]
        ld_sn = dma("sp", lambda e: e.dma_start(pool_rows[:, 0:SC], a["c_steps"]))
        first_i = pool_rows[:, 32:32 + SC].bitcast(I32)

        def load_first(e):
            with nc.allow_non_contiguous_dma(reason="first node of each tile"):
                return e.dma_start(first_i, a["dst"][:, 0:1].rearrange("(c p) o -> p (c o)", p=P))
        ld_first = dma("sp", load_first)
        m_ones = add("dve", lambda e: e.memset(ones[:, :], 1.0))
        m_half = add("dve", lambda e: e.memset(minus_half[:, :], -0.5))
        m_oh = add("dve", lambda e: e.memset(oh_rows[:, :, :], 1.0))
        m_rows = None
        fb = pool_rows[:, 64:64 + SC]
        fbi = pool_rows[:, 96:96 + SC].bitcast(I32)
        keyc = pool_rows[:, 128:128 + SC]
        snum = pool_rows[:, 0:SC]
        tcol = pool_rows[:, 160:160 + SC]
        tcoli = sb("tcoli", [P, SC], I32)
        bcol = pool_rows[:, 192:192 + SC]
        b128 = pool_rows[:, 224:224 + SC]
        h = add("dve", lambda e: e.tensor_single_scalar(fbi, first_i, 7, ALU.arith_shift_right), [ld_first])
        h = add("dve", lambda e: e.tensor_copy(fb, fbi), [h])
        key_done = add("dve", lambda e: e.tensor_tensor(keyc, fb, snum, ALU.add), [h, ld_sn])
        key = big2[:, 0:S]
        compare = big2[:, S:2 * S]
        kcol = big2[:, 2 * S:2 * S + SC * P]
        spread = []
        for c in range(SC):
            spread.append(add("dve", lambda e, c=c: e.tensor_scalar(kcol[:, c * P:(c + 1) * P], ones[:, :],
                                                                  keyc[:, c:c + 1], None, ALU.mult), [key_done, m_ones]))
        key_copied = []
        for c in range(SC):
            mm = add("pe", lambda e, c=c: e.matmul(bank[c % 8][:, 0:P], kcol[:, c * P:(c + 1) * P], ident[:, :],
                                                 start=True, stop=True),
                     [spread[c], ld_id, key_copied[c - 8:c - 7] if c >= 8 else []])
            key_copied.append(add("act", lambda e, c=c: e.copy(key[:, c * P:(c + 1) * P], bank[c % 8][:, 0:P]), [mm]))
        last = None
        for c in range(SC):
            h = add("dve", lambda e, c=c: e.tensor_scalar(compare[:, 1:], key[:, 1:], snum[:, c:c + 1], None, ALU.is_le),
                    [key_copied, last])
            last = add("dve", lambda e, c=c: e.tensor_reduce(tcol[:, c:c + 1], compare[:, 1:], AX.X, ALU.add), [h])
        t_int = add("dve", lambda e: e.tensor_copy(tcoli[:, :], tcol), [last])
        h = add("dve", lambda e: e.tensor_tensor(bcol, snum, tcol, ALU.subtract), [last])
        blk_done = add("dve", lambda e: e.tensor_scalar(bcol, bcol, float(NB - 1), None, ALU.min), [h])
        b128_done = add("dve", lambda e: e.tensor_scalar(b128, bcol, float(P), None, ALU.mult), [blk_done])
        c3b = add("dve", lambda e: e.tensor_copy(col3[:, 0:SC], bcol), [blk_done])

        NR = 2
        base = 256
        W1 = 2 * P + 2

        def tile_set(k):
            o = base + k * 2560
            f = lambda n, w: pool_rows[:, o + n:o + n + w]
            return dict(di=f(0, P).bitcast(I32), si=f(P, P).bitcast(I32), d=f(2 * P, P), s=f(3 * P, P),
                        rel=f(4 * P, P), sq=f(5 * P, P), sqi=f(6 * P, P).bitcast(I32), lo=f(7 * P, P),
                        st=f(8 * P, W1), hl=f(8 * P + W1, 3 * P // 2).bitcast(BF16),
                        qi=f(12 * P, P).bitcast(I32), q=f(13 * P, P), r=f(14 * P, P), rr=f(15 * P, P),
                        rri=f(16 * P, P).bitcast(I32), rlo=f(17 * P, P), sl=f(18 * P, 2 * P).bitcast(BF16))
        edge_stage = big1[:, 0:NG * ET].rearrange("p (g k) -> p g k", k=ET)
        mtmp = big2[:, 3 * S:3 * S + P]
        prev = [None, None]
        st_saved = []
        edge_done = []
        relT_free = None
        for c in range(SC):
            t = tile_set(c % NR)
            g_d = dma("pool", lambda e, t=t, c=c: e.indirect_dma_start(
                t["di"], None, a["dst"], bass.IndirectOffsetOnAxis(ap=tcoli[:, c:c + 1], axis=0)), [t_int, prev[c % NR]])
            g_s = dma("pool", lambda e, t=t, c=c: e.indirect_dma_start(
                t["si"], None, a["src"], bass.IndirectOffsetOnAxis(ap=tcoli[:, c:c + 1], axis=0)), [t_int, prev[c % NR]])
            d_f = add("dve", lambda e, t=t: e.tensor_copy(t["d"], t["di"]), [g_d])
            s_f = add("dve", lambda e, t=t: e.tensor_copy(t["s"], t["si"]), [g_s])
            h = add("dve", lambda e, t=t, c=c: e.tensor_scalar(t["rel"], t["d"], b128[:, c:c + 1], float(P),
                                                              ALU.subtract, ALU.min), [d_f, b128_done])
            rel = add("dve", lambda e, t=t: e.tensor_scalar(t["rel"], t["rel"], -1.0, None, ALU.max), [h])
            p1 = add("dve", lambda e, t=t: e.memset(t["st"][:, 0:P + 1], NEG), [prev[c % NR]])
            p2 = add("dve", lambda e, t=t: e.tensor_tensor(t["st"][:, 1:P], t["d"][:, 1:P], t["d"][:, 0:P - 1],
                                                           ALU.not_equal), [p1, d_f])
            p3 = add("dve", lambda e, t=t: e.tensor_scalar(t["st"][:, 1:P], t["st"][:, 1:P], NEG, None, ALU.mult), [p2])
            p4 = add("dve", lambda e, t=t: e.tensor_scalar(t["st"][:, P + 1:2 * P + 1], t["d"], t["d"][:, 0:1], NEG,
                                                           ALU.not_equal, ALU.mult), [d_f])
            p5 = add("dve", lambda e, t=t: e.tensor_copy(t["st"][:, 2 * P + 1:2 * P + 2], t["rel"][:, 0:1]), [rel])
            st = dma("sp", lambda e, t=t, c=c: e.dma_start(step_tab[c * P:(c + 1) * P, :], t["st"]), [p3, p4, p5])
            h = add("dve", lambda e, t=t: e.tensor_tensor(t["sq"], t["rel"], t["rel"], ALU.mult), [rel])
            h = add("dve", lambda e, t=t: e.tensor_copy(t["sqi"], t["sq"]), [h])
            h = add("dve", lambda e, t=t: e.tensor_single_scalar(t["sqi"], t["sqi"], 255, ALU.bitwise_and), [h])
            h = add("dve", lambda e, t=t: e.tensor_copy(t["lo"], t["sqi"]), [h])
            q1 = add("dve", lambda e, t=t: e.tensor_tensor(t["hl"][:, 0:P], t["sq"], t["lo"], ALU.subtract), [h])
            q2 = add("dve", lambda e, t=t: e.tensor_copy(t["hl"][:, P:2 * P], t["lo"]), [h])
            q3 = add("dve", lambda e, t=t: e.tensor_copy(t["hl"][:, 2 * P:3 * P], t["rel"]), [rel])
            oh = dma("sp", lambda e, t=t, c=c: e.dma_start(
                onehot_tab[:, c * P * P:(c + 1) * P * P].rearrange("k (p n) -> p k n", p=P),
                t["hl"].rearrange("p (k n) -> p k n", k=3)), [q1, q2, q3])
            c1 = add("dve", lambda e, t=t, c=c: e.tensor_copy(col3[:, SC + c:SC + c + 1], t["d"][:, 0:1]), [d_f])
            c2 = add("dve", lambda e, t=t, c=c: e.tensor_copy(col3[:, 2 * SC + c:2 * SC + c + 1], t["d"][:, P - 1:P]), [d_f])
            qa = add("dve", lambda e, t=t: e.tensor_single_scalar(t["qi"], t["si"], 7, ALU.arith_shift_right), [g_s])
            qf = add("dve", lambda e, t=t: e.tensor_copy(t["q"], t["qi"]), [qa])
            h = add("dve", lambda e, t=t: e.scalar_tensor_tensor(t["r"], t["q"], -float(P), t["s"], ALU.mult, ALU.add), [qf, s_f])
            rf = h
            h = add("dve", lambda e, t=t: e.tensor_tensor(t["rr"], t["r"], t["r"], ALU.mult), [h])
            h = add("dve", lambda e, t=t: e.tensor_copy(t["rri"], t["rr"]), [h])
            h = add("dve", lambda e, t=t: e.tensor_single_scalar(t["rri"], t["rri"], 255, ALU.bitwise_and), [h])
            h = add("dve", lambda e, t=t: e.tensor_copy(t["rlo"], t["rri"]), [h])
            r1 = add("dve", lambda e, t=t: e.tensor_tensor(t["sl"][:, 0:P], t["rr"], t["rlo"], ALU.subtract), [h])
            r2 = add("dve", lambda e, t=t: e.tensor_copy(t["sl"][:, P:2 * P], t["rlo"]), [h])
            r3 = add("dve", lambda e, t=t: e.tensor_copy(t["sl"][:, 2 * P:3 * P], t["r"]), [rf])
            r4 = add("dve", lambda e, t=t: e.tensor_scalar(t["sl"][:, 3 * P:4 * P], t["q"], float(P), None, ALU.mult), [qf])
            sv = dma("sp", lambda e, t=t, c=c: e.dma_start(
                source_tab[:, c * P * P:(c + 1) * P * P].rearrange("k (p n) -> p k n", p=P),
                t["sl"].rearrange("p (k n) -> p k n", k=4)), [r1, r2, r3, r4])
            tr = add("pe", lambda e, t=t, c=c: e.transpose(bank[c % 2][:, 0:P], t["rel"], ident[:, :]),
                     [rel, edge_done[-4:]])
            ts = add("pe", lambda e, t=t, c=c: e.transpose(bank[c % 2][:, P:2 * P], t["s"], ident[:, :]),
                     [s_f, edge_done[-4:]])
            ts = add("pe", lambda e, t=t, c=c: e.transpose(bank[c % 2][:, 2 * P:3 * P], t["q"], ident[:, :]), [qf])
            tr = ts
            es = edge_stage[:, c * GC:(c + 1) * GC, :]
            part = lambda n, es=es: es[:, :, n * G:(n + 1) * G]
            ps = lambda n, c=c: bank[c % 2][:, n * P:(n + 1) * P].rearrange("p (g k) -> p g k", k=G)
            e1 = add("dve", lambda e, part=part, ps=ps: e.tensor_copy(part(0).bitcast(I32), ps(1)), [ts])
            e2 = add("dve", lambda e, part=part, ps=ps: e.tensor_copy(part(1), ps(0)), [tr])
            e3 = add("dve", lambda e, part=part, ps=ps: e.tensor_scalar(part(2), ps(0), 0.0, NEG, ALU.is_lt, ALU.mult), [tr])
            mt = mtmp.rearrange("p (g k) -> p g k", k=G)
            e4 = add("dve", lambda e, ps=ps, mt=mt: e.tensor_scalar(mt, ps(0), P - 0.5, NEG, ALU.is_gt, ALU.mult),
                     [tr, relT_free])
            e5 = add("dve", lambda e, part=part, mt=mt: e.tensor_tensor(part(2), part(2), mt, ALU.add), [e3, e4])
            relT_free = e5
            e6 = add("dve", lambda e, part=part, ps=ps: e.tensor_copy(part(3), ps(1)), [ts])
            e7 = add("dve", lambda e, part=part, ps=ps: e.tensor_copy(part(4), ps(2)), [ts])
            edge_done += [e1, e2, e5, e7]
            prev[c % NR] = [tr, ts, st, oh, sv, c1, c2, p4, p5, q3, e7]
            st_saved += [st, oh, sv]
        edge_saved = dma("sp", lambda e: e.dma_start(edge_tab.rearrange("g p k -> p g k"), edge_stage), [edge_done])
        tc = add("pe", lambda e: e.transpose(bank[2][0:3 * SC, 0:P], col3[:, :], ident[:, :]), [c1, c2, c3b, key_copied])
        cc = add("dve", lambda e: e.tensor_copy(seg_fwd[0:3 * SC, :], bank[2][0:3 * SC, 0:P]), [tc])
        cs = dma("sp", lambda e: e.dma_start(col_tab, seg_fwd[0:3 * SC, :]), [cc])
        brow = view(big2[0:1, 0:3 * S], [(1, 3 * S)])
        cl = dma("sp", lambda e: e.dma_start(brow, col_tab.rearrange("(o a) b -> o (a b)", o=1)), [cs, last, relT_free])
        grp = lambda k: big2[0:1, k * S:(k + 1) * S].rearrange("o (g k) -> o g k", k=G)
        rt = big2[0:1, 3 * S:3 * S + NG * R1].rearrange("o (g k) -> o g k", k=R1)
        prevlast = big2[0:1, 3 * S + NG * R1:3 * S + NG * R1 + S]
        z1 = add("dve", lambda e: e.memset(prevlast[:, 0:1], -5.0), [cl])
        z2 = add("dve", lambda e: e.tensor_copy(prevlast[:, 1:S], big2[0:1, 2 * S:3 * S - 1]), [cl])
        pl = prevlast.rearrange("o (g k) -> o g k", k=G)
        z3 = add("dve", lambda e: e.tensor_tensor(rt[:, :, 1:G + 1], grp(2), pl, ALU.not_equal), [z1, z2])
        z4 = add("dve", lambda e: e.tensor_tensor(rt[:, :, G + 1:2 * G + 1], grp(1), pl, ALU.not_equal), [z1, z2])
        z5 = add("dve", lambda e: e.tensor_scalar(rt[:, :, 1:2 * G + 1], rt[:, :, 1:2 * G + 1], NEG, None, ALU.mult), [z3, z4])
        z6 = add("dve", lambda e: e.memset(rt[:, :, 0:1], NEG), [cl])
        z7 = add("dve", lambda e: e.tensor_copy(rt[:, :, 2 * G + 1:R1].bitcast(I32), grp(0)), [cl])
        row_saved = [dma("sp", lambda e: e.dma_start(row_tab1.rearrange("(o g) k -> o g k", o=1), rt), [z5, z6, z7])]
        for hd in range(8):
            row_saved.append(dma("sp", lambda e, hd=hd: e.dma_start(
                row_tab8[:, hd * (G + 1):(hd + 1) * (G + 1)].rearrange("(o g) k -> o g k", o=1), rt[:, :, 0:G + 1]), [z5, z6]))
            row_saved.append(dma("sp", lambda e, hd=hd: e.dma_start(
                row_tab8[:, 8 * (G + 1) + hd * G:8 * (G + 1) + (hd + 1) * G].rearrange("(o g) k -> o g k", o=1),
                rt[:, :, G + 1:2 * G + 1]), [z5]))
        row_saved.append(dma("sp", lambda e: e.dma_start(
            row_tab8[:, 8 * (2 * G + 1):R8].rearrange("(o g) k -> o g k", o=1), rt[:, :, 2 * G + 1:R1]), [z7]))
        tables = [st_saved, edge_saved, row_saved, m_oh]
        idle = [tables, edge_done, prev[0], prev[1], tc]

        def edge_pass(name, src_rows, heads, vector, use_max, ready):
            prog.stage(name)
            RW = heads * G
            width = P if vector else P + 1
            hw = P // heads
            aw = AW if heads > 1 else XW
            z_agg = add("dve", lambda e: e.memset(agg[:, :, :], 0.0), [ready])
            z_one = add("dve", lambda e: e.memset(rows[:, :, :, P:XW], 1.0), [ready])
            z_car = add("dve", lambda e: e.memset(carry[:, :], NEG), [ready])
            begin = [ready, z_agg, z_one, z_car]
            for e_ in prog.ENGINES:
                prog.queue[e_].append(lambda eng, last, w=list(flat(begin)): [eng.wait_ge(x.sem, x.value) for x in w
                                                                            if last.get(id(x.sem), 0) < x.value])
            prog.stage(name + "_loop")
            L = Loop(prog, NG)
            agg_flat = agg[:, :, :].rearrange("p a b -> p (a b)")
            dst_flat = dst_side[:, :, :].rearrange("p a b -> p (a b)")
            rw = R8 if heads > 1 else R1
            rt_ = row_tab8 if heads > 1 else row_tab1
            FC0, BL0 = heads * (G + 1), heads * (2 * G + 1)
            ntab = 3 + (heads if use_max else 0)
            TB, GB = tab_base[0], gat_base[0]
            tab_base[0] += 16 * ntab * (NG // U)
            gat_base[0] += 16 * G * (NG // U)
            holder = {}

            def load_tables(e, u, i):
                e.dma_start(edge_sb[:, u, :], edge_tab[bass.ds(i, 1), :, :].rearrange("o p k -> (o p) k")).then_inc(s_tab[u], 16)
                e.dma_start(oh_rows[0:3, u, :], onehot_tab[:, bass.ds(i * (G * P), G * P)]).then_inc(s_tab[u], 16)
                e.dma_start(row_sb[0:1, u, 0:rw], rt_[bass.ds(i, 1), :]).then_inc(s_tab[u], 16)
                if use_max:
                    for hd in range(heads):
                        e.dma_start(step_sb[hd * G:(hd + 1) * G, u, :],
                                    step_tab[bass.ds(i * G, G), :]).then_inc(s_tab[u], 16)

            def gather(e, u, i):
                for g in range(G):
                    e.indirect_dma_start(rows[:, u, g, 0:width], None, src_rows,
                                         bass.IndirectOffsetOnAxis(ap=edge_sb[:, u, g:g + 1].bitcast(I32), axis=0)
                                         ).then_inc(s_gat[u], 16)

            after_agg, after_acc = [], []
            tab = L.slot_dma("sp", load_tables, after_acc, s_tab, TB, 16 * ntab)
            gat = L.slot_dma("pool", gather, after_agg, s_gat, GB, 16 * G)
            gat.after.append((tab, 0))

            AG, XWc, MX = {}, {}, {}
            Wop, Aop = {}, {}
            w_done, scale_done = [], []

            def c_weight(g):
                def fn(e, u, i, g=g):
                    v = (u - 1) % U
                    if heads > 1:
                        return e.tensor_scalar(oh_e[:, g % 8, :], iota[:, :], edge_sb[:, v, G + g:G + g + 1], None, ALU.is_equal)
                    return e.tensor_scalar(oh_e[:, g % 8, :], iota[:, :], edge_sb[:, v, G + g:G + g + 1],
                                           weight[:, v % 2, g:g + 1], ALU.is_equal, ALU.mult)
                o = L.op("dve", fn, [(AG[g - 8], 0) if g >= 8 else None], lag=1)
                pend_w.append((o, g))
                return o
            pend_w = []

            def c_scaled_rows(c):
                def fn(e, u, i, c=c):
                    v = (u - 1) % U
                    o = view(xw[:, c % 2, :], [(AW, CH), (hw + 1, heads), (1, hw)])
                    x = view(rows[:, v, c * CH:(c + 1) * CH, :], [(XW, CH), (hw, heads), (1, hw)])
                    w = view(weight[:, v % 2, c * CH:(c + 1) * CH], [(1, CH), (G, heads), (0, hw)])
                    return e.tensor_tensor(o, x, w, ALU.mult)

                def fn2(e, u, i, c=c):
                    v = (u - 1) % U
                    o = view(xw[:, c % 2, hw:], [(AW, CH), (hw + 1, heads)])
                    w = view(weight[:, v % 2, c * CH:(c + 1) * CH], [(1, CH), (G, heads)])
                    return e.copy(o, w)
                aft = [(AG[(c - 2) * CH + CH - 1], 0)] if c >= 2 else []
                o1 = L.op("dve", fn, aft, lag=1)
                o2 = L.op("act", fn2, aft, lag=1)
                pend_x.append((o1, c))
                pend_x.append((o2, c))
                return [o1, o2]
            pend_x = []

            def c_agg(g):
                def fn(e, u, i, g=g):
                    v = (u - 1) % U
                    o = bank[4 + g // 2 % 2][:, (g % 2) * AW:(g % 2) * AW + aw]
                    if heads > 1:
                        r = xw[:, (g // CH) % 2, (g % CH) * AW:(g % CH) * AW + AW]
                    else:
                        r = rows[:, v, g, 0:XW]
                    return e.matmul(o, oh_e[:, g % 8, :], r, start=True, stop=True)
                aft = [(Wop[g], 0)]
                if heads > 1:
                    aft += [(o, 0) for o in XWc[g // CH]]
                if g >= 4:
                    aft.append((Aop[g - g % 2 - 3], 0))
                o = L.op("pe", fn, aft, lag=1)
                pend_a.append((o, g))
                AG[g] = o
                return o
            pend_a = []

            def blk_reg(e, u, v, g):
                return e.value_load(row_sb[0:1, v, BL0 + g:BL0 + g + 1].bitcast(I32), min_val=0, max_val=NB - 1)

            def c_acc(g):
                def fn(e, u, i, g=g):
                    v = (u - 1) % U
                    b = blk_reg(e, u, v, g)
                    at = agg_flat[:, bass.ds(b * AW, aw)]
                    s = bank[4 + g // 2 % 2][:, (g % 2) * AW:(g % 2) * AW + aw]
                    if not use_max:
                        return e.tensor_tensor(at, at, s, ALU.add)
                    return e.scalar_tensor_tensor(at, at, rescale[:, v % 2, g:g + 1], s, ALU.mult, ALU.add)

                def fn_a(e, u, i, g=g):
                    v = (u - 1) % U
                    b = blk_reg(e, u, v, g)
                    holder["at"] = agg_flat[:, bass.ds(b * AW, aw)]
                    at = holder["at"].rearrange("p (h d) -> p h d", h=heads)
                    f = view(rescale[:, v % 2, g:], [(G, heads), (0, hw + 1)])
                    return e.tensor_tensor(acc_tmp[:, g % 2, :].rearrange("p (h d) -> p h d", h=heads), at, f, ALU.mult)

                def fn_b(e, u, i, g=g):
                    s = bank[4 + g // 2 % 2][:, (g % 2) * AW:(g % 2) * AW + aw]
                    return e.tensor_tensor(holder["at"], acc_tmp[:, g % 2, :], s, ALU.add)
                before = [(Aop[g - 1], 0)] if g else []
                if heads > 1:
                    o = L.op("dve", fn_a, before, lag=1, anchored=True)
                    if g == 0:
                        pend_first.append(o)
                    o = L.op("dve", fn_b, [(o, 0), (AG[g - g % 2 + 1], 0)], lag=1)
                else:
                    o = L.op("dve", fn, before + [(AG[g - g % 2 + 1], 0)], lag=1, anchored=True)
                    if g == 0:
                        pend_first.append(o)
                Aop[g] = o
                return o
            pend_first = []

            def a_dist(c):
                def fn(e, u, i, c=c):
                    return e.matmul(bank[c % 2][:, :], oh_w[:, :], oh_rows[:, u, c * CH * P:(c + 1) * CH * P],
                                    start=True, stop=True)
                return L.op("pe", fn, [(tab, 0), (OT[c - 2], 0) if c >= 2 else None], anchored=False)

            def a_onehot(c):
                def fn(e, u, i, c=c):
                    return e.activation(oh_t[:, c % 2, :], bank[c % 2][:, :], ACT.Relu, bias=1.0, scale=-1.0)
                return L.op("act", fn, [(Q[c], 0), (Z[c - 2], 0) if c >= 2 else None])

            def a_sum(c):
                def fn(e, u, i, c=c):
                    for k in range(CH):
                        g = c * CH + k
                        b = blk_reg(e, u, u, g)
                        oh = oh_t[:, c % 2, k * P:(k + 1) * P]
                        if vector:
                            o = bank[2 + c % 2][:, k * P:(k + 1) * P]
                            e.matmul(o, oh, dst_flat[:, bass.ds(b * P, P)], start=True, stop=False)
                            ins = e.matmul(o, ident[:, :], rows[:, u, g, 0:P], start=False, stop=True)
                        else:
                            ins = e.matmul(bank[2][:, g:g + 1], oh, dst_score[:, bass.ds(b, 1)], start=True, stop=True)
                    return ins
                return L.op("pe", fn, [(OT[c], 0), (tab, 0)] + ([(gat, 0)] if vector else [])
                            + ([(MX[c - 2], 0)] if vector and c >= 2 else []), anchored=True)

            def a_lrelu(c):
                def fn(e, u, i, c=c):
                    return e.mul(lrelu[:, c % 2, :], bank[2 + c % 2][:, :], SLOPE)
                return L.op("act", fn, [(Z[c], 0), (RD[c - 2], 0) if c >= 2 else None])

            def a_logit(c):
                def fn0(e, u, i, c=c):
                    return e.tensor_tensor(lrelu[:, c % 2, :], lrelu[:, c % 2, :], bank[2 + c % 2][:, :], ALU.max)

                def fn(e, u, i, c=c):
                    x = lrelu[:, c % 2, :].rearrange("p (g n) -> p g n", g=CH)
                    return e.tensor_tensor(x, x, view(att[:, :], [(0, CH), (1, P)]), ALU.mult)

                def fn2(e, u, i, c=c):
                    x = view(lrelu[:, c % 2, :], [(P, CH), (hw, heads), (1, hw)])
                    return e.tensor_reduce(view(logit[:, c * CH:], [(1, CH), (G, heads)]), x, AX.X, ALU.add)
                mx = L.op("dve", fn0, [(LR[c], 0)])
                o = L.op("dve", fn, [(mx, 0)])
                MX[c] = mx
                return L.op("dve", fn2, [(o, 0)])

            Q, OT, Z, LR, RD = {}, {}, {}, {}, {}
            Q[0] = a_dist(0)
            OT[0] = a_onehot(0)
            for c in range(NCH):
                for g in range(c * CH, (c + 1) * CH):
                    Wop[g] = c_weight(g)
                if heads > 1:
                    XWc[c] = c_scaled_rows(c)
                if c + 1 < NCH:
                    Q[c + 1] = a_dist(c + 1)
                    OT[c + 1] = a_onehot(c + 1)
                Z[c] = a_sum(c)
                if vector:
                    LR[c] = a_lrelu(c)
                for g in range(c * CH, (c + 1) * CH):
                    c_agg(g)
                    if g % 2:
                        c_acc(g - 1)
                        c_acc(g)
                if vector:
                    RD[c] = a_logit(c)
            for c in (0, 1):
                Q[c].after.append((OT[c + 2], 1))
                OT[c].after.append((Z[c + 2], 1))
                if vector:
                    Z[c].after.append((MX[c + 2], 1))
                    LR[c].after.append((RD[c + 2], 1))
            for o, g in pend_a:
                if g < 4:
                    o.after.append((Aop[G - 3 + g - g % 2], 1))
            for o, g in pend_w:
                if g < 8:
                    o.after.append((AG[g + 8], 1))
            for o, c in pend_x:
                if c < 2:
                    o.after.append((AG[(c + 2) * CH + CH - 1], 1))
            pend_first[0].after.append((Aop[G - 1], 1))
            gat.after.append((AG[G - 1], 3))
            tab.after.append((Aop[G - 1], 3))

            if not vector:
                def fn(e, u, i):
                    return e.tensor_tensor(logit[:, 0:G], bank[2][:, 0:G], rows[:, u, :, P:P + 1].rearrange("p g o -> p (g o)"), ALU.add)
                sc = L.op("dve", fn, [(Z[NCH - 1], 0), (gat, 0)])
                Z[0].after.append((sc, 1))
                lg = L.op("dve", lambda e, u, i: e.scalar_tensor_tensor(logit[:, 0:G], logit[:, 0:G], SLOPE, logit[:, 0:G],
                                                                       ALU.mult, ALU.max), [(sc, 0)])
            else:
                lg = RD[NCH - 1]
            if not use_max:
                wt = L.op("act", lambda e, u, i: e.activation(weight[:, u % 2, 0:RW], logit[:, 0:RW], ACT.Exp),
                          [(lg, 0), (Wop[G - 1], 1)])
                (sc if not vector else RD[0]).after.append((wt, 1))
                pend_w[0][0].after.append((wt, 1))
            else:
                mk = L.op("dve", lambda e, u, i: e.tensor_tensor(
                    masked[:, 0:RW].rearrange("p (h g) -> p h g", h=heads), logit[:, 0:RW].rearrange("p (h g) -> p h g", h=heads),
                    view(edge_sb[:, u, 2 * G:], [(0, heads), (1, G)]), ALU.add), [(lg, 0)])
                LT = bank[6][0:RW, 0:P]
                RT = bank[6][:, P:P + RW]
                ST_ = bank[6][:, 2 * P:2 * P + RW]
                Y1 = bank[7][0:1, 0:RW]
                Y2 = bank[7][0:RW, P:P + 1]
                tp1 = L.op("pe", lambda e, u, i: e.transpose(LT, masked[:, 0:RW], ident[:, :]), [(mk, 0)], anchored=True)
                sf = L.op("dve", lambda e, u, i: e.tensor_tensor_scan(seg_fwd[0:RW, :], step_sb[0:RW, u, 0:P], LT,
                                                                     NEG, ALU.add, ALU.max), [(tp1, 0)])
                sbk = L.op("dve", lambda e, u, i: e.tensor_tensor_scan(
                    view(seg_max[0:RW, P - 1:], [(-1, P)]), view(step_sb[0:RW, u, P:], [(-1, P)]),
                    view(seg_fwd[0:RW, P - 1:], [(-1, P)]), NEG, ALU.add, ALU.max), [(sf, 0)])
                tp2 = L.op("pe", lambda e, u, i: e.transpose(Y1, seg_max[0:RW, P - 1:P], ident[0:RW, 0:RW]), [(sbk, 0)], anchored=True)
                cv = lambda t, k: t[:, 0:heads * (G + 1)].rearrange("o (h k) -> o h k", h=heads)[:, :, k]
                k0 = L.op("dve", lambda e, u, i: e.tensor_copy(cv(carry_in, slice(0, 1)), cv(carry, slice(G, G + 1))), [])
                k1 = L.op("dve", lambda e, u, i: e.tensor_copy(cv(carry_in, slice(1, G + 1)), Y1.rearrange("o (h g) -> o h g", h=heads)), [(tp2, 0)])
                k2 = L.op("dve", lambda e, u, i: e.tensor_tensor_scan(carry[:, 0:heads * (G + 1)], row_sb[0:1, u, 0:heads * (G + 1)],
                                                                     carry_in[:, 0:heads * (G + 1)], NEG, ALU.add, ALU.max), [(k0, 0), (k1, 0)])
                k0.after.append((k2, 1))
                k3 = L.op("dve", lambda e, u, i: e.tensor_tensor(
                    cin_row[:, 0:RW].rearrange("o (h g) -> o h g", h=heads), cv(carry, slice(0, G)),
                    row_sb[0:1, u, FC0:FC0 + RW].rearrange("o (h g) -> o h g", h=heads), ALU.add), [(k2, 0)])
                tp3 = L.op("pe", lambda e, u, i: e.transpose(Y2, cin_row[:, 0:RW], ident[0:1, 0:1]), [(k3, 0)], anchored=True)
                k4 = L.op("dve", lambda e, u, i: e.tensor_copy(cin[0:RW, 0:1], Y2), [(tp3, 0)])
                rm = L.op("dve", lambda e, u, i: e.scalar_tensor_tensor(run_max[0:RW, :], step_sb[0:RW, u, P + 1:2 * P + 1], cin[0:RW, 0:1],
                                                                       seg_max[0:RW, :], ALU.add, ALU.max), [(k4, 0)])
                tp4 = L.op("pe", lambda e, u, i: e.transpose(RT, run_max[0:RW, :], ident[0:RW, 0:RW]), [(rm, 0)], anchored=True)
                dd = L.op("dve", lambda e, u, i: e.tensor_tensor(cin[0:RW, 1:2], cin[0:RW, 0:1], run_max[0:RW, 0:1], ALU.subtract), [(rm, 0)])
                ce = L.op("act", lambda e, u, i: e.activation(cin[0:RW, 2:3], cin[0:RW, 1:2], ACT.Exp), [(dd, 0)])
                df = L.op("dve", lambda e, u, i: e.tensor_tensor(shifted[:, 0:RW], masked[:, 0:RW], RT, ALU.subtract), [(tp4, 0)])
                wt = L.op("act", lambda e, u, i: e.activation(weight[:, u % 2, 0:RW], shifted[:, 0:RW], ACT.Exp), [(df, 0)])
                cm = L.op("dve", lambda e, u, i: e.tensor_scalar(cin[0:RW, 3:4], cin[0:RW, 2:3], -1.0, None, ALU.add), [(ce, 0)])
                dm = L.op("dve", lambda e, u, i: e.tensor_scalar(decay_m[0:RW, :], iota[0:RW, :], step_sb[0:RW, u, 2 * P + 1:2 * P + 2],
                                                                cin[0:RW, 3:4], ALU.is_equal, ALU.mult), [(cm, 0)])
                tp5 = L.op("pe", lambda e, u, i: e.transpose(ST_, decay_m[0:RW, :], ident[0:RW, 0:RW]), [(dm, 0)], anchored=True)
                sl = L.op("dve", lambda e, u, i: e.tensor_scalar(rescale[:, u % 2, 0:RW], ST_, 1.0, None, ALU.add), [(tp5, 0)])
                df.after.append((wt, 1))
                wt.after.append((Wop[G - 1], 1))
                pend_w[0][0].after.append((wt, 1))
                pend_first[0].after.append((sl, 1))
                if heads > 1:
                    for o, c in pend_x:
                        if c == 0:
                            o.after.append((wt, 1))
                    wt.after += [(XWc[NCH - 1][0], 1), (XWc[NCH - 1][1], 1)]
            tab.after.append((tab, 4))
            L.close()
            done = [L.last(Aop[G - 1])]
            return done

        s_sc = [prog.sem(f"scatter_into_sum{k}") for k in range(NSUM)]

        def source_pass(name, ready):
            prog.stage(name)
            big = dst_side[:, :, :].rearrange("p a b -> p (a b)")
            at = 0

            def part(n, dt=F32):
                nonlocal at
                at += n
                v = big[:, at - n:at]
                return v if dt == F32 else v.bitcast(dt)
            src_rows = part(U * G * P // 2, BF16).rearrange("p (u n) -> p u n", u=U)
            summed = part(8 * XW).rearrange("p (s n) -> p s n", s=8)
            oh_s = part(CH * P)
            same = part(8 * P).rearrange("p (s n) -> p s n", s=8)
            scratch = part(2 * CH * P).rearrange("p (s n) -> p s n", s=2 * CH)
            look = part(G)
            dup = part(G)
            target_f = part(G)
            target = part(U * G, I32).rearrange("p (u n) -> p u n", u=U)
            z = add("dve", lambda e: e.memset(src_rows[0:6, :, :], 1.0), [ready])
            for e_ in prog.ENGINES:
                prog.queue[e_].append(lambda eng, last, w=list(flat([ready, z])): [eng.wait_ge(x.sem, x.value) for x in w
                                                                                 if last.get(id(x.sem), 0) < x.value])
            prog.stage(name + "_loop")
            L = Loop(prog, NG)
            agg_flat = agg[:, :, :].rearrange("p a b -> p (a b)")
            BL0 = 2 * G + 1
            ntab = 4
            TB = tab_base[0]
            tab_base[0] += 16 * ntab * (NG // U)

            def load_tables(e, u, i):
                e.dma_start(edge_sb[:, u, :], edge_tab[bass.ds(i, 1), :, :].rearrange("o p k -> (o p) k")).then_inc(s_tab[u], 16)
                e.dma_start(oh_rows[0:3, u, :], onehot_tab[:, bass.ds(i * (G * P), G * P)]).then_inc(s_tab[u], 16)
                e.dma_start(src_rows[0:4, u, :], source_tab[:, bass.ds(i * (G * P), G * P)]).then_inc(s_tab[u], 16)
                e.dma_start(row_sb[0:1, u, 0:R1], row_tab1[bass.ds(i, 1), :]).then_inc(s_tab[u], 16)
            tab = L.slot_dma("sp", load_tables, [], s_tab, TB, 16 * ntab)

            def scatters_before(g, i, lag):
                return (i - lag) * (16 * G // NSUM) + 16 * (g // NSUM)

            D, OT, XD, EV, DS, OS, LK, SEL, BA, DU = {}, {}, {}, {}, {}, {}, {}, {}, {}, {}
            BC, SM, AG, RV = {}, {}, {}, {}
            for c in range(NCH):
                BC[c] = L.op("pe", lambda e, u, i, c=c: e.matmul(bank[2][:, :], oh_ws[:, P:2 * P],
                                                                 src_rows[0:6, (u - 1) % U, c * CH * P:(c + 1) * CH * P],
                                                                 start=True, stop=True),
                             [(SM[c * CH - 1], 0)] if c else [], lag=1)
                for g in range(c * CH, (c + 1) * CH):
                    SM[g] = L.op("dve", lambda e, u, i, g=g: e.tensor_scalar(
                        same[:, g % 8, :], bank[2][:, (g % CH) * P:(g % CH + 1) * P],
                        edge_sb[:, (u - 1) % U, 3 * G + g:3 * G + g + 1], weight[:, (u - 1) % 2, g:g + 1],
                        ALU.is_equal, ALU.mult), [(BC[c], 0)] + ([(AG[g - 8], 0)] if g >= 8 else []), lag=1)
                D[c] = L.op("pe", lambda e, u, i, c=c: e.matmul(bank[0][:, :], oh_w[:, :], oh_rows[:, u, c * CH * P:(c + 1) * CH * P],
                                                                start=True, stop=True), [(tab, 0)] + ([(OT[c - 1], 0)] if c else []))
                OT[c] = L.op("act", lambda e, u, i, c=c: e.activation(oh_t[:, c % 2, :], bank[0][:, :], ACT.Relu, bias=1.0, scale=-1.0),
                             [(D[c], 0)] + ([(XD[(c - 2) * 2 + 1], 0)] if c >= 2 else []))
                DS[c] = L.op("pe", lambda e, u, i, c=c: e.matmul(bank[1][:, :], oh_ws[:, 0:P], src_rows[0:6, u, c * CH * P:(c + 1) * CH * P],
                                                                 start=True, stop=True), [(tab, 0)] + ([(DU[c * CH - 1], 0)] if c else []))
                OS[c] = L.op("act", lambda e, u, i, c=c: e.activation(oh_s, bank[1][:, :], ACT.Relu, bias=1.0, scale=-1.0),
                             [(DS[c], 0)] + ([(LK[c - 1], 0)] if c else []))
                for g in range(c * CH, (c + 1) * CH):
                    if g % 2 == 0:
                        continue
                    h = g // 2
                    for gg in (g - 1, g):
                        AG[gg] = L.op("pe", lambda e, u, i, g=gg: e.matmul(
                            bank[6 + g // 2 % 2][:, (g % 2) * XW:(g % 2 + 1) * XW], same[:, g % 8, :], rows[:, (u - 1) % U, g, :],
                            start=True, stop=True), [(SM[gg], 0)] + ([(RV[h - 2], 0)] if h >= 2 else []), lag=1)

                    def evac(e, u, i, g=g - 1):
                        for gg in (g, g + 1):
                            if isinstance(i, int):
                                n = scatters_before(gg, i, 1) - 16
                                if n > 0:
                                    e.wait_ge(s_sc[gg % NSUM], n)
                            else:
                                e.wait_ge(s_sc[gg % NSUM], i * (16 * G // NSUM) + (16 * (gg // NSUM) - 16 * G // NSUM - 16))
                        return e.copy(summed[:, g % 8:g % 8 + 2, :].rearrange("p s n -> p (s n)"), bank[6 + g // 2 % 2][:, 0:2 * XW])
                    RV[h] = L.op("act", evac, [(AG[g], 0)], lag=1)

                    def scatter(e, u, i, g=g - 1):
                        for gg in (g, g + 1):
                            k = gg % NSUM
                            if isinstance(i, int):
                                n = scatters_before(gg, i, 1)
                                if n > 0:
                                    e.wait_ge(s_sc[k], n)
                            else:
                                e.wait_ge(s_sc[k], i * (16 * G // NSUM) + (16 * (gg // NSUM) - 16 * G // NSUM))
                                e.sem_inc(prog.anchor, 1)
                            e.indirect_dma_start(scatter_s[k], bass.IndirectOffsetOnAxis(ap=target[:, (u - 1) % U, gg:gg + 1], axis=0),
                                                 summed[:, gg % 8, :], None, compute_op=ALU.add).then_inc(s_sc[k], 16)
                    L.op("pool", scatter, [(RV[h], 0)], lag=1, anchored=True)

                def blk(e, u, g):
                    return e.value_load(row_sb[0:1, u, BL0 + g:BL0 + g + 1].bitcast(I32), min_val=0, max_val=NB - 1)

                def lookup(e, u, i, c=c):
                    for k in range(CH):
                        ins = e.matmul(bank[5][:, k * P:k * P + NB], oh_s[:, k * P:(k + 1) * P], dst_score[:, :], start=True, stop=True)
                    return ins
                LK[c] = L.op("pe", lookup, [(OS[c], 0)] + ([(SEL[c * CH - 1], 0)] if c else []))
                BA[c] = L.op("pe", lambda e, u, i, c=c: e.matmul(bank[1][:, :], oh_ws[:, P:2 * P], src_rows[0:6, u, c * CH * P:(c + 1) * CH * P],
                                                                 start=True, stop=True), [(OS[c], 0)])
                for h in (2 * c, 2 * c + 1):
                    def expand(e, u, i, h=h):
                        for k in (0, 1):
                            g = 2 * h + k
                            b = blk(e, u, g)
                            ins = e.matmul(bank[3 + h % 2][:, k * XW:(k + 1) * XW], oh_t[:, (g // CH) % 2, (g % CH) * P:(g % CH + 1) * P],
                                           agg_flat[:, bass.ds(b * AW, XW)], start=True, stop=True)
                        return ins
                    XD[h] = L.op("pe", expand, [(OT[c], 0)] + ([(EV[h - 2], 0)] if h >= 2 else []), anchored=True)
                    EV[h] = L.op("act", lambda e, u, i, h=h: e.copy(rows[:, u, 2 * h:2 * h + 2, :].rearrange("p s n -> p (s n)"),
                                                                    bank[3 + h % 2][:, 0:2 * XW]), [(XD[h], 0)])
                for g in range(c * CH, (c + 1) * CH):
                    SEL[g] = L.op("dve", lambda e, u, i, g=g: e.scalar_tensor_tensor(
                        scratch[:, g % CH, 0:NB], iota[:, 0:NB], edge_sb[:, u, 4 * G + g:4 * G + g + 1], bank[5][:, (g % CH) * P:(g % CH) * P + NB],
                        ALU.is_equal, ALU.mult, accum_out=look[:, g:g + 1]), [(LK[c], 0)] + ([(SEL[g - CH], 0)] if g >= CH else []))
                for g in range(c * CH, (c + 1) * CH):
                    DU[g] = L.op("dve", lambda e, u, i, g=g: e.scalar_tensor_tensor(
                        scratch[:, CH + g % CH, :], bank[1][:, (g % CH) * P:(g % CH + 1) * P], edge_sb[:, u, 3 * G + g:3 * G + g + 1], att[:, :],
                        ALU.is_equal, ALU.mult, accum_out=dup[:, g:g + 1]), [(BA[c], 0)] + ([(DU[g - CH], 0)] if g >= CH else []))
            a1 = L.op("dve", lambda e, u, i: e.tensor_tensor(logit[:, 0:G], look[:, :], rows[:, u, :, P:P + 1].rearrange("p g o -> p (g o)"),
                                                             ALU.add), [(SEL[G - 1], 0), (EV[G // 2 - 1], 0)])
            a2 = L.op("dve", lambda e, u, i: e.scalar_tensor_tensor(logit[:, 0:G], logit[:, 0:G], SLOPE, logit[:, 0:G], ALU.mult, ALU.max), [(a1, 0)])
            a3_ = L.op("dve", lambda e, u, i: e.tensor_tensor(logit[:, 0:G], logit[:, 0:G], edge_sb[:, u, 2 * G:3 * G], ALU.add), [(a2, 0)])
            wt = L.op("act", lambda e, u, i: e.activation(weight[:, u % 2, 0:G], logit[:, 0:G], ACT.Exp), [(a3_, 0), (SM[G - 1], 1)])
            t1 = L.op("dve", lambda e, u, i: e.tensor_scalar(dup[:, :], dup[:, :], 0.0, None, ALU.is_gt), [(DU[G - 1], 0)])
            t2 = L.op("dve", lambda e, u, i: e.tensor_scalar(target_f[:, :], edge_sb[:, u, 3 * G:4 * G], dump_row[:, 0:1], -1.0,
                                                             ALU.subtract, ALU.mult), [(t1, 0)])
            t3 = L.op("dve", lambda e, u, i: e.tensor_tensor(target_f[:, :], target_f[:, :], dup[:, :], ALU.mult), [(t2, 0)])
            t4 = L.op("dve", lambda e, u, i: e.tensor_tensor(target_f[:, :], target_f[:, :], edge_sb[:, u, 3 * G:4 * G], ALU.add), [(t3, 0)])

            def store_target(e, u, i):
                for k in range(NSUM):
                    if isinstance(i, int):
                        if i >= U:
                            e.wait_ge(s_sc[k], (16 * G // NSUM) * (i - U + 1))
                    else:
                        e.wait_ge(s_sc[k], i * (16 * G // NSUM) - (16 * G // NSUM) * (U - 1))
                return e.tensor_copy(target[:, u, :], target_f[:, :])
            t5 = L.op("dve", store_target, [(t4, 0)])
            BC[0].after.append((SM[G - 1], 1))
            SM[0].after += [(wt, 1), (AG[8], 1)]
            for g in range(1, 8):
                SM[g].after.append((AG[g + 8], 1))
            D[0].after.append((OT[NCH - 1], 1))
            OT[0].after.append((XD[5], 1))
            OT[1].after.append((XD[7], 1))
            DS[0].after.append((DU[G - 1], 1))
            OS[0].after.append((LK[NCH - 1], 1))
            LK[0].after.append((SEL[G - 1], 1))
            for g in (0, 1):
                AG[g].after.append((RV[6], 1))
            for g in (2, 3):
                AG[g].after.append((RV[7], 1))
            XD[0].after.append((EV[6], 1))
            XD[1].after.append((EV[7], 1))
            EV[0].after.append((AG[G - 1], 3))
            RV[0].after.append((t5, 1))
            SEL[0].after += [(a1, 1), (SEL[G - 1], 1)]
            DU[0].after += [(DU[G - 1], 1), (t3, 1)]
            a1.after.append((wt, 1))
            L.ops[[o is AG[G - 1] for o in L.ops].index(True)].counted = True
            tab.after += [(AG[G - 1], 3), (SM[G - 1], 3), (t4, 4), (tab, 4)]
            scat_after = None
            L.close()
            return [L.last(AG[G - 1]), L.last(SM[G - 1])] + [Done(s_sc[k], 16 * (G // NSUM) * NG) for k in range(NSUM)]

        node_tile = lambda n: pool_rows[:, n * NBB * P:(n + 1) * NBB * P]
        tile3 = lambda n: node_tile(n).rearrange("p (b f) -> p b f", b=NBB)
        hT = [sb(f"hT{k}", [P, NBB * P]) for k in range(1)]
        NBT = NB // NBB
        wcol = lambda n, k=1: param[:, n * P:(n + k) * P]

        def row_bcast(x, off=0, n=P):
            return bass.AP(x.tensor, x.offset + off, [(0, P), (1, n)])

        def load_rows(pairs, after):
            return [dma("sp", lambda e, s=s, src=src: e.dma_start(s, src), after) for s, src in pairs]

        def blocks(ap2d, t):
            return ap2d[t * NBB * P:(t + 1) * NBB * P, :].rearrange("(b p) f -> p b f", p=P)

        def transposed(src3, bank0, ready, free):
            outs = []
            dst = hT[0]
            for q, (lo, hi) in enumerate(((0, 4), (4, NBB))):
                for k in range(lo, hi):
                    tp = add("pe", lambda e, k=k, q=q, lo=lo: e.transpose(bank[bank0 + q][:, (k - lo) * P:(k - lo + 1) * P],
                                                                          src3[:, k, :], ident[:, :]), [ready, free])
                outs.append(add("act", lambda e, q=q, lo=lo, hi=hi: e.copy(dst[:, lo * P:hi * P], bank[bank0 + q][:, 0:(hi - lo) * P]),
                                [tp, free]))
            return outs

        def layer_norm(x3, ready, slot):
            hs = [add("dve", lambda e, k=k: e.bn_stats(stats[:, k, :], x3[:, k, :]), [ready]) for k in range(NBB)]
            hs = [add("dve", lambda e, k=k: e.bn_aggr(moments[:, k, :], stats[:, k, :]), [hs[k]]) for k in range(NBB)]
            h = add("dve", lambda e: e.tensor_scalar(rstd[:, 0, :], moments[:, :, 1], LN_EPS, None, ALU.add), [hs])
            h = add("pool", lambda e: e.tensor_tensor(rstd[:, 1, :], rstd[:, 0, :], minus_half[:, :], ALU.pow), [h, m_half])
            return [add("dve", lambda e, k=k: e.tensor_scalar(x3[:, k, :], x3[:, k, :], moments[:, k, 0:1], rstd[:, 1, k:k + 1],
                                                            ALU.subtract, ALU.mult), [h]) for k in range(NBB)]

        def bias3(n):
            return view(wcol(n), [(0, NBB), (1, P)])

        def project(t, w2, evac, ready, free_ps):
            outs = []
            for q in range((NBB + 1) // 2):
                ks = [k for k in (2 * q, 2 * q + 1) if k < NBB]
                for k in ks:
                    mm = add("pe", lambda e, k=k, q=q: e.matmul(bank[4 + q][:, (k % 2) * 2 * P:(k % 2 + 1) * 2 * P],
                                                                hT[0][:, k * P:(k + 1) * P], wcol(w2, 2), start=True, stop=True),
                             [ready, free_ps[q] if free_ps else []])
                outs.append(evac(q, ks, mm))
            return outs

        def two_sided(t, w2, b_src, b_dst, ready, free_ps, stage3, stage_free, table):
            def evac(q, ks, mm):
                n = len(ks)
                src = bank[4 + q][:, 0:n * 2 * P].rearrange("p (k s f) -> p k s f", k=n, s=2)
                def fn(e):
                    o = stage3[:, ks[0]:ks[0] + n, :]
                    if b_src is None:
                        return e.tensor_copy(o, src[:, :, 0, :])
                    return e.tensor_tensor(o, src[:, :, 0, :], view(wcol(b_src), [(0, n), (1, P)]), ALU.add)
                def fn2(e):
                    o = dst_side[:, t * NBB + ks[0]:t * NBB + ks[0] + n, :]
                    if b_dst is None:
                        return e.tensor_copy(o, src[:, :, 1, :])
                    return e.tensor_tensor(o, src[:, :, 1, :], view(wcol(b_dst), [(0, n), (1, P)]), ALU.add)
                return [add("dve", fn, [mm, stage_free]), add("dve", fn2, [mm])]
            outs = project(t, w2, evac, ready, free_ps)
            st = dma("sp", lambda e: e.dma_start(blocks(table, t), stage3), [outs])
            return outs, st

        def load_x(t, dst3, src, after):
            lo, hi = t * NBB * P, (t + 1) * NBB * P
            if src.shape[0] == NB * P or hi <= N:
                return [dma("sp", lambda e: e.dma_start(dst3, src[lo:hi, :].rearrange("(b p) f -> p b f", p=P)), after)]
            zero = add("dve", lambda e: e.memset(dst3, 0.0), after)
            full = (N - lo) // P
            rem = N - lo - full * P
            hs = []
            if full:
                hs.append(dma("sp", lambda e: e.dma_start(dst3[:, 0:full, :], src[lo:lo + full * P, :].rearrange("(b p) f -> p b f", p=P)), [zero]))
            if rem:
                hs.append(dma("sp", lambda e: e.dma_start(dst3[0:rem, full, :], src[lo + full * P:N, :]), [zero]))
            return hs

        prog.stage("dense0")
        prm = load_rows([(wcol(0), a["L0_gnn_Wl1"]), (wcol(1), a["L0_gnn_Wr1"]), (wcol(2), row_bcast(a["L0_gnn_bl1"])),
                         (wcol(3), row_bcast(a["L0_gnn_br1"])), (att[:, :], row_bcast(a["L0_gnn_att1"]))], [idle])
        x_free, ht_free, ps_free, st_free = [[], []], [], None, [[], []]
        tail = []
        for t in range(NBT):
            x3 = tile3(t % 2)
            ld = load_x(t, x3, a["x"], [idle, x_free[t % 2]])
            tt = transposed(x3, 0, [ld, prm], ht_free)
            ev, st = two_sided(t, 0, 2, 3, [tt, prm], ps_free, tile3(2 + t % 2), [st_free[t % 2], idle], gather_a)
            x_free[t % 2], ht_free, ps_free, st_free[t % 2] = tt, ev, ev, [st]
            tail += [st, ev]
        p0 = edge_pass("L0a", gather_a, 1, True, True, [tail, tables])

        def normalise(t, heads, eps, ready, guard=None):
            a3 = agg[:, t * NBB:(t + 1) * NBB, :]
            hw = P // heads
            if heads == 1:
                den = a3[:, :, P + 1]
                r = recip[:, 0:NBB]
                rb = view(recip[:, :], [(1, NBB), (0, P)])
                h = add("dve", lambda e: (e.tensor_scalar(r, den, eps, None, ALU.add) if guard is None else
                                          e.tensor_scalar(r, den, guard, None, ALU.max)), [ready])
                h = add("dve", lambda e: e.reciprocal(r, r), [h])
                return add("dve", lambda e: e.tensor_tensor(a3[:, :, 0:P], a3[:, :, 0:P], rb, ALU.mult), [h])
            den = view(agg[:, t * NBB, hw:], [(AW, NBB), (hw + 1, heads)])
            r = recip[:, :].rearrange("p (b h) -> p b h", b=NBB)
            h = add("dve", lambda e: e.tensor_scalar(r, den, eps, None, ALU.add), [ready])
            h = add("dve", lambda e: e.reciprocal(recip[:, :], recip[:, :]), [h])
            return h

        def bias_add(o3, i3, n, after):
            return add("dve", lambda e: e.tensor_tensor(o3, i3, bias3(n), ALU.add), after)

        prog.stage("dense1")
        prm = load_rows([(wcol(0), a["L0_gnn_Wl2"]), (wcol(1), a["L0_gnn_Wr2"]), (wcol(2), row_bcast(a["L0_gnn_bl2"])),
                         (wcol(3), row_bcast(a["L0_gnn_br2"])), (wcol(4), row_bcast(a["L0_gnn_bias1"])),
                         (att[:, :], row_bcast(a["L0_gnn_att2"]))], [p0])
        ht_free, ps_free, st_free = [], None, [[], []]
        tail = []
        prev_n = None
        for t in range(NBT):
            a3 = agg[:, t * NBB:(t + 1) * NBB, 0:P]
            h = normalise(t, 1, 1e-16, [p0, prev_n])
            prev_n = h
            h = bias_add(a3, a3, 4, [h, prm])
            h = add("act", lambda e, a3=a3: e.activation(a3, a3, ACT.Relu), [h])
            tt = transposed(a3, 0, [h, prm], ht_free)
            ev, st = two_sided(t, 0, 2, 3, [tt, prm], ps_free, tile3(2 + t % 2), [st_free[t % 2], p0], gather_b)
            ht_free, ps_free, st_free[t % 2] = ev, ev, [st]
            tail += [st, ev]
        p1 = edge_pass("L0b", gather_b, 1, True, True, [tail])

        prog.stage("dense2")
        NP_ = 0
        wsb, a12, vsb, wb = wcol(0), wcol(1)[:, 0:2], wcol(1)[:, 4:6], wcol(1)[:, 8:9]
        s12, cvec, abias = wcol(1)[:, 9:10], wcol(1)[:, 10:11], wcol(1)[:, 11:12]
        one_col = lambda x, off=0: bass.AP(x.tensor, x.offset + off, [(1, P), (1, 1)])
        prm = load_rows([(wsb, a["L1_gnn_w_weight"]), (a12[:, 0:1], one_col(a["L1_gnn_a_weight"])),
                         (a12[:, 1:2], one_col(a["L1_gnn_a_weight"], P)), (wb, one_col(a["L1_gnn_w_bias"])),
                         (abias, bass.AP(a["L1_gnn_a_bias"].tensor, 0, [(0, P), (1, 1)])),
                         (wcol(2), row_bcast(a["L0_gnn_bias2"]))], [p1])
        mm = add("pe", lambda e: e.matmul(bank[0][:, 0:2], wsb, a12, start=True, stop=True), [prm])
        v12 = add("dve", lambda e: e.tensor_copy(vsb, bank[0][:, 0:2]), [mm])
        h = add("dve", lambda e: e.tensor_tensor(s12, a12[:, 0:1], a12[:, 1:2], ALU.add), [prm])
        h = add("dve", lambda e: e.tensor_tensor(s12, s12, wb, ALU.mult), [h])
        mm = add("pe", lambda e: e.matmul(bank[1][:, 0:1], ones[:, :], s12, start=True, stop=True), [h])
        v12 = [v12, add("dve", lambda e: e.tensor_tensor(cvec, bank[1][:, 0:1], abias, ALU.add), [mm, prm])]
        x_free, ht_free, sc_free, st_free = [[], []], [], [], [[], []]
        tail, prev_n, rows_ln = [], None, []
        for t in range(NBT):
            a3 = agg[:, t * NBB:(t + 1) * NBB, 0:P]
            x3 = tile3(t % 2)
            ld = load_x(t, x3, a["x"], [p1, x_free[t % 2]])
            h = normalise(t, 1, 1e-16, [p1, prev_n])
            prev_n = h
            h = bias_add(a3, a3, 2, [h, prm])
            h = add("dve", lambda e, a3=a3, x3=x3: e.tensor_tensor(a3, a3, x3, ALU.add), [h, ld])
            x_free[t % 2] = h
            ln = layer_norm(a3, [h, rows_ln], 0)
            rows_ln = ln
            tt = transposed(a3, 2, [ln, v12], ht_free)
            for k in range(NBB):
                mm = add("pe", lambda e, k=k: e.matmul(bank[4][:, 2 * k:2 * k + 2], hT[0][:, k * P:(k + 1) * P], vsb,
                                                       start=True, stop=True), [tt, sc_free])
            ht_free = mm
            ps = bank[4][:, 0:2 * NBB].rearrange("p (k s) -> p k s", s=2)
            s1 = add("dve", lambda e, t=t, ps=ps: e.tensor_scalar(dst_score[:, t * NBB:(t + 1) * NBB], ps[:, :, 0], cvec, None, ALU.add), [mm])
            s2 = add("dve", lambda e, t=t, ps=ps: e.tensor_copy(agg[:, t * NBB:(t + 1) * NBB, P], ps[:, :, 1]), [mm])
            sc_free = [s1, s2]
            s3 = add("dve", lambda e, t=t: e.memset(agg[:, t * NBB:(t + 1) * NBB, P + 1:P + 2], 1.0), [h])
            tail += [ln, s1, s2, s3]
        zt = tile3(4)[:, 0:4, :].rearrange("p b f -> p (b f)")
        zz = add("dve", lambda e: e.memset(node_tile(4), 0.0), [p1])
        NBZ = NB + 1
        zw = 6 * XW
        for k in range(NSUM):
            for z0 in range(0, NBZ, 6):
                z1 = min(z0 + 6, NBZ)
                tail.append(dma("sp", lambda e, k=k, z0=z0, z1=z1: e.dma_start(
                    scatter_s[k][z0 * P:z1 * P, :].rearrange("(p b) f -> p (b f)", p=P), node_tile(4)[:, 0:(z1 - z0) * XW]), [zz]))
        tail.append(dma("sp", lambda e: e.dma_start(att[:, :], a["c_tril"]), [p1]))
        p2 = source_pass("L1", [tail])

        def transpose_weight(n, src, stage_n, after, pb):
            ld = dma("sp", lambda e: e.dma_start(node_tile(stage_n)[:, 0:P], src), after)
            tp = add("pe", lambda e: e.transpose(bank[pb][:, 0:P], node_tile(stage_n)[:, 0:P], ident[:, :]), [ld])
            return add("act", lambda e: e.copy(wcol(n), bank[pb][:, 0:P]), [tp])

        prog.stage("dense3")
        tw = a["L1_gnn_trans_weight"]
        prm = load_rows([(wcol(2), row_bcast(a["L1_gnn_trans_bias"])), (wcol(3), row_bcast(a["L1_gnn_ln_gamma"])),
                         (wcol(4), row_bcast(a["L1_gnn_ln_beta"])), (wcol(6), row_bcast(a["L2_gnn_b2"])),
                         (wcol(7)[:, 0:1], bass.AP(a["L2_gnn_W1"].tensor, 0, [(1, P), (1, 1)])),
                         (wcol(7)[:, 1:2], bass.AP(a["L2_gnn_W1"].tensor, P, [(1, P), (1, 1)])),
                         (wcol(8)[:, 0:1], bass.AP(a["L2_gnn_b1"].tensor, 0, [(0, P), (1, 1)]))], [p2])
        prm.append(transpose_weight(0, tw[:, 0:P], 4, [p2], 0))
        prm.append(transpose_weight(1, tw[:, P:2 * P], 5, [p2], 1))
        prm.append(transpose_weight(5, a["L2_gnn_W2"], 6, [p2], 2))
        aggT = oh_e[:, :, :].rearrange("p a b -> p (a b)")[:, 0:NBB * P]
        x_free, st_free = [[], []], [[], []]
        hT_read, aggT_read, ps_read, prev_n, ln_prev, sc_read = [], [], [[], []], None, [], []
        tail = []
        xT_done = []
        for t in range(NBT):
            x3 = agg[:, t * NBB:(t + 1) * NBB, 0:P]
            sums = [pool_rows[:, (t % 2 * NSUM + k) * NBB * XW:(t % 2 * NSUM + k + 1) * NBB * XW] for k in range(NSUM)]
            lds = [dma("sp", lambda e, t=t, k=k, sums=sums: e.dma_start(sums[k].rearrange("p (b f) -> p b f", b=NBB),
                                                                      blocks(scatter_s[k], t)), [p2, prm, x_free[t % 2]])
                   for k in range(NSUM)]
            h = add("dve", lambda e, sums=sums: e.tensor_tensor(sums[0], sums[0], sums[1], ALU.add), [lds[0], lds[1]])
            h2 = add("dve", lambda e, sums=sums: e.tensor_tensor(sums[2], sums[2], sums[3], ALU.add), [lds[2], lds[3]])
            h = add("dve", lambda e, sums=sums: e.tensor_tensor(sums[0], sums[0], sums[2], ALU.add), [h, h2])
            s3d = sums[0].rearrange("p (b f) -> p b f", b=NBB)
            h = add("dve", lambda e, s3d=s3d: e.tensor_scalar(recip[:, 0:NBB], s3d[:, :, P + 1], 1e-20, None, ALU.add), [h, prev_n])
            h = add("dve", lambda e: e.reciprocal(recip[:, 0:NBB], recip[:, 0:NBB]), [h])
            a3 = s3d[:, :, 0:P]
            h = add("dve", lambda e, a3=a3: e.tensor_tensor(a3, a3, view(recip[:, :], [(1, NBB), (0, P)]), ALU.mult), [h])
            prev_n = h
            ld = []
            tx = transposed(x3, 0, [ld, prm], [hT_read])
            ta = []
            for q, (lo, hi) in enumerate(((0, 4), (4, NBB))):
                for k in range(lo, hi):
                    tp = add("pe", lambda e, k=k, q=q, lo=lo, a3=a3: e.transpose(bank[2 + q][:, (k - lo) * P:(k - lo + 1) * P],
                                                                                a3[:, k, :], ident[:, :]), [h, aggT_read])
                ta.append(add("act", lambda e, q=q, lo=lo, hi=hi: e.copy(aggT[:, lo * P:hi * P], bank[2 + q][:, 0:(hi - lo) * P]),
                              [tp, aggT_read]))
            evs = []
            for q, (lo, hi) in enumerate(((0, 4), (4, NBB))):
                for k in range(lo, hi):
                    o = bank[4 + q][:, (k - lo) * P:(k - lo + 1) * P]
                    add("pe", lambda e, k=k, o=o: e.matmul(o, hT[0][:, k * P:(k + 1) * P], wcol(0), start=True, stop=False),
                        [tx, ta, prm, ps_read[q]])
                    mm = add("pe", lambda e, k=k, o=o: e.matmul(o, aggT[:, k * P:(k + 1) * P], wcol(1), start=False, stop=True), [])
                evs.append(add("dve", lambda e, q=q, lo=lo, hi=hi, a3=a3: e.tensor_tensor(
                    a3[:, lo:hi, :], bank[4 + q][:, 0:(hi - lo) * P].rearrange("p (k f) -> p k f", f=P),
                    view(wcol(2), [(0, hi - lo), (1, P)]), ALU.add), [mm, ta]))
                ps_read[q] = evs[-1]
            aggT_read = mm
            ln = layer_norm(a3, [evs, ln_prev], 0)
            g1 = add("dve", lambda e, a3=a3: e.tensor_tensor(a3, a3, bias3(3), ALU.mult), [ln])
            g2 = bias_add(a3, a3, 4, [g1])
            g3 = add("dve", lambda e, a3=a3, x3=x3: e.tensor_tensor(a3, a3, x3, ALU.add), [g2, ld])
            ln = layer_norm(a3, [g3], 0)
            ln_prev = ln
            sx = dma("sp", lambda e, t=t, a3=a3: e.dma_start(blocks(res[0], t), a3), [ln])
            tt = transposed(a3, 0, [ln], [mm])
            stage = agg
            s3 = tile3(2 + t % 2)
            for q, (lo, hi) in enumerate(((0, 4), (4, NBB))):
                for k in range(lo, hi):
                    m1 = add("pe", lambda e, k=k, q=q, lo=lo: e.matmul(bank[6 + q][:, (k - lo) * P:(k - lo + 1) * P],
                                                                       hT[0][:, k * P:(k + 1) * P], wcol(5), start=True, stop=True),
                             [tt, sc_read])
            for k in range(NBB):
                m2 = add("pe", lambda e, k=k: e.matmul(bank[2][:, 2 * k:2 * k + 2], hT[0][:, k * P:(k + 1) * P], wcol(7)[:, 0:2],
                                                       start=True, stop=True), [tt, ta, sc_read])
            hT_read = m2
            x_free[t % 2] = [tt, sx]
            e1 = [add("dve", lambda e, q=q, lo=lo, hi=hi, x3=x3: e.tensor_tensor(
                x3[:, lo:hi, :], bank[6 + q][:, 0:(hi - lo) * P].rearrange("p (k f) -> p k f", f=P),
                view(wcol(6), [(0, hi - lo), (1, P)]), ALU.add), [m1, sx, tt]) for q, (lo, hi) in enumerate(((0, 4), (4, NBB)))]
            ps = bank[2][:, 0:2 * NBB].rearrange("p (k s) -> p k s", s=2)
            e2 = add("dve", lambda e, t=t, ps=ps: e.tensor_scalar(dst_score[:, t * NBB:(t + 1) * NBB], ps[:, :, 0], wcol(8)[:, 0:1], None,
                                                                 ALU.add), [m2])
            e3 = add("dve", lambda e, t=t, ps=ps: e.tensor_copy(agg[:, t * NBB:(t + 1) * NBB, P], ps[:, :, 1]), [m2])
            sc_read = [e1, e2, e3]
            aggT_read = [aggT_read, e2, e3]
            st = dma("sp", lambda e, t=t: e.dma_start(blocks(gather_s2, t), agg[:, t * NBB:(t + 1) * NBB, 0:P + 1]), [e1, e3])
            tail += [st, sx, e1, e2, e3]
        p3 = edge_pass("L2", gather_s2, 1, False, True, [tail])

        prog.stage("dense4")
        prm = [transpose_weight(k, a["L2_gnn_w_ih"][k * P:(k + 1) * P, :], 4 + k, [p3], k) for k in range(3)]
        prm += [transpose_weight(3 + k, a["L2_gnn_w_hh"][k * P:(k + 1) * P, :], 7 + k if k < 2 else 3, [p3], 3 + k) for k in range(3)]
        prm += load_rows([(wcol(6, 3), row_bcast(a["L2_gnn_b_ih"], 0, 3 * P)), (lrelu[:, 0, 0:3 * P], row_bcast(a["L2_gnn_b_hh"], 0, 3 * P)),
                          (wcol(9), a["L3_gnn_W_src"]), (wcol(10), a["L3_gnn_W_dst"]),
                          (att[:, :], a["attn_row"] if "attn_row" in a else row_bcast(a["L3_gnn_attn"]))], [p3])
        prm.append(add("dve", lambda e: e.tensor_tensor(wcol(6, 2), wcol(6, 2), lrelu[:, 0, 0:2 * P], ALU.add), [prm]))
        bhn = lrelu[:, 0, 2 * P:3 * P]
        oeT = oh_e[:, :, :].rearrange("p a b -> p (a b)")[:, 0:NBB * P]
        rz = tile3(4), tile3(5)
        tmp3, msk3 = tile3(6), tile3(7)
        mask = xw[:, 0, 0:NBB]
        nmask = xw[:, 0, 16:16 + NBB]
        bb3 = lambda ap: view(ap, [(0, NBB), (1, P)])
        every = []
        x_free, st_free = [[], []], [[], []]
        tail = []
        for t in range(NBT):
            a3 = agg[:, t * NBB:(t + 1) * NBB, 0:P]
            x3 = tile3(t % 2)
            ld = dma("sp", lambda e, t=t, x3=x3: e.dma_start(x3, blocks(res[0], t)), [p3, prm, x_free[t % 2]])
            mk = add("dve", lambda e, t=t: e.tensor_scalar(mask, agg[:, t * NBB:(t + 1) * NBB, P + 1], 0.0, None, ALU.is_gt), [p3, every])
            mk2 = add("dve", lambda e: e.tensor_scalar(nmask, mask, -1.0, 1.0, ALU.mult, ALU.add), [mk])
            h = normalise(t, 1, 0.0, [p3, every], guard=1e-30)
            h1 = add("dve", lambda e, a3=a3: e.tensor_scalar(tmp3, a3, 0.0, None, ALU.min), [h, prm, every])
            h2 = add("act", lambda e: e.activation(tmp3, tmp3, ACT.Exp), [h1])
            h3 = add("dve", lambda e, a3=a3: e.tensor_scalar(a3, a3, 0.0, -1.0, ALU.max, ALU.add), [h1])
            h4 = add("dve", lambda e, a3=a3: e.tensor_tensor(a3, a3, tmp3, ALU.add), [h2, h3])
            h5 = add("dve", lambda e, a3=a3: e.tensor_tensor(a3, a3, view(mask, [(1, NBB), (0, P)]), ALU.mult), [h4, mk])
            h6 = add("dve", lambda e, x3=x3: e.tensor_tensor(msk3, x3, view(nmask, [(1, NBB), (0, P)]), ALU.mult), [ld, mk2, every])
            oe = add("dve", lambda e, a3=a3: e.tensor_tensor(a3, a3, msk3, ALU.add), [h5, h6])
            tx = transposed(x3, 0, [ld, prm], [every])
            to = []
            for q, (lo, hi) in enumerate(((0, 4), (4, NBB))):
                for k in range(lo, hi):
                    tp = add("pe", lambda e, k=k, q=q, lo=lo, a3=a3: e.transpose(bank[2 + q][:, (k - lo) * P:(k - lo + 1) * P],
                                                                                a3[:, k, :], ident[:, :]), [oe, every])
                to.append(add("act", lambda e, q=q, lo=lo, hi=hi: e.copy(oeT[:, lo * P:hi * P], bank[2 + q][:, 0:(hi - lo) * P]),
                              [tp, every]))
            evs = []
            bread = {}
            for k in range(NBB):
                B = bank[4 + k % 4]
                wait = [tx, to, prm, every, bread.get(k % 4, [])]
                add("pe", lambda e, k=k, B=B: e.matmul(B[:, 0:2 * P], oeT[:, k * P:(k + 1) * P], wcol(0, 2), start=True, stop=False), wait)
                add("pe", lambda e, k=k, B=B: e.matmul(B[:, 0:2 * P], hT[0][:, k * P:(k + 1) * P], wcol(3, 2), start=False, stop=True), [])
                add("pe", lambda e, k=k, B=B: e.matmul(B[:, 2 * P:3 * P], oeT[:, k * P:(k + 1) * P], wcol(2), start=True, stop=True), [])
                mm = add("pe", lambda e, k=k, B=B: e.matmul(B[:, 3 * P:4 * P], hT[0][:, k * P:(k + 1) * P], wcol(5), start=True, stop=True), [])
                rzk = node_tile(4)[:, 0:1]
                v1 = add("dve", lambda e, k=k, B=B: e.tensor_tensor(view(tile3(4)[:, k, :], [(NBB * P, 2), (1, P)]),
                                                                    B[:, 0:2 * P].rearrange("p (s f) -> p s f", s=2),
                                                                    wcol(6, 2).rearrange("p (s f) -> p s f", s=2), ALU.add), [mm])
                v2 = add("dve", lambda e, k=k, B=B: e.tensor_tensor(msk3[:, k, :], B[:, 2 * P:3 * P], wcol(8), ALU.add), [mm, oe])
                v3 = add("dve", lambda e, k=k, B=B: e.tensor_tensor(tmp3[:, k, :], B[:, 3 * P:4 * P], bhn, ALU.add), [mm, h4])
                bread[k % 4] = [v1, v2, v3]
                evs.append([v1, v2, v3])
            r1 = add("act", lambda e: e.activation(view(node_tile(4), [(1, 2 * NBB * P)]), view(node_tile(4), [(1, 2 * NBB * P)]),
                                                   ACT.Tanh, scale=0.5), [evs])
            r2 = add("dve", lambda e: e.tensor_scalar(view(node_tile(4), [(1, 2 * NBB * P)]), view(node_tile(4), [(1, 2 * NBB * P)]),
                                                      0.5, 0.5, ALU.mult, ALU.add), [r1])
            n1 = add("dve", lambda e: e.tensor_tensor(tmp3, tmp3, rz[0], ALU.mult), [r2])
            n2 = add("dve", lambda e: e.tensor_tensor(tmp3, tmp3, msk3, ALU.add), [n1])
            n3 = add("act", lambda e: e.activation(tmp3, tmp3, ACT.Tanh), [n2])
            o1 = add("dve", lambda e: e.tensor_scalar(rz[0], rz[1], -1.0, 1.0, ALU.mult, ALU.add), [n1, r2])
            o2 = add("dve", lambda e: e.tensor_tensor(tmp3, tmp3, rz[0], ALU.mult), [n3, o1])
            o3 = add("dve", lambda e, x3=x3: e.tensor_tensor(rz[1], rz[1], x3, ALU.mult), [o1])
            o4 = add("dve", lambda e: e.tensor_tensor(tmp3, tmp3, rz[1], ALU.add), [o2, o3])
            o5 = add("dve", lambda e, a3=a3, x3=x3: e.tensor_tensor(a3, tmp3, x3, ALU.add), [o4, to])
            ln = layer_norm(a3, [o5], 0)
            sx = dma("sp", lambda e, t=t, a3=a3: e.dma_start(blocks(res[1], t), a3), [ln])
            tt = transposed(a3, 0, [ln], [mm, tx])
            ev, st = two_sided(t, 9, None, None, [tt, prm], [evs] * 4, tile3(2 + t % 2), [st_free[t % 2], prm], gather_c)
            st_free[t % 2] = [st]
            x_free[t % 2] = [o5, tx, h6]
            every = [ev]
            tail += [st, sx, ev]
        p4 = edge_pass("L3", gather_c, 8, True, True, [tail])

        prog.stage("dense5")
        prm = load_rows([(wcol(0), a["L3_gnn_W_out"]), (wcol(1), row_bcast(a["L3_gnn_b_out"])),
                         (wcol(2), row_bcast(a["L3_gnn_gamma"])), (wcol(3), row_bcast(a["L3_gnn_beta"]))], [p4])
        x_free, n_free = [[], []], [[], []]
        prev_n, ps_read, ht_read, ln_prev = None, [[], []], [], []
        tail = []
        for t in range(NBT):
            a3 = agg[:, t * NBB:(t + 1) * NBB, 0:P]
            x3, n3_ = tile3(t % 2), tile3(2 + t % 2)
            ld = dma("sp", lambda e, t=t, x3=x3: e.dma_start(x3, blocks(res[1], t)), [p4, x_free[t % 2]])
            h = normalise(t, 8, 1e-8, [p4, prev_n])
            hw = P // 8
            muls = []
            for k in range(NBB):
                muls.append(add("dve", lambda e, k=k, t=t, n3_=n3_: e.tensor_tensor(
                    n3_[:, k, :].rearrange("p (h d) -> p h d", h=8), view(agg[:, t * NBB + k, :], [(hw + 1, 8), (1, hw)]),
                    view(recip[:, k * 8:], [(1, 8), (0, hw)]), ALU.mult), [h, n_free[t % 2]]))
            prev_n = muls
            tt = transposed(n3_, 0, [muls, prm], [ht_read])
            n_free[t % 2] = tt
            evs = []
            for q, (lo, hi) in enumerate(((0, 4), (4, NBB))):
                for k in range(lo, hi):
                    mm = add("pe", lambda e, k=k, q=q, lo=lo: e.matmul(bank[4 + q][:, (k - lo) * P:(k - lo + 1) * P],
                                                                       hT[0][:, k * P:(k + 1) * P], wcol(0), start=True, stop=True),
                             [tt, prm, ps_read[q]])
                evs.append(add("dve", lambda e, q=q, lo=lo, hi=hi, a3=a3: e.tensor_tensor(
                    a3[:, lo:hi, :], bank[4 + q][:, 0:(hi - lo) * P].rearrange("p (k f) -> p k f", f=P),
                    view(wcol(1), [(0, hi - lo), (1, P)]), ALU.add), [mm, muls]))
                ps_read[q] = evs[-1]
            ht_read = mm
            h = add("dve", lambda e, a3=a3, x3=x3: e.tensor_tensor(a3, a3, x3, ALU.add), [evs, ld])
            ln = layer_norm(a3, [h, ln_prev], 0)
            h = add("dve", lambda e, a3=a3: e.tensor_tensor(a3, a3, bias3(2), ALU.mult), [ln])
            h = bias_add(a3, a3, 3, [h])
            h = add("dve", lambda e, a3=a3, x3=x3: e.tensor_tensor(a3, a3, x3, ALU.add), [h])
            x_free[t % 2] = h
            ln = layer_norm(a3, [h], 0)
            ln_prev = ln
            lo, hi = t * NBB * P, (t + 1) * NBB * P
            if hi <= N:
                tail.append(dma("sp", lambda e, a3=a3, lo=lo, hi=hi: e.dma_start(out[lo:hi, :].rearrange("(b p) f -> p b f", p=P), a3), [ln]))
            else:
                full = (N - lo) // P
                rem = N - lo - full * P
                if full:
                    tail.append(dma("sp", lambda e, a3=a3, lo=lo, full=full: e.dma_start(
                        out[lo:lo + full * P, :].rearrange("(b p) f -> p b f", p=P), a3[:, 0:full, :]), [ln]))
                if rem:
                    tail.append(dma("sp", lambda e, a3=a3, lo=lo, full=full, rem=rem: e.dma_start(
                        out[lo + full * P:N, :], a3[0:rem, full, :]), [ln]))
        prog.queue["sp"].append(lambda eng, last, w=list(flat(tail)): [eng.wait_ge(x.sem, x.value) for x in w])

        block = ctx.enter_context(nc.Block())

        @block.sync
        def _(eng):
            prog.play("sp", eng)

        @block.gpsimd
        def _(eng):
            prog.play("pool", eng)

        @block.scalar
        def _(eng):
            prog.play("act", eng)

        @block.vector
        def _(eng):
            prog.play("dve", eng)

        @block.tensor
        def _(eng):
            prog.play("pe", eng)


def kernel(**inputs):
    import numpy as _np
    import concourse.bacc as _bacc
    from concourse import mybir as _mybir
    from concourse.bass_utils import run_bass_kernel_spmd as _run

    x = _np.ascontiguousarray(inputs["x"])
    n_nodes, n_edges = x.shape[0], inputs["src"].shape[0]
    nb = -(-n_nodes // P)
    t_real = -(-n_edges // P)
    sc = -(-(t_real + nb) // P)
    pad = sc * P * P - n_edges
    src = _np.concatenate([_np.asarray(inputs["src"]), _np.full(pad, nb * P - 1, _np.int32)]).reshape(sc * P, P)
    dst = _np.concatenate([_np.asarray(inputs["dst"]), _np.full(pad, nb * P - 1, _np.int32)]).reshape(sc * P, P)
    arrays = {name: _np.ascontiguousarray(v) for name, v in inputs.items() if name not in ("x", "src", "dst")}
    arrays.update(x=x, src=src, dst=dst)
    k = _np.arange(P)
    arrays["c_ident"] = _np.eye(P, dtype=_np.float32)
    arrays["c_iota"] = _np.tile(k.astype(_np.float32), (P, 1))
    arrays["c_ohw"] = _np.stack([k * 0 + 1, k * 0 + 1, -2 * k, (k * k) // 256 * 256, (k * k) % 256]).astype(_mybir.dt.np(BF16))
    arrays["c_ohs"] = _np.concatenate([_np.stack([k * 0 + 1, k * 0 + 1, -2 * k, k * 0, (k * k) // 256 * 256, (k * k) % 256]),
                                       _np.repeat(_np.array([[0], [0], [1], [1], [0], [0]]), P, 1)], 1).astype(_mybir.dt.np(BF16))
    arrays["c_dump"] = (nb * P + k[:, None]).astype(_np.float32)
    arrays["c_tril"] = (k[None, :] < k[:, None]).astype(_np.float32)
    arrays["c_steps"] = (_np.arange(sc)[None, :] * P + k[:, None]).astype(_np.float32)

    nc = _bacc.Bacc("TRN2", target_bir_lowering=False, num_devices=1)
    feed, args = {}, {"t_real": t_real}
    for name, v in arrays.items():
        feed[f"in_{name}_dram"] = v
        args[name] = nc.dram_tensor(f"in_{name}_dram", v.shape, _mybir.dt.from_np(v.dtype), kind="ExternalInput").ap()
    out = nc.dram_tensor("out_0_dram", x.shape, F32, kind="ExternalOutput").ap()
    build(nc, args, out)
    r = _run(nc, [feed], core_ids=[0])
    return r.results[0]["out_0_dram"]
```

```python
from contextlib import ExitStack

import concourse.bass as bass
from concourse import mybir

F32 = mybir.dt.float32
BF16 = mybir.dt.bfloat16
I32 = mybir.dt.int32
ALU = mybir.AluOpType
ACT = mybir.ActivationFunctionType
AX = mybir.AxisListType

ENGINE = {"dve": mybir.EngineType.DVE, "pe": mybir.EngineType.PE}

P = 128
NEG = -1.0e30
SLOPE = 0.2
LN_EPS = 1e-5
G = 16
U = 4
CH = 4
NCH = G // CH
AW = 136
XW = 130
NSUM = 4
NBB = 7


def view(ap, free):
    return bass.AP(ap.tensor, ap.offset, [tuple(ap.ap[0])] + [tuple(f) for f in free])


class Done:

    def __init__(self, sem, value):
        self.sem, self.value = sem, value


class Program:
    ENGINES = ("pe", "act", "dve", "pool", "sp")
    DMA_RING = 8

    def __init__(self, nc, ctx):
        self.nc, self.ctx = nc, ctx
        self.queue = {e: [] for e in self.ENGINES}
        self.stage("start")
        self.ring = {e: [self.sem(f"{e}_dma{n}") for n in range(self.DMA_RING)] for e in ("sp", "pool")}
        self.ring_n = {e: 0 for e in ("sp", "pool")}
        self.anchor = self.sem("wait_anchor")

    def sem(self, name):
        return self.ctx.enter_context(self.nc.semaphore(name))

    def stage(self, name):
        self.name = name
        self.done_sem = {}
        self.count = {e: 0 for e in self.ENGINES}

    def engine_sem(self, e):
        if e not in self.done_sem:
            self.done_sem[e] = self.sem(f"{self.name}_{e}_done")
        return self.done_sem[e]

    def add(self, e, fn, after=()):
        sem = self.engine_sem(e)
        self.count[e] += 1
        waits = list(flat(after))

        def emit(eng, last):
            for w in waits:
                if last.get(id(w.sem), 0) < w.value:
                    eng.wait_ge(w.sem, w.value)
                    last[id(w.sem)] = w.value
            fn(eng).then_inc(sem, 1)

        self.queue[e].append(emit)
        return Done(sem, self.count[e])

    def dma(self, e, fn, after=()):
        n = self.ring_n[e]
        self.ring_n[e] += 1
        sem, turn = self.ring[e][n % self.DMA_RING], n // self.DMA_RING
        waits = list(flat(after)) + ([Done(sem, 16 * turn)] if turn else [])

        def emit(eng, last):
            for w in waits:
                if last.get(id(w.sem), 0) < w.value:
                    eng.wait_ge(w.sem, w.value)
                    last[id(w.sem)] = w.value
            fn(eng).then_inc(sem, 16)

        self.queue[e].append(emit)
        return Done(sem, 16 * (turn + 1))

    def play(self, e, eng):
        last = {}
        for emit in self.queue[e]:
            emit(eng, last)


def flat(x):
    if isinstance(x, (Done, tuple)) and not isinstance(x, list) and (isinstance(x, Done)):
        yield x
        return
    for y in x:
        if y is None:
            continue
        if isinstance(y, Done):
            yield y
        else:
            yield from flat(y)


class Op:

    def __init__(self, e, fn, after, lag, anchored):
        self.e, self.fn, self.after, self.lag, self.anchored = e, fn, after, lag, anchored
        self.counted = False


class SlotDma(Op):

    def __init__(self, e, fn, after, sems, base, gain):
        super().__init__(e, fn, after, 0, True)
        self.sems, self.base, self.gain = sems, base, gain


class Loop:

    PEELED = 2 * U

    def __init__(self, prog, n):
        self.prog, self.n, self.ops = prog, n, []
        assert n % U == 0 and n > self.PEELED

    def op(self, e, fn, after=(), lag=0, anchored=False):
        o = Op(e, fn, [(a, 0) if isinstance(a, Op) else a for a in after if a is not None], lag, anchored)
        self.ops.append(o)
        return o

    def slot_dma(self, e, fn, after, sems, base, gain):
        o = SlotDma(e, fn, [(a, 0) if isinstance(a, Op) else a for a in after], sems, base, gain)
        self.ops.append(o)
        return o

    def active(self, o, turn):
        return 0 <= turn - o.lag < self.n

    def close(self):
        prog = self.prog
        for o in self.ops:
            for p, _ in o.after:
                if not isinstance(p, SlotDma):
                    p.counted = True
        self.depth = max(o.lag for o in self.ops)
        self.end = self.n + self.depth
        counted = [o for o in self.ops if o.counted]
        self.per = {}
        for o in counted:
            self.per[o.e] = self.per.get(o.e, 0) + 1
            o.pos = self.per[o.e]
        self.counted = counted
        self.sems = {e: prog.engine_sem(e) for e in self.per}
        self.filled = {e: sum(self.active(o, t) for o in counted if o.e == e for t in range(self.depth)) for e in self.per}
        for e in prog.ENGINES:
            prog.queue[e].append(lambda eng, last, e=e: self.play(e, eng, last))
        for e in self.per:
            prog.count[e] += self.per[e] * self.n

    def last(self, o):
        return Done(self.sems[o.e], self.value(o, self.n - 1 + o.lag))

    def value(self, p, turn):
        if not self.active(p, turn):
            return None
        mine = [o for o in self.counted if o.e == p.e]
        return (sum(min(max(turn - o.lag, 0), self.n) for o in mine)
                + sum(self.active(o, turn) for o in mine if o.pos <= p.pos))

    def play(self, e, eng, last):
        ops = [o for o in self.ops if o.e == e]
        if not ops:
            return
        prog = self.prog
        seen = {}

        def run(o, i, u, reg, j):
            for p, d in o.after:
                if isinstance(p, SlotDma):
                    sem = p.sems[(u - d) % U]
                    if reg is None:
                        if not self.active(p, i - d):
                            continue
                        const, step = p.base + p.gain * ((i - d) // U + 1), 0
                    else:
                        const, step = p.base + p.gain * ((u - d) // U + 1), p.gain
                else:
                    sem = self.sems[p.e]
                    if reg is None:
                        const, step = self.value(p, i - d), 0
                        if const is None:
                            continue
                    else:
                        const = self.filled[p.e] + self.per[p.e] * (u - d - self.depth) + p.pos
                        step = self.per[p.e] * U
                key = id(sem)
                if key in seen and seen[key] >= const:
                    continue
                seen[key] = const
                if reg is None:
                    eng.wait_ge(sem, const)
                else:
                    eng.wait_ge(sem, j * step + const)
                    if o.anchored:
                        eng.sem_inc(prog.anchor, 1)
            ins = o.fn(eng, u, i)
            if o.counted and not isinstance(o, SlotDma):
                ins.then_inc(self.sems[e], 1)

        for i in range(self.PEELED):
            for o in ops:
                if self.active(o, i):
                    run(o, i, i % U, None, None)
        seen.clear()
        with eng.Fori(self.PEELED // U, self.n // U) as j:
            for u in range(U):
                for o in ops:
                    run(o, j * U + u, u, True, j)
        seen.clear()
        for i in range(self.n, self.end):
            for o in ops:
                if self.active(o, i):
                    run(o, i, i % U, None, None)
        last.clear()


def build(nc, a, out):
    N = a["x"].shape[0]
    T = a["src"].shape[0]
    NB = -(-N // P)
    T_REAL = a["t_real"]
    SC = -(-(T_REAL + NB) // P)
    S = SC * P
    NG = S // G
    NEED_PAD = NB * P - N
    assert T == S and NG % U == 0 and NB % NBB == 0
    GC = P // G

    def dram(name, shape, dt=F32):
        return nc.dram_tensor(name, shape, dt).ap()

    ET = 5 * G
    edge_tab = dram("edge_tab", (NG, P, ET))
    onehot_tab = dram("onehot_tab", (3, S * P), BF16)
    source_tab = dram("source_tab", (4, S * P), BF16)
    step_tab = dram("step_tab", (S, 2 * P + 2))
    col_tab = dram("col_tab", (3 * SC, P))
    R1, R8 = 2 * G + 1 + 2 * G, 8 * (2 * G + 1) + 2 * G
    row_tab1 = dram("row_tab1", (NG, R1))
    row_tab8 = dram("row_tab8", (NG, R8))
    gather_a = dram("gather_a", (NB * P, P))
    gather_b = dram("gather_b", (NB * P, P))
    gather_c = dram("gather_c", (NB * P, P))
    scatter_s = [dram(f"scatter_s{k}", (NB * P + P, XW)) for k in range(NSUM)]
    gather_s2 = dram("gather_s2", (NB * P, P + 1))
    res = [dram(f"residual{n}", (NB * P, P)) for n in range(2)]

    with ExitStack() as ctx:
        prog = Program(nc, ctx)
        add, dma = prog.add, prog.dma

        def sb(name, shape, dt=F32):
            return ctx.enter_context(nc.sbuf_tensor(name, shape, dt))

        bank = [ctx.enter_context(nc.psum_tensor(f"bank{n}", [P, 512], F32)) for n in range(8)]

        ident = sb("ident", [P, P])
        iota = sb("iota", [P, P])
        ones = sb("ones", [P, P])
        oh_w = sb("oh_w", [5, P], BF16)
        minus_half = sb("minus_half", [P, NBB])
        agg = sb("agg", [P, NB, AW])
        dst_side = sb("dst_side", [P, max(NB, 64), P])
        dst_score = sb("dst_score", [P, NB])
        rows = sb("rows", [P, U, G, XW])
        lrelu = sb("lrelu", [P, 2, CH * P])
        oh_t = sb("oh_t", [P, 2, CH * P])
        oh_e = sb("oh_e", [P, 8, P])
        xw = sb("xw", [P, 2, CH * AW])
        edge_sb = sb("edge_sb", [P, U, ET])
        oh_ws = sb("oh_ws", [6, 2 * P], BF16)
        dump_row = sb("dump_row", [P, 1])
        oh_rows = sb("oh_rows", [5, U, G * P], BF16)
        step_sb = sb("step_sb", [P, U, 2 * P + 2])
        row_sb = sb("row_sb", [1, U, R8])
        param = sb("param", [P, 12 * P])
        att = sb("att", [P, P])
        logit = sb("logit", [P, P])
        masked = sb("masked", [P, 2, P])
        seg_fwd = sb("seg_fwd", [P, P])
        seg_max = sb("seg_max", [P, P])
        run_max = sb("run_max", [P, P])
        shifted = sb("shifted", [P, P])
        weight = sb("weight", [P, 2, P])
        minus_w = sb("minus_w", [P, 2, G])
        rescale = sb("rescale", [P, 2, P])
        decay_m = sb("decay_m", [P, P])
        carry = sb("carry", [1, 8 * (G + 1)])
        carry_in = sb("carry_in", [1, 8 * (G + 1)])
        cin_row = sb("cin_row", [1, P])
        cin = sb("cin", [P, 4])
        acc_tmp = sb("acc_tmp", [P, 2, AW])
        stats = sb("stats", [P, NBB, 6])
        moments = sb("moments", [P, NBB, 2])
        rstd = sb("rstd", [P, 2, NBB])
        recip = sb("recip", [P, 8 * NBB])
        col3 = sb("col3", [P, 3 * SC])

        s_tab = [prog.sem(f"tables_in_slot{u}") for u in range(U)]
        s_gat = [[prog.sem(f"rows_in_slot{u}_chunk{c}") for u in range(U)] for c in range(NCH)]
        tab_base = [0]
        gat_base = [0]

        prog.stage("prep")
        ld_id = dma("sp", lambda e: e.dma_start(ident[:, :], a["c_ident"]))
        ld_iota = dma("sp", lambda e: e.dma_start(iota[:, :], a["c_iota"]))
        ld_ohw = dma("sp", lambda e: e.dma_start(oh_w[:, :], a["c_ohw"]))
        ld_ohs = dma("sp", lambda e: e.dma_start(oh_ws[:, :], a["c_ohs"]))
        ld_dump = dma("sp", lambda e: e.dma_start(dump_row[:, :], a["c_dump"]))
        big1 = agg[:, :, :].rearrange("p a b -> p (a b)")
        big2 = dst_side[:, :, :].rearrange("p a b -> p (a b)")
        pool_rows = rows[:, :, :, :].rearrange("p a b c -> p (a b c)")
        step_no = col3[:, 0:SC]
        ld_sn = dma("sp", lambda e: e.dma_start(pool_rows[:, 0:SC], a["c_steps"]))
        first_i = pool_rows[:, 32:32 + SC].bitcast(I32)

        def load_first(e):
            with nc.allow_non_contiguous_dma(reason="first node of each tile"):
                return e.dma_start(first_i, a["dst"][:, 0:1].rearrange("(c p) o -> p (c o)", p=P))
        ld_first = dma("sp", load_first)
        m_ones = add("dve", lambda e: e.memset(ones[:, :], 1.0))
        m_half = add("dve", lambda e: e.memset(minus_half[:, :], -0.5))
        m_oh = add("dve", lambda e: e.memset(oh_rows[:, :, :], 1.0))
        m_rows = None
        fb = pool_rows[:, 64:64 + SC]
        fbi = pool_rows[:, 96:96 + SC].bitcast(I32)
        keyc = pool_rows[:, 128:128 + SC]
        snum = pool_rows[:, 0:SC]
        tcol = pool_rows[:, 160:160 + SC]
        tcoli = sb("tcoli", [P, SC], I32)
        bcol = pool_rows[:, 192:192 + SC]
        b128 = pool_rows[:, 224:224 + SC]
        h = add("dve", lambda e: e.tensor_single_scalar(fbi, first_i, 7, ALU.arith_shift_right), [ld_first])
        h = add("dve", lambda e: e.tensor_copy(fb, fbi), [h])
        key_done = add("dve", lambda e: e.tensor_tensor(keyc, fb, snum, ALU.add), [h, ld_sn])
        key = big2[:, 0:S]
        compare = big2[:, S:2 * S]
        kcol = big2[:, 2 * S:2 * S + SC * P]
        spread = []
        for c in range(SC):
            spread.append(add("dve", lambda e, c=c: e.tensor_scalar(kcol[:, c * P:(c + 1) * P], ones[:, :],
                                                                  keyc[:, c:c + 1], None, ALU.mult), [key_done, m_ones]))
        key_copied = []
        for c in range(SC):
            mm = add("pe", lambda e, c=c: e.matmul(bank[c % 8][:, 0:P], kcol[:, c * P:(c + 1) * P], ident[:, :],
                                                 start=True, stop=True),
                     [spread[c], ld_id, key_copied[c - 8:c - 7] if c >= 8 else []])
            key_copied.append(add("act", lambda e, c=c: e.copy(key[:, c * P:(c + 1) * P], bank[c % 8][:, 0:P]), [mm]))
        last = None
        for c in range(SC):
            h = add("dve", lambda e, c=c: e.tensor_scalar(compare[:, 1:], key[:, 1:], snum[:, c:c + 1], None, ALU.is_le),
                    [key_copied, last])
            last = add("dve", lambda e, c=c: e.tensor_reduce(tcol[:, c:c + 1], compare[:, 1:], AX.X, ALU.add), [h])
        t_int = add("dve", lambda e: e.tensor_copy(tcoli[:, :], tcol), [last])
        h = add("dve", lambda e: e.tensor_tensor(bcol, snum, tcol, ALU.subtract), [last])
        blk_done = add("dve", lambda e: e.tensor_scalar(bcol, bcol, float(NB - 1), None, ALU.min), [h])
        b128_done = add("dve", lambda e: e.tensor_scalar(b128, bcol, float(P), None, ALU.mult), [blk_done])
        c3b = add("dve", lambda e: e.tensor_copy(col3[:, 0:SC], bcol), [blk_done])

        NR = 2
        base = 256
        W1 = 2 * P + 2

        def tile_set(k):
            o = base + k * 2560
            f = lambda n, w: pool_rows[:, o + n:o + n + w]
            return dict(di=f(0, P).bitcast(I32), si=f(P, P).bitcast(I32), d=f(2 * P, P), s=f(3 * P, P),
                        rel=f(4 * P, P), sq=f(5 * P, P), sqi=f(6 * P, P).bitcast(I32), lo=f(7 * P, P),
                        st=f(8 * P, W1), hl=f(8 * P + W1, 3 * P // 2).bitcast(BF16),
                        qi=f(12 * P, P).bitcast(I32), q=f(13 * P, P), r=f(14 * P, P), rr=f(15 * P, P),
                        rri=f(16 * P, P).bitcast(I32), rlo=f(17 * P, P), sl=f(18 * P, 2 * P).bitcast(BF16))
        edge_stage = big1[:, 0:NG * ET].rearrange("p (g k) -> p g k", k=ET)
        mtmp = big2[:, 3 * S:3 * S + P]
        prev = [None, None]
        st_saved = []
        edge_done = []
        relT_free = None
        for c in range(SC):
            t = tile_set(c % NR)
            g_d = dma("pool", lambda e, t=t, c=c: e.indirect_dma_start(
                t["di"], None, a["dst"], bass.IndirectOffsetOnAxis(ap=tcoli[:, c:c + 1], axis=0)), [t_int, prev[c % NR]])
            g_s = dma("pool", lambda e, t=t, c=c: e.indirect_dma_start(
                t["si"], None, a["src"], bass.IndirectOffsetOnAxis(ap=tcoli[:, c:c + 1], axis=0)), [t_int, prev[c % NR]])
            d_f = add("dve", lambda e, t=t: e.tensor_copy(t["d"], t["di"]), [g_d])
            s_f = add("dve", lambda e, t=t: e.tensor_copy(t["s"], t["si"]), [g_s])
            h = add("dve", lambda e, t=t, c=c: e.tensor_scalar(t["rel"], t["d"], b128[:, c:c + 1], float(P),
                                                              ALU.subtract, ALU.min), [d_f, b128_done])
            rel = add("dve", lambda e, t=t: e.tensor_scalar(t["rel"], t["rel"], -1.0, None, ALU.max), [h])
            p1 = add("dve", lambda e, t=t: e.memset(t["st"][:, 0:P + 1], NEG), [prev[c % NR]])
            p2 = add("dve", lambda e, t=t: e.tensor_tensor(t["st"][:, 1:P], t["d"][:, 1:P], t["d"][:, 0:P - 1],
                                                           ALU.not_equal), [p1, d_f])
            p3 = add("dve", lambda e, t=t: e.tensor_scalar(t["st"][:, 1:P], t["st"][:, 1:P], NEG, None, ALU.mult), [p2])
            p4 = add("dve", lambda e, t=t: e.tensor_scalar(t["st"][:, P + 1:2 * P + 1], t["d"], t["d"][:, 0:1], NEG,
                                                           ALU.not_equal, ALU.mult), [d_f])
            p5 = add("dve", lambda e, t=t: e.tensor_copy(t["st"][:, 2 * P + 1:2 * P + 2], t["rel"][:, 0:1]), [rel])
            st = dma("sp", lambda e, t=t, c=c: e.dma_start(step_tab[c * P:(c + 1) * P, :], t["st"]), [p3, p4, p5])
            h = add("dve", lambda e, t=t: e.tensor_tensor(t["sq"], t["rel"], t["rel"], ALU.mult), [rel])
            h = add("dve", lambda e, t=t: e.tensor_copy(t["sqi"], t["sq"]), [h])
            h = add("dve", lambda e, t=t: e.tensor_single_scalar(t["sqi"], t["sqi"], 255, ALU.bitwise_and), [h])
            h = add("dve", lambda e, t=t: e.tensor_copy(t["lo"], t["sqi"]), [h])
            q1 = add("dve", lambda e, t=t: e.tensor_tensor(t["hl"][:, 0:P], t["sq"], t["lo"], ALU.subtract), [h])
            q2 = add("dve", lambda e, t=t: e.tensor_copy(t["hl"][:, P:2 * P], t["lo"]), [h])
            q3 = add("dve", lambda e, t=t: e.tensor_copy(t["hl"][:, 2 * P:3 * P], t["rel"]), [rel])
            oh = dma("sp", lambda e, t=t, c=c: e.dma_start(
                onehot_tab[:, c * P * P:(c + 1) * P * P].rearrange("k (p n) -> p k n", p=P),
                t["hl"].rearrange("p (k n) -> p k n", k=3)), [q1, q2, q3])
            c1 = add("dve", lambda e, t=t, c=c: e.tensor_copy(col3[:, SC + c:SC + c + 1], t["d"][:, 0:1]), [d_f])
            c2 = add("dve", lambda e, t=t, c=c: e.tensor_copy(col3[:, 2 * SC + c:2 * SC + c + 1], t["d"][:, P - 1:P]), [d_f])
            qa = add("dve", lambda e, t=t: e.tensor_single_scalar(t["qi"], t["si"], 7, ALU.arith_shift_right), [g_s])
            qf = add("dve", lambda e, t=t: e.tensor_copy(t["q"], t["qi"]), [qa])
            h = add("dve", lambda e, t=t: e.scalar_tensor_tensor(t["r"], t["q"], -float(P), t["s"], ALU.mult, ALU.add), [qf, s_f])
            rf = h
            h = add("dve", lambda e, t=t: e.tensor_tensor(t["rr"], t["r"], t["r"], ALU.mult), [h])
            h = add("dve", lambda e, t=t: e.tensor_copy(t["rri"], t["rr"]), [h])
            h = add("dve", lambda e, t=t: e.tensor_single_scalar(t["rri"], t["rri"], 255, ALU.bitwise_and), [h])
            h = add("dve", lambda e, t=t: e.tensor_copy(t["rlo"], t["rri"]), [h])
            r1 = add("dve", lambda e, t=t: e.tensor_tensor(t["sl"][:, 0:P], t["rr"], t["rlo"], ALU.subtract), [h])
            r2 = add("dve", lambda e, t=t: e.tensor_copy(t["sl"][:, P:2 * P], t["rlo"]), [h])
            r3 = add("dve", lambda e, t=t: e.tensor_copy(t["sl"][:, 2 * P:3 * P], t["r"]), [rf])
            r4 = add("dve", lambda e, t=t: e.tensor_scalar(t["sl"][:, 3 * P:4 * P], t["q"], float(P), None, ALU.mult), [qf])
            sv = dma("sp", lambda e, t=t, c=c: e.dma_start(
                source_tab[:, c * P * P:(c + 1) * P * P].rearrange("k (p n) -> p k n", p=P),
                t["sl"].rearrange("p (k n) -> p k n", k=4)), [r1, r2, r3, r4])
            tr = add("pe", lambda e, t=t, c=c: e.transpose(bank[c % 2][:, 0:P], t["rel"], ident[:, :]),
                     [rel, edge_done[-4:]])
            ts = add("pe", lambda e, t=t, c=c: e.transpose(bank[c % 2][:, P:2 * P], t["s"], ident[:, :]),
                     [s_f, edge_done[-4:]])
            ts = add("pe", lambda e, t=t, c=c: e.transpose(bank[c % 2][:, 2 * P:3 * P], t["q"], ident[:, :]), [qf])
            tr = ts
            es = edge_stage[:, c * GC:(c + 1) * GC, :]
            part = lambda n, es=es: es[:, :, n * G:(n + 1) * G]
            ps = lambda n, c=c: bank[c % 2][:, n * P:(n + 1) * P].rearrange("p (g k) -> p g k", k=G)
            e1 = add("dve", lambda e, part=part, ps=ps: e.tensor_copy(part(0).bitcast(I32), ps(1)), [ts])
            e2 = add("dve", lambda e, part=part, ps=ps: e.tensor_copy(part(1), ps(0)), [tr])
            e3 = add("dve", lambda e, part=part, ps=ps: e.tensor_scalar(part(2), ps(0), 0.0, NEG, ALU.is_lt, ALU.mult), [tr])
            mt = mtmp.rearrange("p (g k) -> p g k", k=G)
            e4 = add("dve", lambda e, ps=ps, mt=mt: e.tensor_scalar(mt, ps(0), P - 0.5, NEG, ALU.is_gt, ALU.mult),
                     [tr, relT_free])
            e5 = add("dve", lambda e, part=part, mt=mt: e.tensor_tensor(part(2), part(2), mt, ALU.add), [e3, e4])
            relT_free = e5
            e6 = add("dve", lambda e, part=part, ps=ps: e.tensor_copy(part(3), ps(1)), [ts])
            e7 = add("dve", lambda e, part=part, ps=ps: e.tensor_copy(part(4), ps(2)), [ts])
            edge_done += [e1, e2, e5, e7]
            prev[c % NR] = [tr, ts, st, oh, sv, c1, c2, p4, p5, q3, e7]
            st_saved += [st, oh, sv]
        edge_saved = dma("sp", lambda e: e.dma_start(edge_tab.rearrange("g p k -> p g k"), edge_stage), [edge_done])
        tc = add("pe", lambda e: e.transpose(bank[2][0:3 * SC, 0:P], col3[:, :], ident[:, :]), [c1, c2, c3b, key_copied])
        cc = add("dve", lambda e: e.tensor_copy(seg_fwd[0:3 * SC, :], bank[2][0:3 * SC, 0:P]), [tc])
        cs = dma("sp", lambda e: e.dma_start(col_tab, seg_fwd[0:3 * SC, :]), [cc])
        brow = view(big2[0:1, 0:3 * S], [(1, 3 * S)])
        cl = dma("sp", lambda e: e.dma_start(brow, col_tab.rearrange("(o a) b -> o (a b)", o=1)), [cs, last, relT_free])
        grp = lambda k: big2[0:1, k * S:(k + 1) * S].rearrange("o (g k) -> o g k", k=G)
        RA = 3 * G + 1
        rt = big2[0:1, 3 * S:3 * S + NG * RA].rearrange("o (g k) -> o g k", k=RA)
        prevlast = big2[0:1, 3 * S + NG * RA:3 * S + NG * RA + S]
        z1 = add("dve", lambda e: e.memset(prevlast[:, 0:1], -5.0), [cl])
        z2 = add("dve", lambda e: e.tensor_copy(prevlast[:, 1:S], big2[0:1, 2 * S:3 * S - 1]), [cl])
        pl = prevlast.rearrange("o (g k) -> o g k", k=G)
        z3 = add("dve", lambda e: e.tensor_tensor(rt[:, :, 1:G + 1], grp(2), pl, ALU.not_equal), [z1, z2])
        z4 = add("dve", lambda e: e.tensor_tensor(rt[:, :, G + 1:2 * G + 1], grp(1), pl, ALU.not_equal), [z1, z2])
        z5 = add("dve", lambda e: e.tensor_scalar(rt[:, :, 1:2 * G + 1], rt[:, :, 1:2 * G + 1], NEG, None, ALU.mult), [z3, z4])
        z6 = add("dve", lambda e: e.memset(rt[:, :, 0:1], NEG), [cl])
        z7 = add("dve", lambda e: e.tensor_scalar(rt[:, :, 2 * G + 1:RA].bitcast(I32), grp(0), float(AW), None, ALU.mult), [cl])
        z8 = add("dve", lambda e: e.tensor_scalar(grp(2).bitcast(I32), grp(0), float(P), None, ALU.mult), [z2, z3])
        row_saved = [dma("sp", lambda e: e.dma_start(row_tab1[:, 0:RA].rearrange("(o g) k -> o g k", o=1), rt), [z5, z6, z7])]
        for tb, off in ((row_tab1, RA), (row_tab8, R8 - G)):
            row_saved.append(dma("sp", lambda e, tb=tb, off=off: e.dma_start(
                tb[:, off:off + G].rearrange("(o g) k -> o g k", o=1), grp(2)), [z8]))
        for hd in range(8):
            row_saved.append(dma("sp", lambda e, hd=hd: e.dma_start(
                row_tab8[:, hd * (G + 1):(hd + 1) * (G + 1)].rearrange("(o g) k -> o g k", o=1), rt[:, :, 0:G + 1]), [z5, z6]))
            row_saved.append(dma("sp", lambda e, hd=hd: e.dma_start(
                row_tab8[:, 8 * (G + 1) + hd * G:8 * (G + 1) + (hd + 1) * G].rearrange("(o g) k -> o g k", o=1),
                rt[:, :, G + 1:2 * G + 1]), [z5]))
        row_saved.append(dma("sp", lambda e: e.dma_start(
            row_tab8[:, 8 * (2 * G + 1):R8 - G].rearrange("(o g) k -> o g k", o=1), rt[:, :, 2 * G + 1:RA]), [z7]))
        tables = [st_saved, edge_saved, row_saved, m_oh]
        idle = [tables, edge_done, prev[0], prev[1], tc]

        def load_offsets(L, e, at, unit, after, lag):
            box = {}

            def fn(eng, u, i):
                _, box["v"] = nc.values_load_multi_w_load_instructions(
                    row_sb[0:1, (u - lag) % U, at:at + G].bitcast(I32), engines=[ENGINE[e]], min_val=0, max_val=(NB - 1) * unit,
                    skip_runtime_bounds_check_because="the blocks are clamped to NB - 1 where the table is made")
            return L.op(e, fn, after, lag=lag, anchored=True), box

        def edge_pass(name, src_rows, heads, vector, ready):
            prog.stage(name)
            RW = heads * G
            width = P if vector else P + 1
            hw = P // heads
            aw = AW if heads > 1 else XW
            z_agg = add("dve", lambda e: e.memset(agg[:, :, :], 0.0), [ready])
            z_one = add("dve", lambda e: e.memset(rows[:, :, :, P:XW], 1.0), [ready])
            z_car = add("dve", lambda e: e.memset(carry[:, :], NEG), [ready])
            begin = [ready, z_agg, z_one, z_car]
            for e_ in prog.ENGINES:
                prog.queue[e_].append(lambda eng, last, w=list(flat(begin)): [eng.wait_ge(x.sem, x.value) for x in w
                                                                            if last.get(id(x.sem), 0) < x.value])
            prog.stage(name + "_loop")
            L = Loop(prog, NG)
            agg_flat = agg[:, :, :].rearrange("p a b -> p (a b)")
            dst_flat = dst_side[:, :, :].rearrange("p a b -> p (a b)")
            rw = R8 if heads > 1 else R1
            rt_ = row_tab8 if heads > 1 else row_tab1
            FC0, BL0 = heads * (G + 1), heads * (2 * G + 1)
            ntab = 3 + heads
            TB, GB = tab_base[0], gat_base[0]
            tab_base[0] += 16 * ntab * (NG // U)
            gat_base[0] += 16 * CH * (NG // U)

            def load_tables(e, u, i):
                e.dma_start(edge_sb[:, u, :], edge_tab[bass.ds(i, 1), :, :].rearrange("o p k -> (o p) k")).then_inc(s_tab[u], 16)
                e.dma_start(oh_rows[0:3, u, :], onehot_tab[:, bass.ds(i * (G * P), G * P)]).then_inc(s_tab[u], 16)
                e.dma_start(row_sb[0:1, u, 0:rw], rt_[bass.ds(i, 1), :]).then_inc(s_tab[u], 16)
                for hd in range(heads):
                    e.dma_start(step_sb[hd * G:(hd + 1) * G, u, :],
                                step_tab[bass.ds(i * G, G), :]).then_inc(s_tab[u], 16)
            tab = L.slot_dma("sp", load_tables, [], s_tab, TB, 16 * ntab)

            def gather(c):
                def fn(e, u, i):
                    for g in range(c * CH, (c + 1) * CH):
                        e.indirect_dma_start(rows[:, u, g, 0:width], None, src_rows,
                                             bass.IndirectOffsetOnAxis(ap=edge_sb[:, u, g:g + 1].bitcast(I32), axis=0)
                                             ).then_inc(s_gat[c][u], 16)
                return L.slot_dma("pool", fn, [(tab, 0)], s_gat[c], GB, 16 * CH)
            gat = [gather(c) for c in range(NCH)]

            _, dst_at = load_offsets(L, "pe", BL0 + G, P, [(tab, 0)], 0)
            _, agg_at = load_offsets(L, "dve", BL0, AW, [(tab, 2)], 2)

            Q, OT, Z, LR, MX, RD = {}, {}, {}, {}, {}, {}

            def a_dist(c):
                def fn(e, u, i):
                    return e.matmul(bank[c % 2][:, :], oh_w[:, :], oh_rows[:, u, c * CH * P:(c + 1) * CH * P],
                                    start=True, stop=True)
                Q[c] = L.op("pe", fn, [(tab, 0), (OT[c - 2], 0) if c >= 2 else None])

            def a_onehot(c):
                def fn(e, u, i):
                    return e.activation(oh_t[:, c % 2, :], bank[c % 2][:, :], ACT.Relu, bias=1.0, scale=-1.0)
                OT[c] = L.op("act", fn, [(Q[c], 0), (Z[c - 2], 0) if c >= 2 else None])

            def a_sum(c):
                def fn(e, u, i):
                    for k in range(CH):
                        g = c * CH + k
                        oh = oh_t[:, c % 2, k * P:(k + 1) * P]
                        if vector:
                            o = bank[2 + c % 2][:, k * P:(k + 1) * P]
                            e.matmul(o, oh, dst_flat[:, bass.ds(dst_at["v"][g], P)], start=True, stop=False)
                            ins = e.matmul(o, ident[:, :], rows[:, u, g, 0:P], start=False, stop=True)
                        else:
                            ins = e.matmul(bank[2][:, g:g + 1], oh, dst_flat[:, bass.ds(dst_at["v"][g], 1)], start=True, stop=True)
                    return ins
                Z[c] = L.op("pe", fn, [(OT[c], 0)] + ([(gat[c], 0)] if vector else [])
                            + ([(MX[c - 2], 0)] if vector and c >= 2 else []), anchored=True)

            def a_lrelu(c):
                LR[c] = L.op("act", lambda e, u, i: e.mul(lrelu[:, c % 2, :], bank[2 + c % 2][:, :], SLOPE),
                             [(Z[c], 0), (RD[c - 2], 0) if c >= 2 else None])

            def a_logit(c):
                x3 = lrelu[:, c % 2, :].rearrange("p (g n) -> p g n", g=CH)
                MX[c] = L.op("dve", lambda e, u, i: e.tensor_tensor(lrelu[:, c % 2, :], lrelu[:, c % 2, :], bank[2 + c % 2][:, :], ALU.max),
                             [(LR[c], 0)])
                o = L.op("dve", lambda e, u, i: e.tensor_tensor(x3, x3, view(att[:, :], [(0, CH), (1, P)]), ALU.mult), [(MX[c], 0)])
                RD[c] = L.op("dve", lambda e, u, i: e.tensor_reduce(
                    view(logit[:, c * CH:], [(1, CH), (G, heads)]), view(lrelu[:, c % 2, :], [(P, CH), (hw, heads), (1, hw)]),
                    AX.X, ALU.add), [(o, 0)])

            hg = lambda x: x.rearrange("p (h g) -> p h g", h=heads)
            cv = lambda t, k: t[:, 0:heads * (G + 1)].rearrange("o (h k) -> o h k", h=heads)[:, :, k]
            LT = bank[6][0:RW, 0:P]
            ST_ = bank[6][:, 0:RW]
            RT = bank[6][:, P:P + RW]
            Y1 = bank[6][0:1, 2 * P:2 * P + RW]
            Y2 = bank[6][0:RW, 3 * P:3 * P + 1]
            B = {}

            def b_logits_to_steps():
                B["tp1"] = L.op("pe", lambda e, u, i: e.transpose(LT, masked[:, (u - 1) % 2, 0:RW], ident[:, :]), [], lag=1, anchored=True)

            def b_segments():
                B["sf"] = L.op("dve", lambda e, u, i: e.tensor_tensor_scan(seg_fwd[0:RW, :], step_sb[0:RW, (u - 1) % U, 0:P], LT,
                                                                          NEG, ALU.add, ALU.max), [(B["tp1"], 0)], lag=1)
                B["sb"] = L.op("dve", lambda e, u, i: e.tensor_tensor_scan(
                    view(seg_max[0:RW, P - 1:], [(-1, P)]), view(step_sb[0:RW, (u - 1) % U, P:], [(-1, P)]),
                    view(seg_fwd[0:RW, P - 1:], [(-1, P)]), NEG, ALU.add, ALU.max), [(B["sf"], 0)], lag=1)

            def b_carry():
                B["k0"] = L.op("dve", lambda e, u, i: e.tensor_copy(cv(carry_in, slice(0, 1)), cv(carry, slice(G, G + 1))), [], lag=1)
                B["k1"] = L.op("dve", lambda e, u, i: e.tensor_copy(cv(carry_in, slice(1, G + 1)), hg(Y1)), [(B["tp2"], 0)], lag=1)
                B["k2"] = L.op("dve", lambda e, u, i: e.tensor_tensor_scan(
                    carry[:, 0:heads * (G + 1)], row_sb[0:1, (u - 1) % U, 0:heads * (G + 1)],
                    carry_in[:, 0:heads * (G + 1)], NEG, ALU.add, ALU.max), [(B["k0"], 0), (B["k1"], 0)], lag=1)
                B["k0"].after.append((B["k2"], 1))
                B["k3"] = L.op("dve", lambda e, u, i: e.tensor_tensor(
                    hg(cin_row[:, 0:RW]), cv(carry, slice(0, G)), hg(row_sb[0:1, (u - 1) % U, FC0:FC0 + RW]), ALU.add),
                    [(B["k2"], 0)], lag=1)

            def b_maxima():
                B["k4"] = L.op("dve", lambda e, u, i: e.tensor_copy(cin[0:RW, 0:1], Y2), [(B["tp3"], 0)], lag=1)
                B["rm"] = L.op("dve", lambda e, u, i: e.scalar_tensor_tensor(
                    run_max[0:RW, :], step_sb[0:RW, (u - 1) % U, P + 1:2 * P + 1], cin[0:RW, 0:1],
                    seg_max[0:RW, :], ALU.add, ALU.max), [(B["k4"], 0)], lag=1)
                B["dd"] = L.op("dve", lambda e, u, i: e.tensor_tensor(cin[0:RW, 1:2], cin[0:RW, 0:1], run_max[0:RW, 0:1], ALU.subtract),
                               [(B["rm"], 0)], lag=1)

            def b_weights():
                B["df"] = L.op("dve", lambda e, u, i: e.tensor_tensor(shifted[:, 0:RW], masked[:, (u - 1) % 2, 0:RW], RT, ALU.subtract),
                               [(B["tp4"], 0)], lag=1)
                B["cm"] = L.op("dve", lambda e, u, i: e.tensor_scalar(cin[0:RW, 3:4], cin[0:RW, 2:3], -1.0, None, ALU.add), [(B["ce"], 0)], lag=1)
                B["dm"] = L.op("dve", lambda e, u, i: e.tensor_scalar(
                    decay_m[0:RW, :], iota[0:RW, :], step_sb[0:RW, (u - 1) % U, 2 * P + 1:2 * P + 2],
                    cin[0:RW, 3:4], ALU.is_equal, ALU.mult), [(B["cm"], 0)], lag=1)

            def b_last_to_row():
                B["tp2"] = L.op("pe", lambda e, u, i: e.transpose(Y1, seg_max[0:RW, P - 1:P], ident[0:RW, 0:RW]), [(B["sb"], 0)],
                                lag=1, anchored=True)

            def b_carry_to_steps():
                B["tp3"] = L.op("pe", lambda e, u, i: e.transpose(Y2, cin_row[:, 0:RW], ident[0:1, 0:1]), [(B["k3"], 0)], lag=1, anchored=True)

            def b_maxima_to_edges():
                B["tp4"] = L.op("pe", lambda e, u, i: e.transpose(RT, run_max[0:RW, :], ident[0:RW, 0:RW]), [(B["rm"], 0)], lag=1, anchored=True)

            def b_factors_to_nodes():
                B["tp5"] = L.op("pe", lambda e, u, i: e.transpose(ST_, decay_m[0:RW, :], ident[0:RW, 0:RW]), [(B["dm"], 0)], lag=1, anchored=True)

            def b_decay():
                B["ce"] = L.op("act", lambda e, u, i: e.activation(cin[0:RW, 2:3], cin[0:RW, 1:2], ACT.Exp), [(B["dd"], 0)], lag=1)

            def b_exp():
                B["wt"] = L.op("act", lambda e, u, i: e.activation(weight[:, (u - 1) % 2, 0:RW], shifted[:, 0:RW], ACT.Exp),
                               [(B["df"], 0)], lag=1)
                B["nw"] = L.op("act", lambda e, u, i: e.mul(minus_w[:, (u - 1) % 2, :], weight[:, (u - 1) % 2, 0:G], -1.0),
                               [(B["wt"], 0)], lag=1)
                B["df"].after.append((B["wt"], 1))

            def b_factors():
                B["sl"] = L.op("dve", lambda e, u, i: e.tensor_scalar(rescale[:, (u - 1) % 2, 0:RW], ST_, 1.0, None, ALU.add),
                               [(B["tp5"], 0)], lag=1)

            WD, W, XS, AG, AC = {}, {}, {}, {}, {}

            def c_dist(c):
                lag = 1 if c == 0 else 2

                def fn(e, u, i):
                    for k in range(CH):
                        g = c * CH + k
                        ins = e.matmul(bank[7][:, k * P:(k + 1) * P], oh_rows[:, (u - lag) % U, g * P:(g + 1) * P], oh_w[:, :],
                                       start=True, stop=True)
                    return ins
                WD[c] = L.op("pe", fn, [(W[(c * CH - 1) % G], 0)], lag=lag, anchored=True)

            def c_weight(c):
                for g in range(c * CH, (c + 1) * CH):
                    ready_q = [(WD[c], 0)] if c else []
                    aft = ready_q + ([(AG[g - 8], 0)] if g >= 8 else [])
                    q = bank[7][:, (g % CH) * P:(g % CH + 1) * P]
                    if heads > 1:
                        if g % CH == 0:
                            o = L.op("act", lambda e, u, i, g=g: e.activation(
                                oh_e[:, g % 8:g % 8 + CH, :].rearrange("p s n -> p (s n)"), bank[7][:, :], ACT.Relu, bias=1.0, scale=-1.0),
                                ready_q + ([(AG[g - 8 + CH - 1], 0)] if g >= 8 else []), lag=2)
                    else:
                        o = L.op("act", lambda e, u, i, g=g, q=q: e.activation(
                            oh_e[:, g % 8, :], q, ACT.Relu, bias=weight[:, (u - 2) % 2, g:g + 1], scale=minus_w[:, (u - 2) % 2, g:g + 1]),
                            aft, lag=2)
                    W[g] = o

            def c_scaled_rows(c):
                def fn(e, u, i):
                    v = (u - 2) % U
                    o = view(xw[:, c % 2, :], [(AW, CH), (hw + 1, heads), (1, hw)])
                    x = view(rows[:, v, c * CH:(c + 1) * CH, :], [(XW, CH), (hw, heads), (1, hw)])
                    w = view(weight[:, v % 2, c * CH:(c + 1) * CH], [(1, CH), (G, heads), (0, hw)])
                    return e.tensor_tensor(o, x, w, ALU.mult)

                def fn2(e, u, i):
                    o = view(xw[:, c % 2, hw:], [(AW, CH), (hw + 1, heads)])
                    return e.copy(o, view(weight[:, (u - 2) % 2, c * CH:(c + 1) * CH], [(1, CH), (G, heads)]))
                aft = [(AG[(c - 2) * CH + CH - 1], 0)] if c >= 2 else []
                XS[c] = [L.op("dve", fn, aft, lag=2), L.op("act", fn2, aft, lag=2)]

            def c_agg(g):
                def fn(e, u, i):
                    o = bank[4 + g // 2 % 2][:, (g % 2) * AW:(g % 2) * AW + aw]
                    r = xw[:, (g // CH) % 2, (g % CH) * AW:(g % CH) * AW + AW] if heads > 1 else rows[:, (u - 2) % U, g, 0:XW]
                    return e.matmul(o, oh_e[:, g % 8, :], r, start=True, stop=True)
                aft = [(W[g], 0)] + ([(o, 0) for o in XS[g // CH]] if heads > 1 else [])
                AG[g] = L.op("pe", fn, aft + ([(AC[g - g % 2 - 3], 0)] if g >= 4 else []), lag=2)

            def c_acc(g):
                s = bank[4 + g // 2 % 2][:, (g % 2) * AW:(g % 2) * AW + aw]

                def fn(e, u, i):
                    at = agg_flat[:, bass.ds(agg_at["v"][g], aw)]
                    return e.scalar_tensor_tensor(at, at, rescale[:, (u - 2) % 2, g:g + 1], s, ALU.mult, ALU.add)

                def fn_a(e, u, i):
                    at = agg_flat[:, bass.ds(agg_at["v"][g], aw)].rearrange("p (h d) -> p h d", h=heads)
                    f = view(rescale[:, (u - 2) % 2, g:], [(G, heads), (0, hw + 1)])
                    return e.tensor_tensor(acc_tmp[:, g % 2, :].rearrange("p (h d) -> p h d", h=heads), at, f, ALU.mult)

                def fn_b(e, u, i):
                    return e.tensor_tensor(agg_flat[:, bass.ds(agg_at["v"][g], aw)], acc_tmp[:, g % 2, :], s, ALU.add)
                before = [(AC[g - 1], 0)] if g else []
                both = [(AG[g - g % 2 + 1], 0)]
                if heads > 1:
                    first = L.op("dve", fn_a, before, lag=2)
                    AC[g] = L.op("dve", fn_b, [(first, 0)] + both, lag=2)
                else:
                    first = AC[g] = L.op("dve", fn, before + both, lag=2)
                return first

            def aggregate(c):
                for g in range(c * CH, (c + 1) * CH):
                    c_agg(g)

            def accumulate(c):
                return [c_acc(g) for g in range(c * CH, (c + 1) * CH)]

            c_weight(0)
            a_dist(0)
            a_onehot(0)
            for c in range(NCH):
                if heads > 1:
                    c_scaled_rows(c)
                if c == 2:
                    b_carry()
                if c == 3:
                    b_decay()
                if c:
                    c_weight(c)
                    acc = accumulate(c - 1)
                    if c == 1:
                        first0 = acc[0]
                if c + 1 < NCH:
                    a_dist(c + 1)
                    a_onehot(c + 1)
                if c == 0:
                    aggregate(0)
                a_sum(c)
                if vector:
                    a_lrelu(c)
                if c == 1:
                    b_segments()
                if c == 2:
                    b_carry_to_steps()
                    b_maxima()
                if c == 3:
                    b_weights()
                    b_exp()
                if c and vector:
                    a_logit(c - 1)
                if c:
                    aggregate(c)
                (b_logits_to_steps, b_last_to_row, b_maxima_to_edges, b_factors_to_nodes)[c]()
                c_dist((c + 1) % NCH)
            b_factors()
            accumulate(NCH - 1)
            if vector:
                a_logit(NCH - 1)
            if not vector:
                sc = L.op("dve", lambda e, u, i: e.tensor_tensor(logit[:, 0:G], bank[2][:, 0:G],
                                                                rows[:, u, :, P:P + 1].rearrange("p g o -> p (g o)"), ALU.add),
                          [(Z[NCH - 1], 0)] + [(x, 0) for x in gat])
                Z[0].after.append((sc, 1))
                lg = L.op("dve", lambda e, u, i: e.scalar_tensor_tensor(logit[:, 0:G], logit[:, 0:G], SLOPE, logit[:, 0:G],
                                                                       ALU.mult, ALU.max), [(sc, 0)])
            else:
                lg = RD[NCH - 1]
            mk = L.op("dve", lambda e, u, i: e.tensor_tensor(
                hg(masked[:, u % 2, 0:RW]), hg(logit[:, 0:RW]), view(edge_sb[:, u, 2 * G:], [(0, heads), (1, G)]), ALU.add), [(lg, 0)])

            B["tp1"].after += [(mk, 1), (B["sl"], 1)]
            for o in ([W[g] for g in range(CH)] if heads == 1 else XS[0]):
                o.after.append((B["nw"] if heads == 1 else B["wt"], 1))
            for g in range(CH):
                W[g].after.append((WD[0], 1))
            first0.after += [(B["sl"], 1), (AC[G - 1], 1)]
            for c in (0, 1):
                Q[c].after.append((OT[c + 2], 1))
                OT[c].after.append((Z[c + 2], 1))
                if vector:
                    Z[c].after.append((MX[c + 2], 1))
                    LR[c].after.append((RD[c + 2], 1))
            B["wt"].after.append((W[G - 1], 1))
            for g in range(8):
                if heads == 1 or g % CH == 0:
                    W[g].after.append((AG[g + 8 if heads == 1 else g + 8 + CH - 1], 1))
            for g in range(4):
                AG[g].after.append((AC[G - 3 + g - g % 2], 1))
            if heads > 1:
                for c in (0, 1):
                    for o in XS[c]:
                        o.after.append((AG[(c + 2) * CH + CH - 1], 1))
                B["wt"].after += [(o, 1) for o in XS[NCH - 1]]
            for c in range(NCH):
                gat[c].after.append((AG[(c + 1) * CH - 1], U - 2))
            tab.after += [(AC[G - 1], U - 2), (tab, U)]
            L.close()
            return [L.last(AC[G - 1])]

        s_sc = [prog.sem(f"scatter_into_sum{k}") for k in range(NSUM)]

        def source_pass(name, ready):
            prog.stage(name)
            big = dst_side[:, :, :].rearrange("p a b -> p (a b)")
            at = 0

            def part(n, dt=F32):
                nonlocal at
                at += n
                v = big[:, at - n:at]
                return v if dt == F32 else v.bitcast(dt)
            src_rows = part(U * G * P // 2, BF16).rearrange("p (u n) -> p u n", u=U)
            summed = part(8 * XW).rearrange("p (s n) -> p s n", s=8)
            oh_s = part(CH * P)
            same = part(8 * P).rearrange("p (s n) -> p s n", s=8)
            scratch = part(2 * CH * P).rearrange("p (s n) -> p s n", s=2 * CH)
            look = part(G)
            dup = part(G)
            target_f = part(G)
            target = part(U * G, I32).rearrange("p (u n) -> p u n", u=U)
            z = add("dve", lambda e: e.memset(src_rows[0:6, :, :], 1.0), [ready])
            for e_ in prog.ENGINES:
                prog.queue[e_].append(lambda eng, last, w=list(flat([ready, z])): [eng.wait_ge(x.sem, x.value) for x in w
                                                                                 if last.get(id(x.sem), 0) < x.value])
            prog.stage(name + "_loop")
            L = Loop(prog, NG)
            agg_flat = agg[:, :, :].rearrange("p a b -> p (a b)")
            BL0 = 2 * G + 1
            ntab = 4
            TB = tab_base[0]
            tab_base[0] += 16 * ntab * (NG // U)

            def load_tables(e, u, i):
                e.dma_start(edge_sb[:, u, :], edge_tab[bass.ds(i, 1), :, :].rearrange("o p k -> (o p) k")).then_inc(s_tab[u], 16)
                e.dma_start(oh_rows[0:3, u, :], onehot_tab[:, bass.ds(i * (G * P), G * P)]).then_inc(s_tab[u], 16)
                e.dma_start(src_rows[0:4, u, :], source_tab[:, bass.ds(i * (G * P), G * P)]).then_inc(s_tab[u], 16)
                e.dma_start(row_sb[0:1, u, 0:R1], row_tab1[bass.ds(i, 1), :]).then_inc(s_tab[u], 16)
            tab = L.slot_dma("sp", load_tables, [], s_tab, TB, 16 * ntab)

            ld, offs = load_offsets(L, "pe", BL0, AW, [(tab, 0)], 0)

            def scatters_before(g, i, lag):
                return (i - lag) * (16 * G // NSUM) + 16 * (g // NSUM)

            D, OT, XD, EV, DS, OS, LK, SEL, BA, DU = {}, {}, {}, {}, {}, {}, {}, {}, {}, {}
            BC, SM, AG, RV = {}, {}, {}, {}
            for c in range(NCH):
                BC[c] = L.op("pe", lambda e, u, i, c=c: e.matmul(bank[2][:, :], oh_ws[:, P:2 * P],
                                                                 src_rows[0:6, (u - 1) % U, c * CH * P:(c + 1) * CH * P],
                                                                 start=True, stop=True),
                             [(SM[c * CH - 1], 0)] if c else [], lag=1)
                for g in range(c * CH, (c + 1) * CH):
                    SM[g] = L.op("dve", lambda e, u, i, g=g: e.tensor_scalar(
                        same[:, g % 8, :], bank[2][:, (g % CH) * P:(g % CH + 1) * P],
                        edge_sb[:, (u - 1) % U, 3 * G + g:3 * G + g + 1], weight[:, (u - 1) % 2, g:g + 1],
                        ALU.is_equal, ALU.mult), [(BC[c], 0)] + ([(AG[g - 8], 0)] if g >= 8 else []), lag=1)
                D[c] = L.op("pe", lambda e, u, i, c=c: e.matmul(bank[0][:, :], oh_w[:, :], oh_rows[:, u, c * CH * P:(c + 1) * CH * P],
                                                                start=True, stop=True), [(tab, 0)] + ([(OT[c - 1], 0)] if c else []))
                OT[c] = L.op("act", lambda e, u, i, c=c: e.activation(oh_t[:, c % 2, :], bank[0][:, :], ACT.Relu, bias=1.0, scale=-1.0),
                             [(D[c], 0)] + ([(XD[(c - 2) * 2 + 1], 0)] if c >= 2 else []))
                DS[c] = L.op("pe", lambda e, u, i, c=c: e.matmul(bank[1][:, :], oh_ws[:, 0:P], src_rows[0:6, u, c * CH * P:(c + 1) * CH * P],
                                                                 start=True, stop=True), [(tab, 0)] + ([(DU[c * CH - 1], 0)] if c else []))
                OS[c] = L.op("act", lambda e, u, i, c=c: e.activation(oh_s, bank[1][:, :], ACT.Relu, bias=1.0, scale=-1.0),
                             [(DS[c], 0)] + ([(LK[c - 1], 0)] if c else []))
                for g in range(c * CH, (c + 1) * CH):
                    if g % 2 == 0:
                        continue
                    h = g // 2
                    for gg in (g - 1, g):
                        AG[gg] = L.op("pe", lambda e, u, i, g=gg: e.matmul(
                            bank[6 + g // 2 % 2][:, (g % 2) * XW:(g % 2 + 1) * XW], same[:, g % 8, :], rows[:, (u - 1) % U, g, :],
                            start=True, stop=True), [(SM[gg], 0)] + ([(RV[h - 2], 0)] if h >= 2 else []), lag=1)

                    def evac(e, u, i, g=g - 1):
                        for gg in (g, g + 1):
                            if isinstance(i, int):
                                n = scatters_before(gg, i, 1) - 16
                                if n > 0:
                                    e.wait_ge(s_sc[gg % NSUM], n)
                            else:
                                e.wait_ge(s_sc[gg % NSUM], i * (16 * G // NSUM) + (16 * (gg // NSUM) - 16 * G // NSUM - 16))
                        return e.copy(summed[:, g % 8:g % 8 + 2, :].rearrange("p s n -> p (s n)"), bank[6 + g // 2 % 2][:, 0:2 * XW])
                    RV[h] = L.op("act", evac, [(AG[g], 0)], lag=1)

                    def scatter(e, u, i, g=g - 1):
                        for gg in (g, g + 1):
                            k = gg % NSUM
                            if isinstance(i, int):
                                n = scatters_before(gg, i, 1)
                                if n > 0:
                                    e.wait_ge(s_sc[k], n)
                            else:
                                e.wait_ge(s_sc[k], i * (16 * G // NSUM) + (16 * (gg // NSUM) - 16 * G // NSUM))
                                e.sem_inc(prog.anchor, 1)
                            e.indirect_dma_start(scatter_s[k], bass.IndirectOffsetOnAxis(ap=target[:, (u - 1) % U, gg:gg + 1], axis=0),
                                                 summed[:, gg % 8, :], None, compute_op=ALU.add).then_inc(s_sc[k], 16)
                    L.op("pool", scatter, [(RV[h], 0)], lag=1, anchored=True)

                def lookup(e, u, i, c=c):
                    for k in range(CH):
                        ins = e.matmul(bank[5][:, k * P:k * P + NB], oh_s[:, k * P:(k + 1) * P], dst_score[:, :], start=True, stop=True)
                    return ins
                LK[c] = L.op("pe", lookup, [(OS[c], 0)] + ([(SEL[c * CH - 1], 0)] if c else []))
                BA[c] = L.op("pe", lambda e, u, i, c=c: e.matmul(bank[1][:, :], oh_ws[:, P:2 * P], src_rows[0:6, u, c * CH * P:(c + 1) * CH * P],
                                                                 start=True, stop=True), [(OS[c], 0)])
                for h in (2 * c, 2 * c + 1):
                    def expand(e, u, i, h=h):
                        for k in (0, 1):
                            g = 2 * h + k
                            ins = e.matmul(bank[3 + h % 2][:, k * XW:(k + 1) * XW], oh_t[:, (g // CH) % 2, (g % CH) * P:(g % CH + 1) * P],
                                           agg_flat[:, bass.ds(offs["v"][g], XW)], start=True, stop=True)
                        return ins
                    XD[h] = L.op("pe", expand, [(OT[c], 0)] + ([(EV[h - 2], 0)] if h >= 2 else []), anchored=True)
                    EV[h] = L.op("act", lambda e, u, i, h=h: e.copy(rows[:, u, 2 * h:2 * h + 2, :].rearrange("p s n -> p (s n)"),
                                                                    bank[3 + h % 2][:, 0:2 * XW]), [(XD[h], 0)])
                for g in range(c * CH, (c + 1) * CH):
                    SEL[g] = L.op("dve", lambda e, u, i, g=g: e.scalar_tensor_tensor(
                        scratch[:, g % CH, 0:NB], iota[:, 0:NB], edge_sb[:, u, 4 * G + g:4 * G + g + 1], bank[5][:, (g % CH) * P:(g % CH) * P + NB],
                        ALU.is_equal, ALU.mult, accum_out=look[:, g:g + 1]), [(LK[c], 0)] + ([(SEL[g - CH], 0)] if g >= CH else []))
                for g in range(c * CH, (c + 1) * CH):
                    DU[g] = L.op("dve", lambda e, u, i, g=g: e.scalar_tensor_tensor(
                        scratch[:, CH + g % CH, :], bank[1][:, (g % CH) * P:(g % CH + 1) * P], edge_sb[:, u, 3 * G + g:3 * G + g + 1], att[:, :],
                        ALU.is_equal, ALU.mult, accum_out=dup[:, g:g + 1]), [(BA[c], 0)] + ([(DU[g - CH], 0)] if g >= CH else []))
            a1 = L.op("dve", lambda e, u, i: e.tensor_tensor(logit[:, 0:G], look[:, :], rows[:, u, :, P:P + 1].rearrange("p g o -> p (g o)"),
                                                             ALU.add), [(SEL[G - 1], 0), (EV[G // 2 - 1], 0)])
            a2 = L.op("dve", lambda e, u, i: e.scalar_tensor_tensor(logit[:, 0:G], logit[:, 0:G], SLOPE, logit[:, 0:G], ALU.mult, ALU.max), [(a1, 0)])
            a3_ = L.op("dve", lambda e, u, i: e.tensor_tensor(logit[:, 0:G], logit[:, 0:G], edge_sb[:, u, 2 * G:3 * G], ALU.add), [(a2, 0)])
            wt = L.op("act", lambda e, u, i: e.activation(weight[:, u % 2, 0:G], logit[:, 0:G], ACT.Exp), [(a3_, 0), (SM[G - 1], 1)])
            t1 = L.op("dve", lambda e, u, i: e.tensor_scalar(dup[:, :], dup[:, :], 0.0, None, ALU.is_gt), [(DU[G - 1], 0)])
            t2 = L.op("dve", lambda e, u, i: e.tensor_scalar(target_f[:, :], edge_sb[:, u, 3 * G:4 * G], dump_row[:, 0:1], -1.0,
                                                             ALU.subtract, ALU.mult), [(t1, 0)])
            t3 = L.op("dve", lambda e, u, i: e.tensor_tensor(target_f[:, :], target_f[:, :], dup[:, :], ALU.mult), [(t2, 0)])
            t4 = L.op("dve", lambda e, u, i: e.tensor_tensor(target_f[:, :], target_f[:, :], edge_sb[:, u, 3 * G:4 * G], ALU.add), [(t3, 0)])

            def store_target(e, u, i):
                for k in range(NSUM):
                    if isinstance(i, int):
                        if i >= U:
                            e.wait_ge(s_sc[k], (16 * G // NSUM) * (i - U + 1))
                    else:
                        e.wait_ge(s_sc[k], i * (16 * G // NSUM) - (16 * G // NSUM) * (U - 1))
                return e.tensor_copy(target[:, u, :], target_f[:, :])
            t5 = L.op("dve", store_target, [(t4, 0)])
            BC[0].after.append((SM[G - 1], 1))
            SM[0].after += [(wt, 1), (AG[8], 1)]
            for g in range(1, 8):
                SM[g].after.append((AG[g + 8], 1))
            D[0].after.append((OT[NCH - 1], 1))
            OT[0].after.append((XD[5], 1))
            OT[1].after.append((XD[7], 1))
            DS[0].after.append((DU[G - 1], 1))
            OS[0].after.append((LK[NCH - 1], 1))
            LK[0].after.append((SEL[G - 1], 1))
            for g in (0, 1):
                AG[g].after.append((RV[6], 1))
            for g in (2, 3):
                AG[g].after.append((RV[7], 1))
            XD[0].after.append((EV[6], 1))
            XD[1].after.append((EV[7], 1))
            EV[0].after.append((AG[G - 1], 3))
            RV[0].after.append((t5, 1))
            SEL[0].after += [(a1, 1), (SEL[G - 1], 1)]
            DU[0].after += [(DU[G - 1], 1), (t3, 1)]
            a1.after.append((wt, 1))
            L.ops[[o is AG[G - 1] for o in L.ops].index(True)].counted = True
            tab.after += [(AG[G - 1], 3), (SM[G - 1], 3), (t4, 4), (tab, 4)]
            scat_after = None
            L.close()
            return [L.last(AG[G - 1]), L.last(SM[G - 1])] + [Done(s_sc[k], 16 * (G // NSUM) * NG) for k in range(NSUM)]

        node_tile = lambda n: pool_rows[:, n * NBB * P:(n + 1) * NBB * P]
        tile3 = lambda n: node_tile(n).rearrange("p (b f) -> p b f", b=NBB)
        hT = [sb(f"hT{k}", [P, NBB * P]) for k in range(1)]
        NBT = NB // NBB
        wcol = lambda n, k=1: param[:, n * P:(n + k) * P]

        def row_bcast(x, off=0, n=P):
            return bass.AP(x.tensor, x.offset + off, [(0, P), (1, n)])

        def load_rows(pairs, after):
            return [dma("sp", lambda e, s=s, src=src: e.dma_start(s, src), after) for s, src in pairs]

        def blocks(ap2d, t):
            return ap2d[t * NBB * P:(t + 1) * NBB * P, :].rearrange("(b p) f -> p b f", p=P)

        def transposed(src3, bank0, ready, free):
            outs = []
            dst = hT[0]
            for q, (lo, hi) in enumerate(((0, 4), (4, NBB))):
                for k in range(lo, hi):
                    tp = add("pe", lambda e, k=k, q=q, lo=lo: e.transpose(bank[bank0 + q][:, (k - lo) * P:(k - lo + 1) * P],
                                                                          src3[:, k, :], ident[:, :]), [ready, free])
                outs.append(add("act", lambda e, q=q, lo=lo, hi=hi: e.copy(dst[:, lo * P:hi * P], bank[bank0 + q][:, 0:(hi - lo) * P]),
                                [tp, free]))
            return outs

        def layer_norm(x3, ready, slot):
            hs = [add("dve", lambda e, k=k: e.bn_stats(stats[:, k, :], x3[:, k, :]), [ready]) for k in range(NBB)]
            hs = [add("dve", lambda e, k=k: e.bn_aggr(moments[:, k, :], stats[:, k, :]), [hs[k]]) for k in range(NBB)]
            h = add("dve", lambda e: e.tensor_scalar(rstd[:, 0, :], moments[:, :, 1], LN_EPS, None, ALU.add), [hs])
            h = add("pool", lambda e: e.tensor_tensor(rstd[:, 1, :], rstd[:, 0, :], minus_half[:, :], ALU.pow), [h, m_half])
            return [add("dve", lambda e, k=k: e.tensor_scalar(x3[:, k, :], x3[:, k, :], moments[:, k, 0:1], rstd[:, 1, k:k + 1],
                                                            ALU.subtract, ALU.mult), [h]) for k in range(NBB)]

        def bias3(n):
            return view(wcol(n), [(0, NBB), (1, P)])

        def project(t, w2, evac, ready, free_ps):
            outs = []
            for q in range((NBB + 1) // 2):
                ks = [k for k in (2 * q, 2 * q + 1) if k < NBB]
                for k in ks:
                    mm = add("pe", lambda e, k=k, q=q: e.matmul(bank[4 + q][:, (k % 2) * 2 * P:(k % 2 + 1) * 2 * P],
                                                                hT[0][:, k * P:(k + 1) * P], wcol(w2, 2), start=True, stop=True),
                             [ready, free_ps[q] if free_ps else []])
                outs.append(evac(q, ks, mm))
            return outs

        def two_sided(t, w2, b_src, b_dst, ready, free_ps, stage3, stage_free, table):
            def evac(q, ks, mm):
                n = len(ks)
                src = bank[4 + q][:, 0:n * 2 * P].rearrange("p (k s f) -> p k s f", k=n, s=2)
                def fn(e):
                    o = stage3[:, ks[0]:ks[0] + n, :]
                    if b_src is None:
                        return e.tensor_copy(o, src[:, :, 0, :])
                    return e.tensor_tensor(o, src[:, :, 0, :], view(wcol(b_src), [(0, n), (1, P)]), ALU.add)
                def fn2(e):
                    o = dst_side[:, t * NBB + ks[0]:t * NBB + ks[0] + n, :]
                    if b_dst is None:
                        return e.tensor_copy(o, src[:, :, 1, :])
                    return e.tensor_tensor(o, src[:, :, 1, :], view(wcol(b_dst), [(0, n), (1, P)]), ALU.add)
                return [add("dve", fn, [mm, stage_free]), add("dve", fn2, [mm])]
            outs = project(t, w2, evac, ready, free_ps)
            st = dma("sp", lambda e: e.dma_start(blocks(table, t), stage3), [outs])
            return outs, st

        def load_x(t, dst3, src, after):
            lo, hi = t * NBB * P, (t + 1) * NBB * P
            if src.shape[0] == NB * P or hi <= N:
                return [dma("sp", lambda e: e.dma_start(dst3, src[lo:hi, :].rearrange("(b p) f -> p b f", p=P)), after)]
            zero = add("dve", lambda e: e.memset(dst3, 0.0), after)
            full = (N - lo) // P
            rem = N - lo - full * P
            hs = []
            if full:
                hs.append(dma("sp", lambda e: e.dma_start(dst3[:, 0:full, :], src[lo:lo + full * P, :].rearrange("(b p) f -> p b f", p=P)), [zero]))
            if rem:
                hs.append(dma("sp", lambda e: e.dma_start(dst3[0:rem, full, :], src[lo + full * P:N, :]), [zero]))
            return hs

        prog.stage("dense0")
        prm = load_rows([(wcol(0), a["L0_gnn_Wl1"]), (wcol(1), a["L0_gnn_Wr1"]), (wcol(2), row_bcast(a["L0_gnn_bl1"])),
                         (wcol(3), row_bcast(a["L0_gnn_br1"])), (att[:, :], row_bcast(a["L0_gnn_att1"]))], [idle])
        x_free, ht_free, ps_free, st_free = [[], []], [], None, [[], []]
        tail = []
        for t in range(NBT):
            x3 = tile3(t % 2)
            ld = load_x(t, x3, a["x"], [idle, x_free[t % 2]])
            tt = transposed(x3, 0, [ld, prm], ht_free)
            ev, st = two_sided(t, 0, 2, 3, [tt, prm], ps_free, tile3(2 + t % 2), [st_free[t % 2], idle], gather_a)
            x_free[t % 2], ht_free, ps_free, st_free[t % 2] = tt, ev, ev, [st]
            tail += [st, ev]
        p0 = edge_pass("L0a", gather_a, 1, True, [tail, tables])

        def normalise(t, heads, eps, ready, guard=None):
            a3 = agg[:, t * NBB:(t + 1) * NBB, :]
            hw = P // heads
            if heads == 1:
                den = a3[:, :, P + 1]
                r = recip[:, 0:NBB]
                rb = view(recip[:, :], [(1, NBB), (0, P)])
                h = add("dve", lambda e: (e.tensor_scalar(r, den, eps, None, ALU.add) if guard is None else
                                          e.tensor_scalar(r, den, guard, None, ALU.max)), [ready])
                h = add("dve", lambda e: e.reciprocal(r, r), [h])
                return add("dve", lambda e: e.tensor_tensor(a3[:, :, 0:P], a3[:, :, 0:P], rb, ALU.mult), [h])
            den = view(agg[:, t * NBB, hw:], [(AW, NBB), (hw + 1, heads)])
            r = recip[:, :].rearrange("p (b h) -> p b h", b=NBB)
            h = add("dve", lambda e: e.tensor_scalar(r, den, eps, None, ALU.add), [ready])
            h = add("dve", lambda e: e.reciprocal(recip[:, :], recip[:, :]), [h])
            return h

        def bias_add(o3, i3, n, after):
            return add("dve", lambda e: e.tensor_tensor(o3, i3, bias3(n), ALU.add), after)

        prog.stage("dense1")
        prm = load_rows([(wcol(0), a["L0_gnn_Wl2"]), (wcol(1), a["L0_gnn_Wr2"]), (wcol(2), row_bcast(a["L0_gnn_bl2"])),
                         (wcol(3), row_bcast(a["L0_gnn_br2"])), (wcol(4), row_bcast(a["L0_gnn_bias1"])),
                         (att[:, :], row_bcast(a["L0_gnn_att2"]))], [p0])
        ht_free, ps_free, st_free = [], None, [[], []]
        tail = []
        prev_n = None
        for t in range(NBT):
            a3 = agg[:, t * NBB:(t + 1) * NBB, 0:P]
            h = normalise(t, 1, 1e-16, [p0, prev_n])
            prev_n = h
            h = bias_add(a3, a3, 4, [h, prm])
            h = add("act", lambda e, a3=a3: e.activation(a3, a3, ACT.Relu), [h])
            tt = transposed(a3, 0, [h, prm], ht_free)
            ev, st = two_sided(t, 0, 2, 3, [tt, prm], ps_free, tile3(2 + t % 2), [st_free[t % 2], p0], gather_b)
            ht_free, ps_free, st_free[t % 2] = ev, ev, [st]
            tail += [st, ev]
        p1 = edge_pass("L0b", gather_b, 1, True, [tail])

        prog.stage("dense2")
        NP_ = 0
        wsb, a12, vsb, wb = wcol(0), wcol(1)[:, 0:2], wcol(1)[:, 4:6], wcol(1)[:, 8:9]
        s12, cvec, abias = wcol(1)[:, 9:10], wcol(1)[:, 10:11], wcol(1)[:, 11:12]
        one_col = lambda x, off=0: bass.AP(x.tensor, x.offset + off, [(1, P), (1, 1)])
        prm = load_rows([(wsb, a["L1_gnn_w_weight"]), (a12[:, 0:1], one_col(a["L1_gnn_a_weight"])),
                         (a12[:, 1:2], one_col(a["L1_gnn_a_weight"], P)), (wb, one_col(a["L1_gnn_w_bias"])),
                         (abias, bass.AP(a["L1_gnn_a_bias"].tensor, 0, [(0, P), (1, 1)])),
                         (wcol(2), row_bcast(a["L0_gnn_bias2"]))], [p1])
        mm = add("pe", lambda e: e.matmul(bank[0][:, 0:2], wsb, a12, start=True, stop=True), [prm])
        v12 = add("dve", lambda e: e.tensor_copy(vsb, bank[0][:, 0:2]), [mm])
        h = add("dve", lambda e: e.tensor_tensor(s12, a12[:, 0:1], a12[:, 1:2], ALU.add), [prm])
        h = add("dve", lambda e: e.tensor_tensor(s12, s12, wb, ALU.mult), [h])
        mm = add("pe", lambda e: e.matmul(bank[1][:, 0:1], ones[:, :], s12, start=True, stop=True), [h])
        v12 = [v12, add("dve", lambda e: e.tensor_tensor(cvec, bank[1][:, 0:1], abias, ALU.add), [mm, prm])]
        x_free, ht_free, sc_free, st_free = [[], []], [], [], [[], []]
        tail, prev_n, rows_ln = [], None, []
        for t in range(NBT):
            a3 = agg[:, t * NBB:(t + 1) * NBB, 0:P]
            x3 = tile3(t % 2)
            ld = load_x(t, x3, a["x"], [p1, x_free[t % 2]])
            h = normalise(t, 1, 1e-16, [p1, prev_n])
            prev_n = h
            h = bias_add(a3, a3, 2, [h, prm])
            h = add("dve", lambda e, a3=a3, x3=x3: e.tensor_tensor(a3, a3, x3, ALU.add), [h, ld])
            x_free[t % 2] = h
            ln = layer_norm(a3, [h, rows_ln], 0)
            rows_ln = ln
            tt = transposed(a3, 2, [ln, v12], ht_free)
            for k in range(NBB):
                mm = add("pe", lambda e, k=k: e.matmul(bank[4][:, 2 * k:2 * k + 2], hT[0][:, k * P:(k + 1) * P], vsb,
                                                       start=True, stop=True), [tt, sc_free])
            ht_free = mm
            ps = bank[4][:, 0:2 * NBB].rearrange("p (k s) -> p k s", s=2)
            s1 = add("dve", lambda e, t=t, ps=ps: e.tensor_scalar(dst_score[:, t * NBB:(t + 1) * NBB], ps[:, :, 0], cvec, None, ALU.add), [mm])
            s2 = add("dve", lambda e, t=t, ps=ps: e.tensor_copy(agg[:, t * NBB:(t + 1) * NBB, P], ps[:, :, 1]), [mm])
            sc_free = [s1, s2]
            s3 = add("dve", lambda e, t=t: e.memset(agg[:, t * NBB:(t + 1) * NBB, P + 1:P + 2], 1.0), [h])
            tail += [ln, s1, s2, s3]
        zt = tile3(4)[:, 0:4, :].rearrange("p b f -> p (b f)")
        zz = add("dve", lambda e: e.memset(node_tile(4), 0.0), [p1])
        NBZ = NB + 1
        zw = 6 * XW
        for k in range(NSUM):
            for z0 in range(0, NBZ, 6):
                z1 = min(z0 + 6, NBZ)
                tail.append(dma("sp", lambda e, k=k, z0=z0, z1=z1: e.dma_start(
                    scatter_s[k][z0 * P:z1 * P, :].rearrange("(p b) f -> p (b f)", p=P), node_tile(4)[:, 0:(z1 - z0) * XW]), [zz]))
        tail.append(dma("sp", lambda e: e.dma_start(att[:, :], a["c_tril"]), [p1]))
        p2 = source_pass("L1", [tail])

        def transpose_weight(n, src, stage_n, after, pb):
            ld = dma("sp", lambda e: e.dma_start(node_tile(stage_n)[:, 0:P], src), after)
            tp = add("pe", lambda e: e.transpose(bank[pb][:, 0:P], node_tile(stage_n)[:, 0:P], ident[:, :]), [ld])
            return add("act", lambda e: e.copy(wcol(n), bank[pb][:, 0:P]), [tp])

        prog.stage("dense3")
        tw = a["L1_gnn_trans_weight"]
        prm = load_rows([(wcol(2), row_bcast(a["L1_gnn_trans_bias"])), (wcol(3), row_bcast(a["L1_gnn_ln_gamma"])),
                         (wcol(4), row_bcast(a["L1_gnn_ln_beta"])), (wcol(6), row_bcast(a["L2_gnn_b2"])),
                         (wcol(7)[:, 0:1], bass.AP(a["L2_gnn_W1"].tensor, 0, [(1, P), (1, 1)])),
                         (wcol(7)[:, 1:2], bass.AP(a["L2_gnn_W1"].tensor, P, [(1, P), (1, 1)])),
                         (wcol(8)[:, 0:1], bass.AP(a["L2_gnn_b1"].tensor, 0, [(0, P), (1, 1)]))], [p2])
        prm.append(transpose_weight(0, tw[:, 0:P], 4, [p2], 0))
        prm.append(transpose_weight(1, tw[:, P:2 * P], 5, [p2], 1))
        prm.append(transpose_weight(5, a["L2_gnn_W2"], 6, [p2], 2))
        aggT = oh_e[:, :, :].rearrange("p a b -> p (a b)")[:, 0:NBB * P]
        x_free, st_free = [[], []], [[], []]
        hT_read, aggT_read, ps_read, prev_n, ln_prev, sc_read = [], [], [[], []], None, [], []
        tail = []
        xT_done = []
        for t in range(NBT):
            x3 = agg[:, t * NBB:(t + 1) * NBB, 0:P]
            sums = [pool_rows[:, (t % 2 * NSUM + k) * NBB * XW:(t % 2 * NSUM + k + 1) * NBB * XW] for k in range(NSUM)]
            lds = [dma("sp", lambda e, t=t, k=k, sums=sums: e.dma_start(sums[k].rearrange("p (b f) -> p b f", b=NBB),
                                                                      blocks(scatter_s[k], t)), [p2, prm, x_free[t % 2]])
                   for k in range(NSUM)]
            h = add("dve", lambda e, sums=sums: e.tensor_tensor(sums[0], sums[0], sums[1], ALU.add), [lds[0], lds[1]])
            h2 = add("dve", lambda e, sums=sums: e.tensor_tensor(sums[2], sums[2], sums[3], ALU.add), [lds[2], lds[3]])
            h = add("dve", lambda e, sums=sums: e.tensor_tensor(sums[0], sums[0], sums[2], ALU.add), [h, h2])
            s3d = sums[0].rearrange("p (b f) -> p b f", b=NBB)
            h = add("dve", lambda e, s3d=s3d: e.tensor_scalar(recip[:, 0:NBB], s3d[:, :, P + 1], 1e-20, None, ALU.add), [h, prev_n])
            h = add("dve", lambda e: e.reciprocal(recip[:, 0:NBB], recip[:, 0:NBB]), [h])
            a3 = s3d[:, :, 0:P]
            h = add("dve", lambda e, a3=a3: e.tensor_tensor(a3, a3, view(recip[:, :], [(1, NBB), (0, P)]), ALU.mult), [h])
            prev_n = h
            ld = []
            tx = transposed(x3, 0, [ld, prm], [hT_read])
            ta = []
            for q, (lo, hi) in enumerate(((0, 4), (4, NBB))):
                for k in range(lo, hi):
                    tp = add("pe", lambda e, k=k, q=q, lo=lo, a3=a3: e.transpose(bank[2 + q][:, (k - lo) * P:(k - lo + 1) * P],
                                                                                a3[:, k, :], ident[:, :]), [h, aggT_read])
                ta.append(add("act", lambda e, q=q, lo=lo, hi=hi: e.copy(aggT[:, lo * P:hi * P], bank[2 + q][:, 0:(hi - lo) * P]),
                              [tp, aggT_read]))
            evs = []
            for q, (lo, hi) in enumerate(((0, 4), (4, NBB))):
                for k in range(lo, hi):
                    o = bank[4 + q][:, (k - lo) * P:(k - lo + 1) * P]
                    add("pe", lambda e, k=k, o=o: e.matmul(o, hT[0][:, k * P:(k + 1) * P], wcol(0), start=True, stop=False),
                        [tx, ta, prm, ps_read[q]])
                    mm = add("pe", lambda e, k=k, o=o: e.matmul(o, aggT[:, k * P:(k + 1) * P], wcol(1), start=False, stop=True), [])
                evs.append(add("dve", lambda e, q=q, lo=lo, hi=hi, a3=a3: e.tensor_tensor(
                    a3[:, lo:hi, :], bank[4 + q][:, 0:(hi - lo) * P].rearrange("p (k f) -> p k f", f=P),
                    view(wcol(2), [(0, hi - lo), (1, P)]), ALU.add), [mm, ta]))
                ps_read[q] = evs[-1]
            aggT_read = mm
            ln = layer_norm(a3, [evs, ln_prev], 0)
            g1 = add("dve", lambda e, a3=a3: e.tensor_tensor(a3, a3, bias3(3), ALU.mult), [ln])
            g2 = bias_add(a3, a3, 4, [g1])
            g3 = add("dve", lambda e, a3=a3, x3=x3: e.tensor_tensor(a3, a3, x3, ALU.add), [g2, ld])
            ln = layer_norm(a3, [g3], 0)
            ln_prev = ln
            sx = dma("sp", lambda e, t=t, a3=a3: e.dma_start(blocks(res[0], t), a3), [ln])
            tt = transposed(a3, 0, [ln], [mm])
            stage = agg
            s3 = tile3(2 + t % 2)
            for q, (lo, hi) in enumerate(((0, 4), (4, NBB))):
                for k in range(lo, hi):
                    m1 = add("pe", lambda e, k=k, q=q, lo=lo: e.matmul(bank[6 + q][:, (k - lo) * P:(k - lo + 1) * P],
                                                                       hT[0][:, k * P:(k + 1) * P], wcol(5), start=True, stop=True),
                             [tt, sc_read])
            for k in range(NBB):
                m2 = add("pe", lambda e, k=k: e.matmul(bank[2][:, 2 * k:2 * k + 2], hT[0][:, k * P:(k + 1) * P], wcol(7)[:, 0:2],
                                                       start=True, stop=True), [tt, ta, sc_read])
            hT_read = m2
            x_free[t % 2] = [tt, sx]
            e1 = [add("dve", lambda e, q=q, lo=lo, hi=hi, x3=x3: e.tensor_tensor(
                x3[:, lo:hi, :], bank[6 + q][:, 0:(hi - lo) * P].rearrange("p (k f) -> p k f", f=P),
                view(wcol(6), [(0, hi - lo), (1, P)]), ALU.add), [m1, sx, tt]) for q, (lo, hi) in enumerate(((0, 4), (4, NBB)))]
            ps = bank[2][:, 0:2 * NBB].rearrange("p (k s) -> p k s", s=2)
            e2 = add("dve", lambda e, t=t, ps=ps: e.tensor_scalar(dst_side[:, t * NBB:(t + 1) * NBB, 0], ps[:, :, 0], wcol(8)[:, 0:1], None,
                                                                 ALU.add), [m2])
            e3 = add("dve", lambda e, t=t, ps=ps: e.tensor_copy(agg[:, t * NBB:(t + 1) * NBB, P], ps[:, :, 1]), [m2])
            sc_read = [e1, e2, e3]
            aggT_read = [aggT_read, e2, e3]
            st = dma("sp", lambda e, t=t: e.dma_start(blocks(gather_s2, t), agg[:, t * NBB:(t + 1) * NBB, 0:P + 1]), [e1, e3])
            tail += [st, sx, e1, e2, e3]
        p3 = edge_pass("L2", gather_s2, 1, False, [tail])

        prog.stage("dense4")
        prm = [transpose_weight(k, a["L2_gnn_w_ih"][k * P:(k + 1) * P, :], 4 + k, [p3], k) for k in range(3)]
        prm += [transpose_weight(3 + k, a["L2_gnn_w_hh"][k * P:(k + 1) * P, :], 7 + k if k < 2 else 3, [p3], 3 + k) for k in range(3)]
        prm += load_rows([(wcol(6, 3), row_bcast(a["L2_gnn_b_ih"], 0, 3 * P)), (lrelu[:, 0, 0:3 * P], row_bcast(a["L2_gnn_b_hh"], 0, 3 * P)),
                          (wcol(9), a["L3_gnn_W_src"]), (wcol(10), a["L3_gnn_W_dst"]),
                          (att[:, :], a["attn_row"] if "attn_row" in a else row_bcast(a["L3_gnn_attn"]))], [p3])
        prm.append(add("dve", lambda e: e.tensor_tensor(wcol(6, 2), wcol(6, 2), lrelu[:, 0, 0:2 * P], ALU.add), [prm]))
        bhn = lrelu[:, 0, 2 * P:3 * P]
        oeT = oh_e[:, :, :].rearrange("p a b -> p (a b)")[:, 0:NBB * P]
        rz = tile3(4), tile3(5)
        tmp3, msk3 = tile3(6), tile3(7)
        mask = xw[:, 0, 0:NBB]
        nmask = xw[:, 0, 16:16 + NBB]
        bb3 = lambda ap: view(ap, [(0, NBB), (1, P)])
        every = []
        x_free, st_free = [[], []], [[], []]
        tail = []
        for t in range(NBT):
            a3 = agg[:, t * NBB:(t + 1) * NBB, 0:P]
            x3 = tile3(t % 2)
            ld = dma("sp", lambda e, t=t, x3=x3: e.dma_start(x3, blocks(res[0], t)), [p3, prm, x_free[t % 2]])
            mk = add("dve", lambda e, t=t: e.tensor_scalar(mask, agg[:, t * NBB:(t + 1) * NBB, P + 1], 0.0, None, ALU.is_gt), [p3, every])
            mk2 = add("dve", lambda e: e.tensor_scalar(nmask, mask, -1.0, 1.0, ALU.mult, ALU.add), [mk])
            h = normalise(t, 1, 0.0, [p3, every], guard=1e-30)
            h1 = add("dve", lambda e, a3=a3: e.tensor_scalar(tmp3, a3, 0.0, None, ALU.min), [h, prm, every])
            h2 = add("act", lambda e: e.activation(tmp3, tmp3, ACT.Exp), [h1])
            h3 = add("dve", lambda e, a3=a3: e.tensor_scalar(a3, a3, 0.0, -1.0, ALU.max, ALU.add), [h1])
            h4 = add("dve", lambda e, a3=a3: e.tensor_tensor(a3, a3, tmp3, ALU.add), [h2, h3])
            h5 = add("dve", lambda e, a3=a3: e.tensor_tensor(a3, a3, view(mask, [(1, NBB), (0, P)]), ALU.mult), [h4, mk])
            h6 = add("dve", lambda e, x3=x3: e.tensor_tensor(msk3, x3, view(nmask, [(1, NBB), (0, P)]), ALU.mult), [ld, mk2, every])
            oe = add("dve", lambda e, a3=a3: e.tensor_tensor(a3, a3, msk3, ALU.add), [h5, h6])
            tx = transposed(x3, 0, [ld, prm], [every])
            to = []
            for q, (lo, hi) in enumerate(((0, 4), (4, NBB))):
                for k in range(lo, hi):
                    tp = add("pe", lambda e, k=k, q=q, lo=lo, a3=a3: e.transpose(bank[2 + q][:, (k - lo) * P:(k - lo + 1) * P],
                                                                                a3[:, k, :], ident[:, :]), [oe, every])
                to.append(add("act", lambda e, q=q, lo=lo, hi=hi: e.copy(oeT[:, lo * P:hi * P], bank[2 + q][:, 0:(hi - lo) * P]),
                              [tp, every]))
            evs = []
            bread = {}
            for k in range(NBB):
                B = bank[4 + k % 4]
                wait = [tx, to, prm, every, bread.get(k % 4, [])]
                add("pe", lambda e, k=k, B=B: e.matmul(B[:, 0:2 * P], oeT[:, k * P:(k + 1) * P], wcol(0, 2), start=True, stop=False), wait)
                add("pe", lambda e, k=k, B=B: e.matmul(B[:, 0:2 * P], hT[0][:, k * P:(k + 1) * P], wcol(3, 2), start=False, stop=True), [])
                add("pe", lambda e, k=k, B=B: e.matmul(B[:, 2 * P:3 * P], oeT[:, k * P:(k + 1) * P], wcol(2), start=True, stop=True), [])
                mm = add("pe", lambda e, k=k, B=B: e.matmul(B[:, 3 * P:4 * P], hT[0][:, k * P:(k + 1) * P], wcol(5), start=True, stop=True), [])
                rzk = node_tile(4)[:, 0:1]
                v1 = add("dve", lambda e, k=k, B=B: e.tensor_tensor(view(tile3(4)[:, k, :], [(NBB * P, 2), (1, P)]),
                                                                    B[:, 0:2 * P].rearrange("p (s f) -> p s f", s=2),
                                                                    wcol(6, 2).rearrange("p (s f) -> p s f", s=2), ALU.add), [mm])
                v2 = add("dve", lambda e, k=k, B=B: e.tensor_tensor(msk3[:, k, :], B[:, 2 * P:3 * P], wcol(8), ALU.add), [mm, oe])
                v3 = add("dve", lambda e, k=k, B=B: e.tensor_tensor(tmp3[:, k, :], B[:, 3 * P:4 * P], bhn, ALU.add), [mm, h4])
                bread[k % 4] = [v1, v2, v3]
                evs.append([v1, v2, v3])
            r1 = add("act", lambda e: e.activation(view(node_tile(4), [(1, 2 * NBB * P)]), view(node_tile(4), [(1, 2 * NBB * P)]),
                                                   ACT.Tanh, scale=0.5), [evs])
            r2 = add("dve", lambda e: e.tensor_scalar(view(node_tile(4), [(1, 2 * NBB * P)]), view(node_tile(4), [(1, 2 * NBB * P)]),
                                                      0.5, 0.5, ALU.mult, ALU.add), [r1])
            n1 = add("dve", lambda e: e.tensor_tensor(tmp3, tmp3, rz[0], ALU.mult), [r2])
            n2 = add("dve", lambda e: e.tensor_tensor(tmp3, tmp3, msk3, ALU.add), [n1])
            n3 = add("act", lambda e: e.activation(tmp3, tmp3, ACT.Tanh), [n2])
            o1 = add("dve", lambda e: e.tensor_scalar(rz[0], rz[1], -1.0, 1.0, ALU.mult, ALU.add), [n1, r2])
            o2 = add("dve", lambda e: e.tensor_tensor(tmp3, tmp3, rz[0], ALU.mult), [n3, o1])
            o3 = add("dve", lambda e, x3=x3: e.tensor_tensor(rz[1], rz[1], x3, ALU.mult), [o1])
            o4 = add("dve", lambda e: e.tensor_tensor(tmp3, tmp3, rz[1], ALU.add), [o2, o3])
            o5 = add("dve", lambda e, a3=a3, x3=x3: e.tensor_tensor(a3, tmp3, x3, ALU.add), [o4, to])
            ln = layer_norm(a3, [o5], 0)
            sx = dma("sp", lambda e, t=t, a3=a3: e.dma_start(blocks(res[1], t), a3), [ln])
            tt = transposed(a3, 0, [ln], [mm, tx])
            ev, st = two_sided(t, 9, None, None, [tt, prm], [evs] * 4, tile3(2 + t % 2), [st_free[t % 2], prm], gather_c)
            st_free[t % 2] = [st]
            x_free[t % 2] = [o5, tx, h6]
            every = [ev]
            tail += [st, sx, ev]
        p4 = edge_pass("L3", gather_c, 8, True, [tail])

        prog.stage("dense5")
        prm = load_rows([(wcol(0), a["L3_gnn_W_out"]), (wcol(1), row_bcast(a["L3_gnn_b_out"])),
                         (wcol(2), row_bcast(a["L3_gnn_gamma"])), (wcol(3), row_bcast(a["L3_gnn_beta"]))], [p4])
        x_free, n_free = [[], []], [[], []]
        prev_n, ps_read, ht_read, ln_prev = None, [[], []], [], []
        tail = []
        for t in range(NBT):
            a3 = agg[:, t * NBB:(t + 1) * NBB, 0:P]
            x3, n3_ = tile3(t % 2), tile3(2 + t % 2)
            ld = dma("sp", lambda e, t=t, x3=x3: e.dma_start(x3, blocks(res[1], t)), [p4, x_free[t % 2]])
            h = normalise(t, 8, 1e-8, [p4, prev_n])
            hw = P // 8
            muls = []
            for k in range(NBB):
                muls.append(add("dve", lambda e, k=k, t=t, n3_=n3_: e.tensor_tensor(
                    n3_[:, k, :].rearrange("p (h d) -> p h d", h=8), view(agg[:, t * NBB + k, :], [(hw + 1, 8), (1, hw)]),
                    view(recip[:, k * 8:], [(1, 8), (0, hw)]), ALU.mult), [h, n_free[t % 2]]))
            prev_n = muls
            tt = transposed(n3_, 0, [muls, prm], [ht_read])
            n_free[t % 2] = tt
            evs = []
            for q, (lo, hi) in enumerate(((0, 4), (4, NBB))):
                for k in range(lo, hi):
                    mm = add("pe", lambda e, k=k, q=q, lo=lo: e.matmul(bank[4 + q][:, (k - lo) * P:(k - lo + 1) * P],
                                                                       hT[0][:, k * P:(k + 1) * P], wcol(0), start=True, stop=True),
                             [tt, prm, ps_read[q]])
                evs.append(add("dve", lambda e, q=q, lo=lo, hi=hi, a3=a3: e.tensor_tensor(
                    a3[:, lo:hi, :], bank[4 + q][:, 0:(hi - lo) * P].rearrange("p (k f) -> p k f", f=P),
                    view(wcol(1), [(0, hi - lo), (1, P)]), ALU.add), [mm, muls]))
                ps_read[q] = evs[-1]
            ht_read = mm
            h = add("dve", lambda e, a3=a3, x3=x3: e.tensor_tensor(a3, a3, x3, ALU.add), [evs, ld])
            ln = layer_norm(a3, [h, ln_prev], 0)
            h = add("dve", lambda e, a3=a3: e.tensor_tensor(a3, a3, bias3(2), ALU.mult), [ln])
            h = bias_add(a3, a3, 3, [h])
            h = add("dve", lambda e, a3=a3, x3=x3: e.tensor_tensor(a3, a3, x3, ALU.add), [h])
            x_free[t % 2] = h
            ln = layer_norm(a3, [h], 0)
            ln_prev = ln
            lo, hi = t * NBB * P, (t + 1) * NBB * P
            if hi <= N:
                tail.append(dma("sp", lambda e, a3=a3, lo=lo, hi=hi: e.dma_start(out[lo:hi, :].rearrange("(b p) f -> p b f", p=P), a3), [ln]))
            else:
                full = (N - lo) // P
                rem = N - lo - full * P
                if full:
                    tail.append(dma("sp", lambda e, a3=a3, lo=lo, full=full: e.dma_start(
                        out[lo:lo + full * P, :].rearrange("(b p) f -> p b f", p=P), a3[:, 0:full, :]), [ln]))
                if rem:
                    tail.append(dma("sp", lambda e, a3=a3, lo=lo, full=full, rem=rem: e.dma_start(
                        out[lo + full * P:N, :], a3[0:rem, full, :]), [ln]))
        prog.queue["sp"].append(lambda eng, last, w=list(flat(tail)): [eng.wait_ge(x.sem, x.value) for x in w])

        block = ctx.enter_context(nc.Block())

        @block.sync
        def _(eng):
            prog.play("sp", eng)

        @block.gpsimd
        def _(eng):
            prog.play("pool", eng)

        @block.scalar
        def _(eng):
            prog.play("act", eng)

        @block.vector
        def _(eng):
            prog.play("dve", eng)

        @block.tensor
        def _(eng):
            prog.play("pe", eng)


def kernel(**inputs):
    import numpy as _np
    import concourse.bacc as _bacc
    from concourse import mybir as _mybir
    from concourse.bass_utils import run_bass_kernel_spmd as _run

    x = _np.ascontiguousarray(inputs["x"])
    n_nodes, n_edges = x.shape[0], inputs["src"].shape[0]
    nb = -(-n_nodes // P)
    t_real = -(-n_edges // P)
    sc = -(-(t_real + nb) // P)
    pad = sc * P * P - n_edges
    src = _np.concatenate([_np.asarray(inputs["src"]), _np.full(pad, nb * P - 1, _np.int32)]).reshape(sc * P, P)
    dst = _np.concatenate([_np.asarray(inputs["dst"]), _np.full(pad, nb * P - 1, _np.int32)]).reshape(sc * P, P)
    arrays = {name: _np.ascontiguousarray(v) for name, v in inputs.items() if name not in ("x", "src", "dst")}
    arrays.update(x=x, src=src, dst=dst)
    k = _np.arange(P)
    arrays["c_ident"] = _np.eye(P, dtype=_np.float32)
    arrays["c_iota"] = _np.tile(k.astype(_np.float32), (P, 1))
    arrays["c_ohw"] = _np.stack([k * 0 + 1, k * 0 + 1, -2 * k, (k * k) // 256 * 256, (k * k) % 256]).astype(_mybir.dt.np(BF16))
    arrays["c_ohs"] = _np.concatenate([_np.stack([k * 0 + 1, k * 0 + 1, -2 * k, k * 0, (k * k) // 256 * 256, (k * k) % 256]),
                                       _np.repeat(_np.array([[0], [0], [1], [1], [0], [0]]), P, 1)], 1).astype(_mybir.dt.np(BF16))
    arrays["c_dump"] = (nb * P + k[:, None]).astype(_np.float32)
    arrays["c_tril"] = (k[None, :] < k[:, None]).astype(_np.float32)
    arrays["c_steps"] = (_np.arange(sc)[None, :] * P + k[:, None]).astype(_np.float32)

    nc = _bacc.Bacc("TRN2", target_bir_lowering=False, num_devices=1)
    feed, args = {}, {"t_real": t_real}
    for name, v in arrays.items():
        feed[f"in_{name}_dram"] = v
        args[name] = nc.dram_tensor(f"in_{name}_dram", v.shape, _mybir.dt.from_np(v.dtype), kind="ExternalInput").ap()
    out = nc.dram_tensor("out_0_dram", x.shape, F32, kind="ExternalOutput").ap()
    build(nc, args, out)
    r = _run(nc, [feed], core_ids=[0])
    return r.results[0]["out_0_dram"]
```

```python
from contextlib import ExitStack

import concourse.bass as bass
from concourse import mybir

F32 = mybir.dt.float32
BF16 = mybir.dt.bfloat16
I32 = mybir.dt.int32
ALU = mybir.AluOpType
ACT = mybir.ActivationFunctionType
AX = mybir.AxisListType

ENGINE = {"dve": mybir.EngineType.DVE, "pe": mybir.EngineType.PE}

P = 128
NEG = -1.0e30
SLOPE = 0.2
LN_EPS = 1e-5
G = 16
U = 4
CH = 4
NCH = G // CH
AW = 136
XW = 130
NSUM = 4
NBB = 7


def view(ap, free):
    return bass.AP(ap.tensor, ap.offset, [tuple(ap.ap[0])] + [tuple(f) for f in free])


class Done:

    def __init__(self, sem, value):
        self.sem, self.value = sem, value


class Program:
    ENGINES = ("pe", "act", "dve", "pool", "sp")
    DMA_RING = 8

    def __init__(self, nc, ctx):
        self.nc, self.ctx = nc, ctx
        self.queue = {e: [] for e in self.ENGINES}
        self.stage("start")
        self.ring = {e: [self.sem(f"{e}_dma{n}") for n in range(self.DMA_RING)] for e in ("sp", "pool")}
        self.ring_n = {e: 0 for e in ("sp", "pool")}
        self.anchor = self.sem("wait_anchor")

    def sem(self, name):
        return self.ctx.enter_context(self.nc.semaphore(name))

    def stage(self, name):
        self.name = name
        self.done_sem = {}
        self.count = {e: 0 for e in self.ENGINES}

    def engine_sem(self, e):
        if e not in self.done_sem:
            self.done_sem[e] = self.sem(f"{self.name}_{e}_done")
        return self.done_sem[e]

    def add(self, e, fn, after=()):
        sem = self.engine_sem(e)
        self.count[e] += 1
        waits = list(flat(after))

        def emit(eng, last):
            for w in waits:
                if last.get(id(w.sem), 0) < w.value:
                    eng.wait_ge(w.sem, w.value)
                    last[id(w.sem)] = w.value
            fn(eng).then_inc(sem, 1)

        self.queue[e].append(emit)
        return Done(sem, self.count[e])

    def dma(self, e, fn, after=()):
        n = self.ring_n[e]
        self.ring_n[e] += 1
        sem, turn = self.ring[e][n % self.DMA_RING], n // self.DMA_RING
        waits = list(flat(after)) + ([Done(sem, 16 * turn)] if turn else [])

        def emit(eng, last):
            for w in waits:
                if last.get(id(w.sem), 0) < w.value:
                    eng.wait_ge(w.sem, w.value)
                    last[id(w.sem)] = w.value
            fn(eng).then_inc(sem, 16)

        self.queue[e].append(emit)
        return Done(sem, 16 * (turn + 1))

    def play(self, e, eng):
        last = {}
        for emit in self.queue[e]:
            emit(eng, last)


def flat(x):
    if isinstance(x, Done):
        yield x
    elif x is not None:
        for y in x:
            yield from flat(y)


class Op:

    def __init__(self, e, fn, after, lag, anchored):
        self.e, self.fn, self.after, self.lag, self.anchored = e, fn, after, lag, anchored
        self.counted = False


class SlotDma(Op):

    def __init__(self, e, fn, after, sems, base, gain):
        super().__init__(e, fn, after, 0, True)
        self.sems, self.base, self.gain = sems, base, gain


class Loop:

    PEELED = 2 * U

    def __init__(self, prog, n):
        self.prog, self.n, self.ops = prog, n, []
        assert n % U == 0 and n > self.PEELED

    def op(self, e, fn, after=(), lag=0, anchored=False):
        o = Op(e, fn, [(a, 0) if isinstance(a, Op) else a for a in after if a is not None], lag, anchored)
        self.ops.append(o)
        return o

    def slot_dma(self, e, fn, after, sems, base, gain):
        o = SlotDma(e, fn, [(a, 0) if isinstance(a, Op) else a for a in after], sems, base, gain)
        self.ops.append(o)
        return o

    def active(self, o, turn):
        return 0 <= turn - o.lag < self.n

    def close(self):
        prog = self.prog
        for o in self.ops:
            for p, _ in o.after:
                if not isinstance(p, SlotDma):
                    p.counted = True
        self.depth = max(o.lag for o in self.ops)
        self.end = self.n + self.depth
        counted = [o for o in self.ops if o.counted]
        self.per = {}
        for o in counted:
            self.per[o.e] = self.per.get(o.e, 0) + 1
            o.pos = self.per[o.e]
        self.counted = counted
        self.sems = {e: prog.engine_sem(e) for e in self.per}
        self.filled = {e: sum(self.active(o, t) for o in counted if o.e == e for t in range(self.depth)) for e in self.per}
        for e in prog.ENGINES:
            prog.queue[e].append(lambda eng, last, e=e: self.play(e, eng, last))
        for e in self.per:
            prog.count[e] += self.per[e] * self.n

    def last(self, o):
        return Done(self.sems[o.e], self.value(o, self.n - 1 + o.lag))

    def value(self, p, turn):
        if not self.active(p, turn):
            return None
        mine = [o for o in self.counted if o.e == p.e]
        return (sum(min(max(turn - o.lag, 0), self.n) for o in mine)
                + sum(self.active(o, turn) for o in mine if o.pos <= p.pos))

    def play(self, e, eng, last):
        ops = [o for o in self.ops if o.e == e]
        if not ops:
            return
        prog = self.prog
        seen = {}

        def run(o, i, u, reg, j):
            for p, d in o.after:
                if isinstance(p, SlotDma):
                    sem = p.sems[(u - d) % U]
                    if reg is None:
                        if not self.active(p, i - d):
                            continue
                        const, step = p.base + p.gain * ((i - d) // U + 1), 0
                    else:
                        const, step = p.base + p.gain * ((u - d) // U + 1), p.gain
                else:
                    sem = self.sems[p.e]
                    if reg is None:
                        const, step = self.value(p, i - d), 0
                        if const is None:
                            continue
                    else:
                        const = self.filled[p.e] + self.per[p.e] * (u - d - self.depth) + p.pos
                        step = self.per[p.e] * U
                key = id(sem)
                if key in seen and seen[key] >= const:
                    continue
                seen[key] = const
                if reg is None:
                    eng.wait_ge(sem, const)
                else:
                    eng.wait_ge(sem, j * step + const)
                    if o.anchored:
                        eng.sem_inc(prog.anchor, 1)
            ins = o.fn(eng, u, i)
            if o.counted and not isinstance(o, SlotDma):
                ins.then_inc(self.sems[e], 1)

        for i in range(self.PEELED):
            for o in ops:
                if self.active(o, i):
                    run(o, i, i % U, None, None)
        seen.clear()
        with eng.Fori(self.PEELED // U, self.n // U) as j:
            for u in range(U):
                for o in ops:
                    run(o, j * U + u, u, True, j)
        seen.clear()
        for i in range(self.n, self.end):
            for o in ops:
                if self.active(o, i):
                    run(o, i, i % U, None, None)
        last.clear()


def build(nc, a, out):
    N = a["x"].shape[0]
    T = a["src"].shape[0]
    NB = -(-N // P)
    T_REAL = a["t_real"]
    SC = -(-(T_REAL + NB) // P)
    S = SC * P
    NG = S // G
    assert T == S and NG % U == 0 and NB % NBB == 0
    GC = P // G

    def dram(name, shape, dt=F32):
        return nc.dram_tensor(name, shape, dt).ap()

    ET = 5 * G
    edge_tab = dram("edge_tab", (NG, P, ET))
    onehot_tab = dram("onehot_tab", (3, S * P), BF16)
    source_tab = dram("source_tab", (4, S * P), BF16)
    step_tab = dram("step_tab", (S, 2 * P + 2))
    col_tab = dram("col_tab", (3 * SC, P))
    R1, R8 = 2 * G + 1 + 2 * G, 8 * (2 * G + 1) + 2 * G
    row_tab1 = dram("row_tab1", (NG, R1))
    row_tab8 = dram("row_tab8", (NG, R8))
    gather_a = dram("gather_a", (NB * P, P))
    gather_b = dram("gather_b", (NB * P, P))
    gather_c = dram("gather_c", (NB * P, P))
    scatter_s = [dram(f"scatter_s{k}", (NB * P + P, XW)) for k in range(NSUM)]
    gather_s2 = dram("gather_s2", (NB * P, P + 1))
    res = [dram(f"residual{n}", (NB * P, P)) for n in range(2)]

    with ExitStack() as ctx:
        prog = Program(nc, ctx)
        add, dma = prog.add, prog.dma

        def sb(name, shape, dt=F32):
            return ctx.enter_context(nc.sbuf_tensor(name, shape, dt))

        bank = [ctx.enter_context(nc.psum_tensor(f"bank{n}", [P, 512], F32)) for n in range(8)]

        ident = sb("ident", [P, P])
        iota = sb("iota", [P, P])
        ones = sb("ones", [P, P])
        oh_w = sb("oh_w", [5, P], BF16)
        minus_half = sb("minus_half", [P, NBB])
        agg = sb("agg", [P, NB, AW])
        dst_side = sb("dst_side", [P, max(NB, 64), P])
        dst_score = sb("dst_score", [P, NB])
        rows = sb("rows", [P, U, G, XW])
        lrelu = sb("lrelu", [P, 2, CH * P])
        oh_t = sb("oh_t", [P, 2, CH * P])
        oh_e = sb("oh_e", [P, 8, P])
        xw = sb("xw", [P, 2, CH * AW])
        edge_sb = sb("edge_sb", [P, U, ET])
        oh_ws = sb("oh_ws", [6, 2 * P], BF16)
        dump_row = sb("dump_row", [P, 1])
        oh_rows = sb("oh_rows", [5, U, G * P], BF16)
        step_sb = sb("step_sb", [P, U, 2 * P + 2])
        row_sb = sb("row_sb", [1, U, R8])
        param = sb("param", [P, 12 * P])
        att = sb("att", [P, P])
        logit = sb("logit", [P, P])
        masked = sb("masked", [P, 2, P])
        seg_fwd = sb("seg_fwd", [P, P])
        seg_max = sb("seg_max", [P, P])
        run_max = sb("run_max", [P, P])
        shifted = sb("shifted", [P, P])
        weight = sb("weight", [P, 2, P])
        minus_w = sb("minus_w", [P, 2, G])
        rescale = sb("rescale", [P, 2, P])
        decay_m = sb("decay_m", [P, P])
        carry = sb("carry", [1, 8 * (G + 1)])
        carry_in = sb("carry_in", [1, 8 * (G + 1)])
        cin_row = sb("cin_row", [1, P])
        cin = sb("cin", [P, 4])
        acc_tmp = sb("acc_tmp", [P, 2, AW])
        stats = sb("stats", [P, NBB, 6])
        moments = sb("moments", [P, NBB, 2])
        rstd = sb("rstd", [P, 2, NBB])
        recip = sb("recip", [P, 8 * NBB])
        col3 = sb("col3", [P, 3 * SC])

        s_tab = [prog.sem(f"tables_in_slot{u}") for u in range(U)]
        s_gat = [[prog.sem(f"rows_in_slot{u}_chunk{c}") for u in range(U)] for c in range(NCH)]
        tab_base = [0]
        gat_base = [0]

        prog.stage("prep")
        ld_id = dma("sp", lambda e: e.dma_start(ident[:, :], a["c_ident"]))
        ld_iota = dma("sp", lambda e: e.dma_start(iota[:, :], a["c_iota"]))
        ld_ohw = dma("sp", lambda e: e.dma_start(oh_w[:, :], a["c_ohw"]))
        ld_ohs = dma("sp", lambda e: e.dma_start(oh_ws[:, :], a["c_ohs"]))
        ld_dump = dma("sp", lambda e: e.dma_start(dump_row[:, :], a["c_dump"]))
        big1 = agg[:, :, :].rearrange("p a b -> p (a b)")
        big2 = dst_side[:, :, :].rearrange("p a b -> p (a b)")
        pool_rows = rows[:, :, :, :].rearrange("p a b c -> p (a b c)")
        ld_sn = dma("sp", lambda e: e.dma_start(pool_rows[:, 0:SC], a["c_steps"]))
        first_i = pool_rows[:, 32:32 + SC].bitcast(I32)

        def load_first(e):
            with nc.allow_non_contiguous_dma(reason="first node of each tile"):
                return e.dma_start(first_i, a["dst"][:, 0:1].rearrange("(c p) o -> p (c o)", p=P))
        ld_first = dma("sp", load_first)
        m_ones = add("dve", lambda e: e.memset(ones[:, :], 1.0))
        m_half = add("dve", lambda e: e.memset(minus_half[:, :], -0.5))
        m_oh = add("dve", lambda e: e.memset(oh_rows[:, :, :], 1.0))
        fb = pool_rows[:, 64:64 + SC]
        fbi = pool_rows[:, 96:96 + SC].bitcast(I32)
        keyc = pool_rows[:, 128:128 + SC]
        snum = pool_rows[:, 0:SC]
        tcol = pool_rows[:, 160:160 + SC]
        tcoli = sb("tcoli", [P, SC], I32)
        bcol = pool_rows[:, 192:192 + SC]
        b128 = pool_rows[:, 224:224 + SC]
        h = add("dve", lambda e: e.tensor_single_scalar(fbi, first_i, 7, ALU.arith_shift_right), [ld_first])
        h = add("dve", lambda e: e.tensor_copy(fb, fbi), [h])
        key_done = add("dve", lambda e: e.tensor_tensor(keyc, fb, snum, ALU.add), [h, ld_sn])
        key = big2[:, 0:S]
        compare = big2[:, S:2 * S]
        kcol = big2[:, 2 * S:2 * S + SC * P]
        spread = []
        for c in range(SC):
            spread.append(add("dve", lambda e, c=c: e.tensor_scalar(kcol[:, c * P:(c + 1) * P], ones[:, :],
                                                                  keyc[:, c:c + 1], None, ALU.mult), [key_done, m_ones]))
        key_copied = []
        for c in range(SC):
            mm = add("pe", lambda e, c=c: e.matmul(bank[c % 8][:, 0:P], kcol[:, c * P:(c + 1) * P], ident[:, :],
                                                 start=True, stop=True),
                     [spread[c], ld_id, key_copied[c - 8:c - 7] if c >= 8 else []])
            key_copied.append(add("act", lambda e, c=c: e.copy(key[:, c * P:(c + 1) * P], bank[c % 8][:, 0:P]), [mm]))
        last = None
        for c in range(SC):
            h = add("dve", lambda e, c=c: e.tensor_scalar(compare[:, 1:], key[:, 1:], snum[:, c:c + 1], None, ALU.is_le),
                    [key_copied, last])
            last = add("dve", lambda e, c=c: e.tensor_reduce(tcol[:, c:c + 1], compare[:, 1:], AX.X, ALU.add), [h])
        t_int = add("dve", lambda e: e.tensor_copy(tcoli[:, :], tcol), [last])
        h = add("dve", lambda e: e.tensor_tensor(bcol, snum, tcol, ALU.subtract), [last])
        blk_done = add("dve", lambda e: e.tensor_scalar(bcol, bcol, float(NB - 1), None, ALU.min), [h])
        b128_done = add("dve", lambda e: e.tensor_scalar(b128, bcol, float(P), None, ALU.mult), [blk_done])
        c3b = add("dve", lambda e: e.tensor_copy(col3[:, 0:SC], bcol), [blk_done])

        NR = 2
        base = 256
        W1 = 2 * P + 2

        def tile_set(k):
            o = base + k * 2560
            f = lambda n, w: pool_rows[:, o + n:o + n + w]
            return dict(di=f(0, P).bitcast(I32), si=f(P, P).bitcast(I32), d=f(2 * P, P), s=f(3 * P, P),
                        rel=f(4 * P, P), sq=f(5 * P, P), sqi=f(6 * P, P).bitcast(I32), lo=f(7 * P, P),
                        st=f(8 * P, W1), hl=f(8 * P + W1, 3 * P // 2).bitcast(BF16),
                        qi=f(12 * P, P).bitcast(I32), q=f(13 * P, P), r=f(14 * P, P), rr=f(15 * P, P),
                        rri=f(16 * P, P).bitcast(I32), rlo=f(17 * P, P), sl=f(18 * P, 2 * P).bitcast(BF16))
        edge_stage = big1[:, 0:NG * ET].rearrange("p (g k) -> p g k", k=ET)
        mtmp = big2[:, 3 * S:3 * S + P]
        prev = [None, None]
        st_saved = []
        edge_done = []
        relT_free = None
        for c in range(SC):
            t = tile_set(c % NR)
            g_d = dma("pool", lambda e, t=t, c=c: e.indirect_dma_start(
                t["di"], None, a["dst"], bass.IndirectOffsetOnAxis(ap=tcoli[:, c:c + 1], axis=0)), [t_int, prev[c % NR]])
            g_s = dma("pool", lambda e, t=t, c=c: e.indirect_dma_start(
                t["si"], None, a["src"], bass.IndirectOffsetOnAxis(ap=tcoli[:, c:c + 1], axis=0)), [t_int, prev[c % NR]])
            d_f = add("dve", lambda e, t=t: e.tensor_copy(t["d"], t["di"]), [g_d])
            s_f = add("dve", lambda e, t=t: e.tensor_copy(t["s"], t["si"]), [g_s])
            h = add("dve", lambda e, t=t, c=c: e.tensor_scalar(t["rel"], t["d"], b128[:, c:c + 1], float(P),
                                                              ALU.subtract, ALU.min), [d_f, b128_done])
            rel = add("dve", lambda e, t=t: e.tensor_scalar(t["rel"], t["rel"], -1.0, None, ALU.max), [h])
            p1 = add("dve", lambda e, t=t: e.memset(t["st"][:, 0:P + 1], NEG), [prev[c % NR]])
            p2 = add("dve", lambda e, t=t: e.tensor_tensor(t["st"][:, 1:P], t["d"][:, 1:P], t["d"][:, 0:P - 1],
                                                           ALU.not_equal), [p1, d_f])
            p3 = add("dve", lambda e, t=t: e.tensor_scalar(t["st"][:, 1:P], t["st"][:, 1:P], NEG, None, ALU.mult), [p2])
            p4 = add("dve", lambda e, t=t: e.tensor_scalar(t["st"][:, P + 1:2 * P + 1], t["d"], t["d"][:, 0:1], NEG,
                                                           ALU.not_equal, ALU.mult), [d_f])
            p5 = add("dve", lambda e, t=t: e.tensor_copy(t["st"][:, 2 * P + 1:2 * P + 2], t["rel"][:, 0:1]), [rel])
            st = dma("sp", lambda e, t=t, c=c: e.dma_start(step_tab[c * P:(c + 1) * P, :], t["st"]), [p3, p4, p5])
            h = add("dve", lambda e, t=t: e.tensor_tensor(t["sq"], t["rel"], t["rel"], ALU.mult), [rel])
            h = add("dve", lambda e, t=t: e.tensor_copy(t["sqi"], t["sq"]), [h])
            h = add("dve", lambda e, t=t: e.tensor_single_scalar(t["sqi"], t["sqi"], 255, ALU.bitwise_and), [h])
            h = add("dve", lambda e, t=t: e.tensor_copy(t["lo"], t["sqi"]), [h])
            q1 = add("dve", lambda e, t=t: e.tensor_tensor(t["hl"][:, 0:P], t["sq"], t["lo"], ALU.subtract), [h])
            q2 = add("dve", lambda e, t=t: e.tensor_copy(t["hl"][:, P:2 * P], t["lo"]), [h])
            q3 = add("dve", lambda e, t=t: e.tensor_copy(t["hl"][:, 2 * P:3 * P], t["rel"]), [rel])
            oh = dma("sp", lambda e, t=t, c=c: e.dma_start(
                onehot_tab[:, c * P * P:(c + 1) * P * P].rearrange("k (p n) -> p k n", p=P),
                t["hl"].rearrange("p (k n) -> p k n", k=3)), [q1, q2, q3])
            c1 = add("dve", lambda e, t=t, c=c: e.tensor_copy(col3[:, SC + c:SC + c + 1], t["d"][:, 0:1]), [d_f])
            c2 = add("dve", lambda e, t=t, c=c: e.tensor_copy(col3[:, 2 * SC + c:2 * SC + c + 1], t["d"][:, P - 1:P]), [d_f])
            qa = add("dve", lambda e, t=t: e.tensor_single_scalar(t["qi"], t["si"], 7, ALU.arith_shift_right), [g_s])
            qf = add("dve", lambda e, t=t: e.tensor_copy(t["q"], t["qi"]), [qa])
            h = add("dve", lambda e, t=t: e.scalar_tensor_tensor(t["r"], t["q"], -float(P), t["s"], ALU.mult, ALU.add), [qf, s_f])
            rf = h
            h = add("dve", lambda e, t=t: e.tensor_tensor(t["rr"], t["r"], t["r"], ALU.mult), [h])
            h = add("dve", lambda e, t=t: e.tensor_copy(t["rri"], t["rr"]), [h])
            h = add("dve", lambda e, t=t: e.tensor_single_scalar(t["rri"], t["rri"], 255, ALU.bitwise_and), [h])
            h = add("dve", lambda e, t=t: e.tensor_copy(t["rlo"], t["rri"]), [h])
            r1 = add("dve", lambda e, t=t: e.tensor_tensor(t["sl"][:, 0:P], t["rr"], t["rlo"], ALU.subtract), [h])
            r2 = add("dve", lambda e, t=t: e.tensor_copy(t["sl"][:, P:2 * P], t["rlo"]), [h])
            r3 = add("dve", lambda e, t=t: e.tensor_copy(t["sl"][:, 2 * P:3 * P], t["r"]), [rf])
            r4 = add("dve", lambda e, t=t: e.tensor_scalar(t["sl"][:, 3 * P:4 * P], t["q"], float(P), None, ALU.mult), [qf])
            sv = dma("sp", lambda e, t=t, c=c: e.dma_start(
                source_tab[:, c * P * P:(c + 1) * P * P].rearrange("k (p n) -> p k n", p=P),
                t["sl"].rearrange("p (k n) -> p k n", k=4)), [r1, r2, r3, r4])
            tr = add("pe", lambda e, t=t, c=c: e.transpose(bank[c % 2][:, 0:P], t["rel"], ident[:, :]),
                     [rel, edge_done[-4:]])
            ts = add("pe", lambda e, t=t, c=c: e.transpose(bank[c % 2][:, P:2 * P], t["s"], ident[:, :]),
                     [s_f, edge_done[-4:]])
            ts = add("pe", lambda e, t=t, c=c: e.transpose(bank[c % 2][:, 2 * P:3 * P], t["q"], ident[:, :]), [qf])
            tr = ts
            es = edge_stage[:, c * GC:(c + 1) * GC, :]
            part = lambda n, es=es: es[:, :, n * G:(n + 1) * G]
            ps = lambda n, c=c: bank[c % 2][:, n * P:(n + 1) * P].rearrange("p (g k) -> p g k", k=G)
            e1 = add("dve", lambda e, part=part, ps=ps: e.tensor_copy(part(0).bitcast(I32), ps(1)), [ts])
            e2 = add("dve", lambda e, part=part, ps=ps: e.tensor_copy(part(1), ps(0)), [tr])
            e3 = add("dve", lambda e, part=part, ps=ps: e.tensor_scalar(part(2), ps(0), 0.0, NEG, ALU.is_lt, ALU.mult), [tr])
            mt = mtmp.rearrange("p (g k) -> p g k", k=G)
            e4 = add("dve", lambda e, ps=ps, mt=mt: e.tensor_scalar(mt, ps(0), P - 0.5, NEG, ALU.is_gt, ALU.mult),
                     [tr, relT_free])
            e5 = add("dve", lambda e, part=part, mt=mt: e.tensor_tensor(part(2), part(2), mt, ALU.add), [e3, e4])
            relT_free = e5
            e6 = add("dve", lambda e, part=part, ps=ps: e.tensor_copy(part(3), ps(1)), [ts])
            e7 = add("dve", lambda e, part=part, ps=ps: e.tensor_copy(part(4), ps(2)), [ts])
            edge_done += [e1, e2, e5, e7]
            prev[c % NR] = [tr, ts, st, oh, sv, c1, c2, p4, p5, q3, e7]
            st_saved += [st, oh, sv]
        edge_saved = dma("sp", lambda e: e.dma_start(edge_tab.rearrange("g p k -> p g k"), edge_stage), [edge_done])
        tc = add("pe", lambda e: e.transpose(bank[2][0:3 * SC, 0:P], col3[:, :], ident[:, :]), [c1, c2, c3b, key_copied])
        cc = add("dve", lambda e: e.tensor_copy(seg_fwd[0:3 * SC, :], bank[2][0:3 * SC, 0:P]), [tc])
        cs = dma("sp", lambda e: e.dma_start(col_tab, seg_fwd[0:3 * SC, :]), [cc])
        brow = view(big2[0:1, 0:3 * S], [(1, 3 * S)])
        cl = dma("sp", lambda e: e.dma_start(brow, col_tab.rearrange("(o a) b -> o (a b)", o=1)), [cs, last, relT_free])
        grp = lambda k: big2[0:1, k * S:(k + 1) * S].rearrange("o (g k) -> o g k", k=G)
        RA = 3 * G + 1
        rt = big2[0:1, 3 * S:3 * S + NG * RA].rearrange("o (g k) -> o g k", k=RA)
        prevlast = big2[0:1, 3 * S + NG * RA:3 * S + NG * RA + S]
        z1 = add("dve", lambda e: e.memset(prevlast[:, 0:1], -5.0), [cl])
        z2 = add("dve", lambda e: e.tensor_copy(prevlast[:, 1:S], big2[0:1, 2 * S:3 * S - 1]), [cl])
        pl = prevlast.rearrange("o (g k) -> o g k", k=G)
        z3 = add("dve", lambda e: e.tensor_tensor(rt[:, :, 1:G + 1], grp(2), pl, ALU.not_equal), [z1, z2])
        z4 = add("dve", lambda e: e.tensor_tensor(rt[:, :, G + 1:2 * G + 1], grp(1), pl, ALU.not_equal), [z1, z2])
        z5 = add("dve", lambda e: e.tensor_scalar(rt[:, :, 1:2 * G + 1], rt[:, :, 1:2 * G + 1], NEG, None, ALU.mult), [z3, z4])
        z6 = add("dve", lambda e: e.memset(rt[:, :, 0:1], NEG), [cl])
        z7 = add("dve", lambda e: e.tensor_scalar(rt[:, :, 2 * G + 1:RA].bitcast(I32), grp(0), float(AW), None, ALU.mult), [cl])
        z8 = add("dve", lambda e: e.tensor_scalar(grp(2).bitcast(I32), grp(0), float(P), None, ALU.mult), [z2, z3])
        row_saved = [dma("sp", lambda e: e.dma_start(row_tab1[:, 0:RA].rearrange("(o g) k -> o g k", o=1), rt), [z5, z6, z7])]
        for tb, off in ((row_tab1, RA), (row_tab8, R8 - G)):
            row_saved.append(dma("sp", lambda e, tb=tb, off=off: e.dma_start(
                tb[:, off:off + G].rearrange("(o g) k -> o g k", o=1), grp(2)), [z8]))
        for hd in range(8):
            row_saved.append(dma("sp", lambda e, hd=hd: e.dma_start(
                row_tab8[:, hd * (G + 1):(hd + 1) * (G + 1)].rearrange("(o g) k -> o g k", o=1), rt[:, :, 0:G + 1]), [z5, z6]))
            row_saved.append(dma("sp", lambda e, hd=hd: e.dma_start(
                row_tab8[:, 8 * (G + 1) + hd * G:8 * (G + 1) + (hd + 1) * G].rearrange("(o g) k -> o g k", o=1),
                rt[:, :, G + 1:2 * G + 1]), [z5]))
        row_saved.append(dma("sp", lambda e: e.dma_start(
            row_tab8[:, 8 * (2 * G + 1):R8 - G].rearrange("(o g) k -> o g k", o=1), rt[:, :, 2 * G + 1:RA]), [z7]))
        tables = [st_saved, edge_saved, row_saved, m_oh, e6, ld_iota, ld_ohw, ld_ohs, ld_dump]
        idle = [tables, edge_done, prev[0], prev[1], tc]

        def load_offsets(L, e, at, unit, after, lag):
            box = {}

            def fn(eng, u, i):
                _, box["v"] = nc.values_load_multi_w_load_instructions(
                    row_sb[0:1, (u - lag) % U, at:at + G].bitcast(I32), engines=[ENGINE[e]], min_val=0, max_val=(NB - 1) * unit,
                    skip_runtime_bounds_check_because="the blocks are clamped to NB - 1 where the table is made")
            return L.op(e, fn, after, lag=lag, anchored=True), box

        def edge_pass(name, src_rows, heads, vector, ready):
            prog.stage(name)
            RW = heads * G
            width = P if vector else P + 1
            hw = P // heads
            aw = AW if heads > 1 else XW
            z_agg = add("dve", lambda e: e.memset(agg[:, :, :], 0.0), [ready])
            z_one = add("dve", lambda e: e.memset(rows[:, :, :, P:XW], 1.0), [ready])
            z_car = add("dve", lambda e: e.memset(carry[:, :], NEG), [ready])
            begin = [ready, z_agg, z_one, z_car]
            for e_ in prog.ENGINES:
                prog.queue[e_].append(lambda eng, last, w=list(flat(begin)): [eng.wait_ge(x.sem, x.value) for x in w
                                                                            if last.get(id(x.sem), 0) < x.value])
            prog.stage(name + "_loop")
            L = Loop(prog, NG)
            agg_flat = agg[:, :, :].rearrange("p a b -> p (a b)")
            dst_flat = dst_side[:, :, :].rearrange("p a b -> p (a b)")
            rw = R8 if heads > 1 else R1
            rt_ = row_tab8 if heads > 1 else row_tab1
            FC0, BL0 = heads * (G + 1), heads * (2 * G + 1)
            ntab = 3 + heads
            TB, GB = tab_base[0], gat_base[0]
            tab_base[0] += 16 * ntab * (NG // U)
            gat_base[0] += 16 * CH * (NG // U)

            def load_tables(e, u, i):
                e.dma_start(edge_sb[:, u, :], edge_tab[bass.ds(i, 1), :, :].rearrange("o p k -> (o p) k")).then_inc(s_tab[u], 16)
                e.dma_start(oh_rows[0:3, u, :], onehot_tab[:, bass.ds(i * (G * P), G * P)]).then_inc(s_tab[u], 16)
                e.dma_start(row_sb[0:1, u, 0:rw], rt_[bass.ds(i, 1), :]).then_inc(s_tab[u], 16)
                for hd in range(heads):
                    e.dma_start(step_sb[hd * G:(hd + 1) * G, u, :],
                                step_tab[bass.ds(i * G, G), :]).then_inc(s_tab[u], 16)
            tab = L.slot_dma("sp", load_tables, [], s_tab, TB, 16 * ntab)

            def gather(c):
                def fn(e, u, i):
                    for g in range(c * CH, (c + 1) * CH):
                        e.indirect_dma_start(rows[:, u, g, 0:width], None, src_rows,
                                             bass.IndirectOffsetOnAxis(ap=edge_sb[:, u, g:g + 1].bitcast(I32), axis=0)
                                             ).then_inc(s_gat[c][u], 16)
                return L.slot_dma("pool", fn, [(tab, 0)], s_gat[c], GB, 16 * CH)
            gat = [gather(c) for c in range(NCH)]

            _, dst_at = load_offsets(L, "pe", BL0 + G, P, [(tab, 0)], 0)
            _, agg_at = load_offsets(L, "dve", BL0, AW, [(tab, 2)], 2)

            Q, OT, Z, LR, MX, TA, RD = {}, {}, {}, {}, {}, {}, {}

            def a_dist(c):
                def fn(e, u, i):
                    return e.matmul(bank[0][:, :], oh_w[:, :], oh_rows[:, u, c * CH * P:(c + 1) * CH * P],
                                    start=True, stop=True)
                Q[c] = L.op("pe", fn, [(tab, 0), (OT[c - 1], 0) if c else None])

            def a_onehot(c):
                def fn(e, u, i):
                    return e.activation(oh_t[:, c % 2, :], bank[0][:, :], ACT.Relu, bias=1.0, scale=-1.0)
                OT[c] = L.op("act", fn, [(Q[c], 0), (Z[c - 2], 0) if c >= 2 else None])

            def a_sum(c):
                def fn(e, u, i):
                    for k in range(CH):
                        g = c * CH + k
                        oh = oh_t[:, c % 2, k * P:(k + 1) * P]
                        if vector:
                            o = bank[2 + c % 2][:, k * P:(k + 1) * P]
                            e.matmul(o, oh, dst_flat[:, bass.ds(dst_at["v"][g], P)], start=True, stop=False)
                            ins = e.matmul(o, ident[:, :], rows[:, u, g, 0:P], start=False, stop=True)
                        else:
                            ins = e.matmul(bank[2][:, g:g + 1], oh, dst_flat[:, bass.ds(dst_at["v"][g], 1)], start=True, stop=True)
                    return ins
                Z[c] = L.op("pe", fn, [(OT[c], 0)] + ([(gat[c], 0)] if vector else [])
                            + ([(MX[c - 2], 0)] if vector and c >= 2 else []), anchored=True)

            def a_lrelu(c):
                LR[c] = L.op("act", lambda e, u, i: e.mul(lrelu[:, c % 2, :], bank[2 + c % 2][:, :], SLOPE),
                             [(Z[c], 0), (RD[c - 2], 0) if c >= 2 else None])

            def a_max(c):
                MX[c] = L.op("dve", lambda e, u, i: e.tensor_tensor(lrelu[:, c % 2, :], lrelu[:, c % 2, :], bank[2 + c % 2][:, :], ALU.max),
                             [(LR[c], 0)])

            def a_times_att(c):
                x3 = lrelu[:, c % 2, :].rearrange("p (g n) -> p g n", g=CH)
                TA[c] = L.op("dve", lambda e, u, i: e.tensor_tensor(x3, x3, view(att[:, :], [(0, CH), (1, P)]), ALU.mult), [(MX[c], 0)])

            def a_reduce(c):
                RD[c] = L.op("dve", lambda e, u, i: e.tensor_reduce(
                    view(logit[:, c * CH:], [(1, CH), (G, heads)]), view(lrelu[:, c % 2, :], [(P, CH), (hw, heads), (1, hw)]),
                    AX.X, ALU.add), [(TA[c], 0)])

            hg = lambda x: x.rearrange("p (h g) -> p h g", h=heads)
            cv = lambda t, k: t[:, 0:heads * (G + 1)].rearrange("o (h k) -> o h k", h=heads)[:, :, k]
            LT = bank[6][0:RW, 0:P]
            ST_ = bank[6][:, P:P + RW]
            RT = bank[6][:, P:P + RW]
            Y1 = bank[6][0:1, 2 * P:2 * P + RW]
            Y2 = bank[6][0:RW, 3 * P:3 * P + 1]
            B = {}

            def b_logits_to_steps():
                B["tp1"] = L.op("pe", lambda e, u, i: e.transpose(LT, masked[:, (u - 1) % 2, 0:RW], ident[:, :]), [], lag=1, anchored=True)

            def b_sf():
                B["sf"] = L.op("dve", lambda e, u, i: e.tensor_tensor_scan(seg_fwd[0:RW, :], step_sb[0:RW, (u - 1) % U, 0:P], LT,
                                                                          NEG, ALU.add, ALU.max), [(B["tp1"], 0)], lag=1)

            def b_sb():
                B["sb"] = L.op("dve", lambda e, u, i: e.tensor_tensor_scan(
                    view(seg_max[0:RW, P - 1:], [(-1, P)]), view(step_sb[0:RW, (u - 1) % U, P:], [(-1, P)]),
                    view(seg_fwd[0:RW, P - 1:], [(-1, P)]), NEG, ALU.add, ALU.max), [(B["sf"], 0)], lag=1)

            def b_k0():
                B["k0"] = L.op("dve", lambda e, u, i: e.tensor_copy(cv(carry_in, slice(0, 1)), cv(carry, slice(G, G + 1))), [], lag=1)

            def b_k1():
                B["k1"] = L.op("dve", lambda e, u, i: e.tensor_copy(cv(carry_in, slice(1, G + 1)), hg(Y1)), [(B["tp2"], 0)], lag=1)

            def b_k2():
                B["k2"] = L.op("dve", lambda e, u, i: e.tensor_tensor_scan(
                    carry[:, 0:heads * (G + 1)], row_sb[0:1, (u - 1) % U, 0:heads * (G + 1)],
                    carry_in[:, 0:heads * (G + 1)], NEG, ALU.add, ALU.max), [(B["k0"], 0), (B["k1"], 0)], lag=1)
                B["k0"].after.append((B["k2"], 1))

            def b_k3():
                B["k3"] = L.op("dve", lambda e, u, i: e.tensor_tensor(
                    hg(cin_row[:, 0:RW]), cv(carry, slice(0, G)), hg(row_sb[0:1, (u - 1) % U, FC0:FC0 + RW]), ALU.add),
                    [(B["k2"], 0)], lag=1)

            def b_k4():
                B["k4"] = L.op("dve", lambda e, u, i: e.tensor_copy(cin[0:RW, 0:1], Y2), [(B["tp3"], 0)], lag=1)

            def b_rm():
                B["rm"] = L.op("dve", lambda e, u, i: e.scalar_tensor_tensor(
                    run_max[0:RW, :], step_sb[0:RW, (u - 1) % U, P + 1:2 * P + 1], cin[0:RW, 0:1],
                    seg_max[0:RW, :], ALU.add, ALU.max), [(B["k4"], 0)], lag=1)

            def b_dd():
                B["dd"] = L.op("dve", lambda e, u, i: e.tensor_tensor(cin[0:RW, 1:2], cin[0:RW, 0:1], run_max[0:RW, 0:1], ALU.subtract),
                               [(B["rm"], 0)], lag=1)

            def b_df():
                B["df"] = L.op("dve", lambda e, u, i: e.tensor_tensor(shifted[:, 0:RW], masked[:, (u - 1) % 2, 0:RW], RT, ALU.subtract),
                               [(B["tp4"], 0)], lag=1)

            def b_cm():
                B["cm"] = L.op("dve", lambda e, u, i: e.tensor_scalar(cin[0:RW, 3:4], cin[0:RW, 2:3], -1.0, None, ALU.add), [(B["ce"], 0)], lag=1)

            def b_dm():
                B["dm"] = L.op("dve", lambda e, u, i: e.tensor_scalar(
                    decay_m[0:RW, :], iota[0:RW, :], step_sb[0:RW, (u - 1) % U, 2 * P + 1:2 * P + 2],
                    cin[0:RW, 3:4], ALU.is_equal, ALU.mult), [(B["cm"], 0)], lag=1)

            def b_last_to_row():
                B["tp2"] = L.op("pe", lambda e, u, i: e.transpose(Y1, seg_max[0:RW, P - 1:P], ident[0:RW, 0:RW]), [(B["sb"], 0)],
                                lag=1, anchored=True)

            def b_carry_to_steps():
                B["tp3"] = L.op("pe", lambda e, u, i: e.transpose(Y2, cin_row[:, 0:RW], ident[0:1, 0:1]), [(B["k3"], 0)], lag=1, anchored=True)

            def b_maxima_to_edges():
                B["tp4"] = L.op("pe", lambda e, u, i: e.transpose(RT, run_max[0:RW, :], ident[0:RW, 0:RW]), [(B["rm"], 0)], lag=1, anchored=True)

            def b_factors_to_nodes():
                B["tp5"] = L.op("pe", lambda e, u, i: e.transpose(ST_, decay_m[0:RW, :], ident[0:RW, 0:RW]), [], lag=2, anchored=True)

            def b_decay():
                B["ce"] = L.op("act", lambda e, u, i: e.activation(cin[0:RW, 2:3], cin[0:RW, 1:2], ACT.Exp), [(B["dd"], 0)], lag=1)

            def b_exp():
                B["wt"] = L.op("act", lambda e, u, i: e.activation(weight[:, (u - 2) % 2, 0:RW], shifted[:, 0:RW], ACT.Exp), [], lag=2)
                B["nw"] = L.op("act", lambda e, u, i: e.mul(minus_w[:, (u - 2) % 2, :], weight[:, (u - 2) % 2, 0:G], -1.0),
                               [(B["wt"], 0)], lag=2)

            def b_sl():
                B["sl"] = L.op("dve", lambda e, u, i: e.tensor_scalar(rescale[:, (u - 2) % 2, 0:RW], ST_, 1.0, None, ALU.add),
                               [(B["tp5"], 0)], lag=2)

            def sum_bank(g):
                return bank[(1, 4, 5)[g // 2 % 3]]

            WD, W, XS, AG, AC, AC1 = {}, {}, {}, {}, {}, {}

            def c_dist(c):
                lag = 1 if c == 0 else 2

                def fn(e, u, i):
                    for k in range(CH):
                        g = c * CH + k
                        ins = e.matmul(bank[7][:, k * P:(k + 1) * P], oh_rows[:, (u - lag) % U, g * P:(g + 1) * P], oh_w[:, :],
                                       start=True, stop=True)
                    return ins
                WD[c] = L.op("pe", fn, [(W[(c * CH - 1) % G], 0)], lag=lag, anchored=True)

            def c_weight(c):
                for g in range(c * CH, (c + 1) * CH):
                    ready_q = [(WD[c], 0)] if c else []
                    aft = ready_q + ([(AG[g - 8], 0)] if g >= 8 else [])
                    q = bank[7][:, (g % CH) * P:(g % CH + 1) * P]
                    if heads > 1:
                        if g % CH == 0:
                            o = L.op("act", lambda e, u, i, g=g: e.activation(
                                oh_e[:, g % 8:g % 8 + CH, :].rearrange("p s n -> p (s n)"), bank[7][:, :], ACT.Relu, bias=1.0, scale=-1.0),
                                ready_q + ([(AG[g - 8 + CH - 1], 0)] if g >= 8 else []), lag=2)
                    else:
                        o = L.op("act", lambda e, u, i, g=g, q=q: e.activation(
                            oh_e[:, g % 8, :], q, ACT.Relu, bias=weight[:, (u - 2) % 2, g:g + 1], scale=minus_w[:, (u - 2) % 2, g:g + 1]),
                            aft, lag=2)
                    W[g] = o

            def c_scaled_rows(c):
                def fn(e, u, i):
                    v = (u - 2) % U
                    o = view(xw[:, c % 2, :], [(AW, CH), (hw + 1, heads), (1, hw)])
                    x = view(rows[:, v, c * CH:(c + 1) * CH, :], [(XW, CH), (hw, heads), (1, hw)])
                    w = view(weight[:, v % 2, c * CH:(c + 1) * CH], [(1, CH), (G, heads), (0, hw)])
                    return e.tensor_tensor(o, x, w, ALU.mult)

                def fn2(e, u, i):
                    o = view(xw[:, c % 2, hw:], [(AW, CH), (hw + 1, heads)])
                    return e.copy(o, view(weight[:, (u - 2) % 2, c * CH:(c + 1) * CH], [(1, CH), (G, heads)]))
                aft = [(AG[(c - 2) * CH + CH - 1], 0)] if c >= 2 else []
                XS[c] = [L.op("dve", fn, aft, lag=2), L.op("act", fn2, aft, lag=2)]

            def c_agg(g):
                def fn(e, u, i):
                    o = sum_bank(g)[:, (g % 2) * AW:(g % 2) * AW + aw]
                    r = xw[:, (g // CH) % 2, (g % CH) * AW:(g % CH) * AW + AW] if heads > 1 else rows[:, (u - 2) % U, g, 0:XW]
                    return e.matmul(o, oh_e[:, g % 8, :], r, start=True, stop=True)
                aft = [(W[g], 0)] + ([(o, 0) for o in XS[g // CH]] if heads > 1 else [])
                AG[g] = L.op("pe", fn, aft + ([(AC[g - g % 2 - 5], 0)] if g >= 6 else []), lag=2)

            def c_acc(g, second=False):
                s = sum_bank(g)[:, (g % 2) * AW:(g % 2) * AW + aw]

                def fn(e, u, i):
                    at = agg_flat[:, bass.ds(agg_at["v"][g], aw)]
                    return e.scalar_tensor_tensor(at, at, rescale[:, (u - 2) % 2, g:g + 1], s, ALU.mult, ALU.add)

                def fn_a(e, u, i):
                    at = agg_flat[:, bass.ds(agg_at["v"][g], aw)].rearrange("p (h d) -> p h d", h=heads)
                    f = view(rescale[:, (u - 2) % 2, g:], [(G, heads), (0, hw + 1)])
                    return e.tensor_tensor(acc_tmp[:, g % 2, :].rearrange("p (h d) -> p h d", h=heads), at, f, ALU.mult)

                def fn_b(e, u, i):
                    return e.tensor_tensor(agg_flat[:, bass.ds(agg_at["v"][g], aw)], acc_tmp[:, g % 2, :], s, ALU.add)
                before = [(AC[g - 1], 0)] if g else []
                both = [(AG[g - g % 2 + 1], 0)]
                if heads == 1:
                    AC1[g] = AC[g] = L.op("dve", fn, before + both, lag=2)
                elif not second:
                    AC1[g] = L.op("dve", fn_a, before, lag=2)
                else:
                    AC[g] = L.op("dve", fn_b, [(AC1[g], 0)] + both, lag=2)

            def aggregate(c):
                for g in range(c * CH, (c + 1) * CH):
                    c_agg(g)

            def dve_part(c, order):
                half = None
                for name in order.split():
                    if name[0] == "A":
                        g = c * CH + int(name[1])
                        if half is not None:
                            c_acc(half, True)
                        c_acc(g)
                        half = g if heads > 1 else None
                        continue
                    if name in ("max", "att", "red"):
                        if vector:
                            {"max": a_max, "att": a_times_att, "red": a_reduce}[name](c)
                    else:
                        maxima_ops[name]()
                    if half is not None:
                        c_acc(half, True)
                        half = None
                if half is not None:
                    c_acc(half, True)
            maxima_ops = dict(sf=b_sf, sb=b_sb, k0=b_k0, k1=b_k1, k2=b_k2, k3=b_k3, k4=b_k4, rm=b_rm, dd=b_dd, df=b_df,
                              cm=b_cm, dm=b_dm, sl=b_sl)

            a_dist(0)
            a_onehot(0)
            b_exp()
            c_weight(0)
            for c in range(NCH):
                if heads > 1:
                    c_scaled_rows(c)
                if c:
                    c_weight(c)
                if c + 1 < NCH:
                    a_dist(c + 1)
                    a_onehot(c + 1)
                a_sum(c)
                if vector:
                    a_lrelu(c)
                if c == 1:
                    dve_part(0, "max sl A0 sf A1 att sb A2 red A3")
                if c == 2:
                    dve_part(1, "k0 A0 max k1 A1 k2 att k3 A2 red A3")
                if c == 3:
                    dve_part(2, "A0 max k4 A1 rm att dd A2 red A3")
                aggregate(c)
                (b_logits_to_steps, b_last_to_row, b_carry_to_steps, b_maxima_to_edges)[c]()
                if c == 0:
                    b_factors_to_nodes()
                c_dist((c + 1) % NCH)
            b_decay()
            dve_part(NCH - 1, "df A0 max cm A1 dm att A2 red A3")
            if not vector:
                sc = L.op("dve", lambda e, u, i: e.tensor_tensor(logit[:, 0:G], bank[2][:, 0:G],
                                                                rows[:, u, :, P:P + 1].rearrange("p g o -> p (g o)"), ALU.add),
                          [(Z[NCH - 1], 0)] + [(x, 0) for x in gat])
                Z[0].after.append((sc, 1))
                lg = L.op("dve", lambda e, u, i: e.scalar_tensor_tensor(logit[:, 0:G], logit[:, 0:G], SLOPE, logit[:, 0:G],
                                                                       ALU.mult, ALU.max), [(sc, 0)])
            else:
                lg = RD[NCH - 1]
            mk = L.op("dve", lambda e, u, i: e.tensor_tensor(
                hg(masked[:, u % 2, 0:RW]), hg(logit[:, 0:RW]), view(edge_sb[:, u, 2 * G:], [(0, heads), (1, G)]), ALU.add), [(lg, 0)])

            B["tp1"].after.append((mk, 1))
            for o in ([W[g] for g in range(CH)] if heads == 1 else XS[0]):
                o.after.append((B["nw"] if heads == 1 else B["wt"], 0))
            for g in range(CH):
                W[g].after.append((WD[0], 1))
            AC1[0].after += [(B["sl"], 0), (AC[G - 1], 1)]
            B["tp5"].after.append((B["dm"], 1))
            for c in (0, 1):
                OT[c].after.append((Z[c + 2], 1))
                if vector:
                    Z[c].after.append((MX[c + 2], 1))
                    LR[c].after.append((RD[c + 2], 1))
            Q[0].after.append((OT[NCH - 1], 1))
            B["wt"].after += [(B["df"], 1), (W[G - 1], 1)]
            B["df"].after.append((B["wt"], 0))
            for g in range(8):
                if heads == 1 or g % CH == 0:
                    W[g].after.append((AG[g + 8 if heads == 1 else g + 8 + CH - 1], 1))
            for g in range(6):
                same_bank = [p for p in range(G // 2) if sum_bank(2 * p) is sum_bank(g)]
                AG[g].after.append((AC[2 * same_bank[-1] + 1], 1))
            if heads > 1:
                for c in (0, 1):
                    for o in XS[c]:
                        o.after.append((AG[(c + 2) * CH + CH - 1], 1))
                B["wt"].after += [(o, 1) for o in XS[NCH - 1]]
            for c in range(NCH):
                gat[c].after.append((AG[(c + 1) * CH - 1], U - 2))
            tab.after += [(AC[G - 1], U - 2), (tab, U)]
            L.close()
            return [L.last(AC[G - 1])]

        s_sc = [prog.sem(f"scatter_into_sum{k}") for k in range(NSUM)]

        def source_pass(name, ready):
            prog.stage(name)
            big = dst_side[:, :, :].rearrange("p a b -> p (a b)")
            at = 0

            def part(n, dt=F32):
                nonlocal at
                at += n
                v = big[:, at - n:at]
                return v if dt == F32 else v.bitcast(dt)
            src_rows = part(U * G * P // 2, BF16).rearrange("p (u n) -> p u n", u=U)
            summed = part(8 * XW).rearrange("p (s n) -> p s n", s=8)
            oh_s = part(CH * P)
            same = part(8 * P).rearrange("p (s n) -> p s n", s=8)
            scratch = part(2 * CH * P).rearrange("p (s n) -> p s n", s=2 * CH)
            look = part(G)
            dup = part(G)
            target_f = part(G)
            target = part(U * G, I32).rearrange("p (u n) -> p u n", u=U)
            z = add("dve", lambda e: e.memset(src_rows[0:6, :, :], 1.0), [ready])
            for e_ in prog.ENGINES:
                prog.queue[e_].append(lambda eng, last, w=list(flat([ready, z])): [eng.wait_ge(x.sem, x.value) for x in w
                                                                                 if last.get(id(x.sem), 0) < x.value])
            prog.stage(name + "_loop")
            L = Loop(prog, NG)
            agg_flat = agg[:, :, :].rearrange("p a b -> p (a b)")
            BL0 = 2 * G + 1
            ntab = 4
            TB = tab_base[0]
            tab_base[0] += 16 * ntab * (NG // U)

            def load_tables(e, u, i):
                e.dma_start(edge_sb[:, u, :], edge_tab[bass.ds(i, 1), :, :].rearrange("o p k -> (o p) k")).then_inc(s_tab[u], 16)
                e.dma_start(oh_rows[0:3, u, :], onehot_tab[:, bass.ds(i * (G * P), G * P)]).then_inc(s_tab[u], 16)
                e.dma_start(src_rows[0:4, u, :], source_tab[:, bass.ds(i * (G * P), G * P)]).then_inc(s_tab[u], 16)
                e.dma_start(row_sb[0:1, u, 0:R1], row_tab1[bass.ds(i, 1), :]).then_inc(s_tab[u], 16)
            tab = L.slot_dma("sp", load_tables, [], s_tab, TB, 16 * ntab)

            ld, offs = load_offsets(L, "pe", BL0, AW, [(tab, 0)], 0)

            def scatters_before(g, i, lag):
                return (i - lag) * (16 * G // NSUM) + 16 * (g // NSUM)

            D, OT, XD, EV, DS, OS, LK, SEL, BA, DU = {}, {}, {}, {}, {}, {}, {}, {}, {}, {}
            BC, SM, AG, RV = {}, {}, {}, {}
            for c in range(NCH):
                BC[c] = L.op("pe", lambda e, u, i, c=c: e.matmul(bank[2][:, :], oh_ws[:, P:2 * P],
                                                                 src_rows[0:6, (u - 1) % U, c * CH * P:(c + 1) * CH * P],
                                                                 start=True, stop=True),
                             [(SM[c * CH - 1], 0)] if c else [], lag=1)
                for g in range(c * CH, (c + 1) * CH):
                    SM[g] = L.op("dve", lambda e, u, i, g=g: e.tensor_scalar(
                        same[:, g % 8, :], bank[2][:, (g % CH) * P:(g % CH + 1) * P],
                        edge_sb[:, (u - 1) % U, 3 * G + g:3 * G + g + 1], weight[:, (u - 1) % 2, g:g + 1],
                        ALU.is_equal, ALU.mult), [(BC[c], 0)] + ([(AG[g - 8], 0)] if g >= 8 else []), lag=1)
                D[c] = L.op("pe", lambda e, u, i, c=c: e.matmul(bank[0][:, :], oh_w[:, :], oh_rows[:, u, c * CH * P:(c + 1) * CH * P],
                                                                start=True, stop=True), [(tab, 0)] + ([(OT[c - 1], 0)] if c else []))
                OT[c] = L.op("act", lambda e, u, i, c=c: e.activation(oh_t[:, c % 2, :], bank[0][:, :], ACT.Relu, bias=1.0, scale=-1.0),
                             [(D[c], 0)] + ([(XD[(c - 2) * 2 + 1], 0)] if c >= 2 else []))
                DS[c] = L.op("pe", lambda e, u, i, c=c: e.matmul(bank[1][:, :], oh_ws[:, 0:P], src_rows[0:6, u, c * CH * P:(c + 1) * CH * P],
                                                                 start=True, stop=True), [(tab, 0)] + ([(DU[c * CH - 1], 0)] if c else []))
                OS[c] = L.op("act", lambda e, u, i, c=c: e.activation(oh_s, bank[1][:, :], ACT.Relu, bias=1.0, scale=-1.0),
                             [(DS[c], 0)] + ([(LK[c - 1], 0)] if c else []))
                for g in range(c * CH, (c + 1) * CH):
                    if g % 2 == 0:
                        continue
                    h = g // 2
                    for gg in (g - 1, g):
                        AG[gg] = L.op("pe", lambda e, u, i, g=gg: e.matmul(
                            bank[6 + g // 2 % 2][:, (g % 2) * XW:(g % 2 + 1) * XW], same[:, g % 8, :], rows[:, (u - 1) % U, g, :],
                            start=True, stop=True), [(SM[gg], 0)] + ([(RV[h - 2], 0)] if h >= 2 else []), lag=1)

                    def evac(e, u, i, g=g - 1):
                        for gg in (g, g + 1):
                            if isinstance(i, int):
                                n = scatters_before(gg, i, 1) - 16
                                if n > 0:
                                    e.wait_ge(s_sc[gg % NSUM], n)
                            else:
                                e.wait_ge(s_sc[gg % NSUM], i * (16 * G // NSUM) + (16 * (gg // NSUM) - 16 * G // NSUM - 16))
                        return e.copy(summed[:, g % 8:g % 8 + 2, :].rearrange("p s n -> p (s n)"), bank[6 + g // 2 % 2][:, 0:2 * XW])
                    RV[h] = L.op("act", evac, [(AG[g], 0)], lag=1)

                    def scatter(e, u, i, g=g - 1):
                        for gg in (g, g + 1):
                            k = gg % NSUM
                            if isinstance(i, int):
                                n = scatters_before(gg, i, 1)
                                if n > 0:
                                    e.wait_ge(s_sc[k], n)
                            else:
                                e.wait_ge(s_sc[k], i * (16 * G // NSUM) + (16 * (gg // NSUM) - 16 * G // NSUM))
                                e.sem_inc(prog.anchor, 1)
                            e.indirect_dma_start(scatter_s[k], bass.IndirectOffsetOnAxis(ap=target[:, (u - 1) % U, gg:gg + 1], axis=0),
                                                 summed[:, gg % 8, :], None, compute_op=ALU.add).then_inc(s_sc[k], 16)
                    L.op("pool", scatter, [(RV[h], 0)], lag=1, anchored=True)

                def lookup(e, u, i, c=c):
                    for k in range(CH):
                        ins = e.matmul(bank[5][:, k * P:k * P + NB], oh_s[:, k * P:(k + 1) * P], dst_score[:, :], start=True, stop=True)
                    return ins
                LK[c] = L.op("pe", lookup, [(OS[c], 0)] + ([(SEL[c * CH - 1], 0)] if c else []))
                BA[c] = L.op("pe", lambda e, u, i, c=c: e.matmul(bank[1][:, :], oh_ws[:, P:2 * P], src_rows[0:6, u, c * CH * P:(c + 1) * CH * P],
                                                                 start=True, stop=True), [(OS[c], 0)])
                for h in (2 * c, 2 * c + 1):
                    def expand(e, u, i, h=h):
                        for k in (0, 1):
                            g = 2 * h + k
                            ins = e.matmul(bank[3 + h % 2][:, k * XW:(k + 1) * XW], oh_t[:, (g // CH) % 2, (g % CH) * P:(g % CH + 1) * P],
                                           agg_flat[:, bass.ds(offs["v"][g], XW)], start=True, stop=True)
                        return ins
                    XD[h] = L.op("pe", expand, [(OT[c], 0)] + ([(EV[h - 2], 0)] if h >= 2 else []), anchored=True)
                    EV[h] = L.op("act", lambda e, u, i, h=h: e.copy(rows[:, u, 2 * h:2 * h + 2, :].rearrange("p s n -> p (s n)"),
                                                                    bank[3 + h % 2][:, 0:2 * XW]), [(XD[h], 0)])
                for g in range(c * CH, (c + 1) * CH):
                    SEL[g] = L.op("dve", lambda e, u, i, g=g: e.scalar_tensor_tensor(
                        scratch[:, g % CH, 0:NB], iota[:, 0:NB], edge_sb[:, u, 4 * G + g:4 * G + g + 1], bank[5][:, (g % CH) * P:(g % CH) * P + NB],
                        ALU.is_equal, ALU.mult, accum_out=look[:, g:g + 1]), [(LK[c], 0)] + ([(SEL[g - CH], 0)] if g >= CH else []))
                for g in range(c * CH, (c + 1) * CH):
                    DU[g] = L.op("dve", lambda e, u, i, g=g: e.scalar_tensor_tensor(
                        scratch[:, CH + g % CH, :], bank[1][:, (g % CH) * P:(g % CH + 1) * P], edge_sb[:, u, 3 * G + g:3 * G + g + 1], att[:, :],
                        ALU.is_equal, ALU.mult, accum_out=dup[:, g:g + 1]), [(BA[c], 0)] + ([(DU[g - CH], 0)] if g >= CH else []))
            a1 = L.op("dve", lambda e, u, i: e.tensor_tensor(logit[:, 0:G], look[:, :], rows[:, u, :, P:P + 1].rearrange("p g o -> p (g o)"),
                                                             ALU.add), [(SEL[G - 1], 0), (EV[G // 2 - 1], 0)])
            a2 = L.op("dve", lambda e, u, i: e.scalar_tensor_tensor(logit[:, 0:G], logit[:, 0:G], SLOPE, logit[:, 0:G], ALU.mult, ALU.max), [(a1, 0)])
            a3_ = L.op("dve", lambda e, u, i: e.tensor_tensor(logit[:, 0:G], logit[:, 0:G], edge_sb[:, u, 2 * G:3 * G], ALU.add), [(a2, 0)])
            wt = L.op("act", lambda e, u, i: e.activation(weight[:, u % 2, 0:G], logit[:, 0:G], ACT.Exp), [(a3_, 0), (SM[G - 1], 1)])
            t1 = L.op("dve", lambda e, u, i: e.tensor_scalar(dup[:, :], dup[:, :], 0.0, None, ALU.is_gt), [(DU[G - 1], 0)])
            t2 = L.op("dve", lambda e, u, i: e.tensor_scalar(target_f[:, :], edge_sb[:, u, 3 * G:4 * G], dump_row[:, 0:1], -1.0,
                                                             ALU.subtract, ALU.mult), [(t1, 0)])
            t3 = L.op("dve", lambda e, u, i: e.tensor_tensor(target_f[:, :], target_f[:, :], dup[:, :], ALU.mult), [(t2, 0)])
            t4 = L.op("dve", lambda e, u, i: e.tensor_tensor(target_f[:, :], target_f[:, :], edge_sb[:, u, 3 * G:4 * G], ALU.add), [(t3, 0)])

            def store_target(e, u, i):
                for k in range(NSUM):
                    if isinstance(i, int):
                        if i >= U:
                            e.wait_ge(s_sc[k], (16 * G // NSUM) * (i - U + 1))
                    else:
                        e.wait_ge(s_sc[k], i * (16 * G // NSUM) - (16 * G // NSUM) * (U - 1))
                return e.tensor_copy(target[:, u, :], target_f[:, :])
            t5 = L.op("dve", store_target, [(t4, 0)])
            BC[0].after.append((SM[G - 1], 1))
            SM[0].after += [(wt, 1), (AG[8], 1)]
            for g in range(1, 8):
                SM[g].after.append((AG[g + 8], 1))
            D[0].after.append((OT[NCH - 1], 1))
            OT[0].after.append((XD[5], 1))
            OT[1].after.append((XD[7], 1))
            DS[0].after.append((DU[G - 1], 1))
            OS[0].after.append((LK[NCH - 1], 1))
            LK[0].after.append((SEL[G - 1], 1))
            for g in (0, 1):
                AG[g].after.append((RV[6], 1))
            for g in (2, 3):
                AG[g].after.append((RV[7], 1))
            XD[0].after.append((EV[6], 1))
            XD[1].after.append((EV[7], 1))
            EV[0].after.append((AG[G - 1], 3))
            RV[0].after.append((t5, 1))
            SEL[0].after += [(a1, 1), (SEL[G - 1], 1)]
            DU[0].after += [(DU[G - 1], 1), (t3, 1)]
            a1.after.append((wt, 1))
            tab.after += [(AG[G - 1], 3), (SM[G - 1], 3), (t4, 4), (tab, 4)]
            L.close()
            return [L.last(AG[G - 1]), L.last(SM[G - 1])] + [Done(s_sc[k], 16 * (G // NSUM) * NG) for k in range(NSUM)]

        node_tile = lambda n: pool_rows[:, n * NBB * P:(n + 1) * NBB * P]
        tile3 = lambda n: node_tile(n).rearrange("p (b f) -> p b f", b=NBB)
        flat3 = lambda x: x[:, :, :].rearrange("p a b -> p (a b)")
        hT = [sb("hT", [P, NBB * P]), flat3(oh_t)[:, 0:NBB * P]]

        def overlapped(batches):
            now = batches[0]
            next(now)
            next(now)
            for following in batches[1:] + [None]:
                if following:
                    next(following)
                next(now, None)
                if following:
                    next(following)
                next(now, None)
                now = following

        NBT = NB // NBB
        wcol = lambda n, k=1: param[:, n * P:(n + k) * P]

        def row_bcast(x, off=0, n=P):
            return bass.AP(x.tensor, x.offset + off, [(0, P), (1, n)])

        def load_rows(pairs, after):
            return [dma("sp", lambda e, s=s, src=src: e.dma_start(s, src), after) for s, src in pairs]

        def blocks(ap2d, t):
            return ap2d[t * NBB * P:(t + 1) * NBB * P, :].rearrange("(b p) f -> p b f", p=P)

        def transposed(src3, bank0, ready, free, dst):
            outs = []
            for q, (lo, hi) in enumerate(((0, 4), (4, NBB))):
                for k in range(lo, hi):
                    tp = add("pe", lambda e, k=k, q=q, lo=lo: e.transpose(bank[bank0 + q][:, (k - lo) * P:(k - lo + 1) * P],
                                                                          src3[:, k, :], ident[:, :]), [ready, free])
                outs.append(add("act", lambda e, q=q, lo=lo, hi=hi: e.copy(dst[:, lo * P:hi * P], bank[bank0 + q][:, 0:(hi - lo) * P]),
                                [tp, free]))
            return outs

        def layer_norm(x3, ready):
            hs = [add("dve", lambda e, k=k: e.bn_stats(stats[:, k, :], x3[:, k, :]), [ready]) for k in range(NBB)]
            hs = [add("dve", lambda e, k=k: e.bn_aggr(moments[:, k, :], stats[:, k, :]), [hs[k]]) for k in range(NBB)]
            h = add("dve", lambda e: e.tensor_scalar(rstd[:, 0, :], moments[:, :, 1], LN_EPS, None, ALU.add), [hs])
            h = add("pool", lambda e: e.tensor_tensor(rstd[:, 1, :], rstd[:, 0, :], minus_half[:, :], ALU.pow), [h, m_half])
            return [add("dve", lambda e, k=k: e.tensor_scalar(x3[:, k, :], x3[:, k, :], moments[:, k, 0:1], rstd[:, 1, k:k + 1],
                                                            ALU.subtract, ALU.mult), [h]) for k in range(NBB)]

        def bias3(n):
            return view(wcol(n), [(0, NBB), (1, P)])

        def project(t, w2, evac, ready, free_ps, hT_):
            outs = []
            for q in range((NBB + 1) // 2):
                ks = [k for k in (2 * q, 2 * q + 1) if k < NBB]
                for k in ks:
                    mm = add("pe", lambda e, k=k, q=q: e.matmul(bank[4 + q][:, (k % 2) * 2 * P:(k % 2 + 1) * 2 * P],
                                                                hT_[:, k * P:(k + 1) * P], wcol(w2, 2), start=True, stop=True),
                             [ready, free_ps[q] if free_ps else []])
                outs.append(evac(q, ks, mm))
            return outs

        def two_sided(t, w2, b_src, b_dst, ready, free_ps, stage3, stage_free, table, hT_):
            def evac(q, ks, mm):
                n = len(ks)
                src = bank[4 + q][:, 0:n * 2 * P].rearrange("p (k s f) -> p k s f", k=n, s=2)
                def fn(e):
                    o = stage3[:, ks[0]:ks[0] + n, :]
                    if b_src is None:
                        return e.tensor_copy(o, src[:, :, 0, :])
                    return e.tensor_tensor(o, src[:, :, 0, :], view(wcol(b_src), [(0, n), (1, P)]), ALU.add)
                def fn2(e):
                    o = dst_side[:, t * NBB + ks[0]:t * NBB + ks[0] + n, :]
                    if b_dst is None:
                        return e.tensor_copy(o, src[:, :, 1, :])
                    return e.tensor_tensor(o, src[:, :, 1, :], view(wcol(b_dst), [(0, n), (1, P)]), ALU.add)
                return [add("dve", fn, [mm, stage_free]), add("dve", fn2, [mm])]
            outs = project(t, w2, evac, ready, free_ps, hT_)
            st = dma("sp", lambda e: e.dma_start(blocks(table, t), stage3), [outs])
            return outs, st

        def load_x(t, dst3, src, after):
            lo, hi = t * NBB * P, (t + 1) * NBB * P
            if src.shape[0] == NB * P or hi <= N:
                return [dma("sp", lambda e: e.dma_start(dst3, src[lo:hi, :].rearrange("(b p) f -> p b f", p=P)), after)]
            zero = add("dve", lambda e: e.memset(dst3, 0.0), after)
            full = (N - lo) // P
            rem = N - lo - full * P
            hs = []
            if full:
                hs.append(dma("sp", lambda e: e.dma_start(dst3[:, 0:full, :], src[lo:lo + full * P, :].rearrange("(b p) f -> p b f", p=P)), [zero]))
            if rem:
                hs.append(dma("sp", lambda e: e.dma_start(dst3[0:rem, full, :], src[lo + full * P:N, :]), [zero]))
            return hs

        prog.stage("dense0")
        prm = load_rows([(wcol(0), a["L0_gnn_Wl1"]), (wcol(1), a["L0_gnn_Wr1"]), (wcol(2), row_bcast(a["L0_gnn_bl1"])),
                         (wcol(3), row_bcast(a["L0_gnn_br1"])), (att[:, :], row_bcast(a["L0_gnn_att1"]))], [idle])
        x_free, ht_free, ps_free, st_free = [[], []], [[], []], [[]] * 4, [[], []]
        tail = []

        def batch(t):
            x3 = tile3(t % 2)
            ld = load_x(t, x3, a["x"], [idle, x_free[t % 2]])
            yield
            tt = transposed(x3, 2 * (t % 2), [ld, prm], ht_free[t % 2], hT[t % 2])
            yield
            yield
            ev, st = two_sided(t, 0, 2, 3, [tt, prm], ps_free, tile3(2 + t % 2), [st_free[t % 2], idle], gather_a, hT[t % 2])
            x_free[t % 2], ht_free[t % 2], ps_free[:], st_free[t % 2] = tt, ev, ev, [st]
            tail.extend([st, ev])
        overlapped([batch(t) for t in range(NBT)])
        p0 = edge_pass("L0a", gather_a, 1, True, [tail, tables])

        def normalise(t, heads, eps, ready, guard=None):
            a3 = agg[:, t * NBB:(t + 1) * NBB, :]
            hw = P // heads
            if heads == 1:
                den = a3[:, :, P + 1]
                r = recip[:, 0:NBB]
                rb = view(recip[:, :], [(1, NBB), (0, P)])
                h = add("dve", lambda e: (e.tensor_scalar(r, den, eps, None, ALU.add) if guard is None else
                                          e.tensor_scalar(r, den, guard, None, ALU.max)), [ready])
                h = add("dve", lambda e: e.reciprocal(r, r), [h])
                return add("dve", lambda e: e.tensor_tensor(a3[:, :, 0:P], a3[:, :, 0:P], rb, ALU.mult), [h])
            den = view(agg[:, t * NBB, hw:], [(AW, NBB), (hw + 1, heads)])
            r = recip[:, :].rearrange("p (b h) -> p b h", b=NBB)
            h = add("dve", lambda e: e.tensor_scalar(r, den, eps, None, ALU.add), [ready])
            h = add("dve", lambda e: e.reciprocal(recip[:, :], recip[:, :]), [h])
            return h

        def bias_add(o3, i3, n, after):
            return add("dve", lambda e: e.tensor_tensor(o3, i3, bias3(n), ALU.add), after)

        prog.stage("dense1")
        prm = load_rows([(wcol(0), a["L0_gnn_Wl2"]), (wcol(1), a["L0_gnn_Wr2"]), (wcol(2), row_bcast(a["L0_gnn_bl2"])),
                         (wcol(3), row_bcast(a["L0_gnn_br2"])), (wcol(4), row_bcast(a["L0_gnn_bias1"])),
                         (att[:, :], row_bcast(a["L0_gnn_att2"]))], [p0])
        ht_free, ps_free, st_free, recip_free = [[], []], [[]] * 4, [[], []], [None]
        tail = []

        def batch(t):
            a3 = agg[:, t * NBB:(t + 1) * NBB, 0:P]
            h = normalise(t, 1, 1e-16, [p0, recip_free])
            recip_free[0] = h
            h = bias_add(a3, a3, 4, [h, prm])
            h = add("act", lambda e, a3=a3: e.activation(a3, a3, ACT.Relu), [h])
            yield
            tt = transposed(a3, 2 * (t % 2), [h, prm], ht_free[t % 2], hT[t % 2])
            yield
            yield
            ev, st = two_sided(t, 0, 2, 3, [tt, prm], ps_free, tile3(2 + t % 2), [st_free[t % 2], p0], gather_b, hT[t % 2])
            ht_free[t % 2], ps_free[:], st_free[t % 2] = ev, ev, [st]
            tail.extend([st, ev])
        overlapped([batch(t) for t in range(NBT)])
        p1 = edge_pass("L0b", gather_b, 1, True, [tail])

        prog.stage("dense2")
        wsb, a12, vsb, wb = wcol(0), wcol(1)[:, 0:2], wcol(1)[:, 4:6], wcol(1)[:, 8:9]
        s12, cvec, abias = wcol(1)[:, 9:10], wcol(1)[:, 10:11], wcol(1)[:, 11:12]
        one_col = lambda x, off=0: bass.AP(x.tensor, x.offset + off, [(1, P), (1, 1)])
        prm = load_rows([(wsb, a["L1_gnn_w_weight"]), (a12[:, 0:1], one_col(a["L1_gnn_a_weight"])),
                         (a12[:, 1:2], one_col(a["L1_gnn_a_weight"], P)), (wb, one_col(a["L1_gnn_w_bias"])),
                         (abias, bass.AP(a["L1_gnn_a_bias"].tensor, 0, [(0, P), (1, 1)])),
                         (wcol(2), row_bcast(a["L0_gnn_bias2"]))], [p1])
        mm = add("pe", lambda e: e.matmul(bank[0][:, 0:2], wsb, a12, start=True, stop=True), [prm])
        v12 = add("dve", lambda e: e.tensor_copy(vsb, bank[0][:, 0:2]), [mm])
        h = add("dve", lambda e: e.tensor_tensor(s12, a12[:, 0:1], a12[:, 1:2], ALU.add), [prm])
        h = add("dve", lambda e: e.tensor_tensor(s12, s12, wb, ALU.mult), [h])
        mm = add("pe", lambda e: e.matmul(bank[1][:, 0:1], ones[:, :], s12, start=True, stop=True), [h])
        v12 = [v12, add("dve", lambda e: e.tensor_tensor(cvec, bank[1][:, 0:1], abias, ALU.add), [mm, prm])]
        x_free, ht_free, sc_free = [[], []], [[], []], [None]
        tail, recip_free, ln_free = [], [None], [None]

        def batch(t):
            a3 = agg[:, t * NBB:(t + 1) * NBB, 0:P]
            x3 = tile3(t % 2)
            ld = load_x(t, x3, a["x"], [p1, x_free[t % 2]])
            h = normalise(t, 1, 1e-16, [p1, recip_free])
            recip_free[0] = h
            h = bias_add(a3, a3, 2, [h, prm])
            h = add("dve", lambda e, a3=a3, x3=x3: e.tensor_tensor(a3, a3, x3, ALU.add), [h, ld])
            x_free[t % 2] = h
            ln = layer_norm(a3, [h, ln_free])
            ln_free[0] = ln
            yield
            yield
            yield
            tt = transposed(a3, 2 * (t % 2), [ln, v12], ht_free[t % 2], hT[t % 2])
            for k in range(NBB):
                mm = add("pe", lambda e, k=k: e.matmul(bank[4][:, 2 * k:2 * k + 2], hT[t % 2][:, k * P:(k + 1) * P], vsb,
                                                       start=True, stop=True), [tt, sc_free])
            ht_free[t % 2] = mm
            ps = bank[4][:, 0:2 * NBB].rearrange("p (k s) -> p k s", s=2)
            s1 = add("dve", lambda e, t=t, ps=ps: e.tensor_scalar(dst_score[:, t * NBB:(t + 1) * NBB], ps[:, :, 0], cvec, None, ALU.add), [mm])
            s2 = add("dve", lambda e, t=t, ps=ps: e.tensor_copy(agg[:, t * NBB:(t + 1) * NBB, P], ps[:, :, 1]), [mm])
            sc_free[0] = [s1, s2]
            s3 = add("dve", lambda e, t=t: e.memset(agg[:, t * NBB:(t + 1) * NBB, P + 1:P + 2], 1.0), [h])
            tail.extend([ln, s1, s2, s3])
        overlapped([batch(t) for t in range(NBT)])
        zz = add("dve", lambda e: e.memset(node_tile(4), 0.0), [p1])
        NBZ = NB + 1
        for k in range(NSUM):
            for z0 in range(0, NBZ, 6):
                z1 = min(z0 + 6, NBZ)
                tail.append(dma("sp", lambda e, k=k, z0=z0, z1=z1: e.dma_start(
                    scatter_s[k][z0 * P:z1 * P, :].rearrange("(p b) f -> p (b f)", p=P), node_tile(4)[:, 0:(z1 - z0) * XW]), [zz]))
        tail.append(dma("sp", lambda e: e.dma_start(att[:, :], a["c_tril"]), [p1]))
        p2 = source_pass("L1", [tail])

        def transpose_weight(n, src, stage_n, after, pb):
            ld = dma("sp", lambda e: e.dma_start(node_tile(stage_n)[:, 0:P], src), after)
            tp = add("pe", lambda e: e.transpose(bank[pb][:, 0:P], node_tile(stage_n)[:, 0:P], ident[:, :]), [ld])
            return add("act", lambda e: e.copy(wcol(n), bank[pb][:, 0:P]), [tp])

        prog.stage("dense3")
        tw = a["L1_gnn_trans_weight"]
        prm = load_rows([(wcol(2), row_bcast(a["L1_gnn_trans_bias"])), (wcol(3), row_bcast(a["L1_gnn_ln_gamma"])),
                         (wcol(4), row_bcast(a["L1_gnn_ln_beta"])), (wcol(6), row_bcast(a["L2_gnn_b2"])),
                         (wcol(7)[:, 0:1], bass.AP(a["L2_gnn_W1"].tensor, 0, [(1, P), (1, 1)])),
                         (wcol(7)[:, 1:2], bass.AP(a["L2_gnn_W1"].tensor, P, [(1, P), (1, 1)])),
                         (wcol(8)[:, 0:1], bass.AP(a["L2_gnn_b1"].tensor, 0, [(0, P), (1, 1)]))], [p2])
        prm.append(transpose_weight(0, tw[:, 0:P], 4, [p2], 0))
        prm.append(transpose_weight(1, tw[:, P:2 * P], 5, [p2], 1))
        prm.append(transpose_weight(5, a["L2_gnn_W2"], 6, [p2], 2))
        aggT = oh_e[:, :, :].rearrange("p a b -> p (a b)")[:, 0:NBB * P]
        x_free = [[], []]
        hT_read, aggT_read, ps_read, b2_read, b2_copied, recip_free, ln_free, sc_read = (
            [None], [None], [[], []], [None], [None], [None], [None], [None])
        tail = []

        def batch(t):
            x3 = agg[:, t * NBB:(t + 1) * NBB, 0:P]
            sums = [pool_rows[:, (t % 2 * NSUM + k) * NBB * XW:(t % 2 * NSUM + k + 1) * NBB * XW] for k in range(NSUM)]
            lds = [dma("sp", lambda e, t=t, k=k, sums=sums: e.dma_start(sums[k].rearrange("p (b f) -> p b f", b=NBB),
                                                                      blocks(scatter_s[k], t)), [p2, prm, x_free[t % 2]])
                   for k in range(NSUM)]
            h = add("dve", lambda e, sums=sums: e.tensor_tensor(sums[0], sums[0], sums[1], ALU.add), [lds[0], lds[1]])
            h2 = add("dve", lambda e, sums=sums: e.tensor_tensor(sums[2], sums[2], sums[3], ALU.add), [lds[2], lds[3]])
            h = add("dve", lambda e, sums=sums: e.tensor_tensor(sums[0], sums[0], sums[2], ALU.add), [h, h2])
            s3d = sums[0].rearrange("p (b f) -> p b f", b=NBB)
            h = add("dve", lambda e, s3d=s3d: e.tensor_scalar(recip[:, 0:NBB], s3d[:, :, P + 1], 1e-20, None, ALU.add), [h, recip_free])
            h = add("dve", lambda e: e.reciprocal(recip[:, 0:NBB], recip[:, 0:NBB]), [h])
            a3 = s3d[:, :, 0:P]
            h = add("dve", lambda e, a3=a3: e.tensor_tensor(a3, a3, view(recip[:, :], [(1, NBB), (0, P)]), ALU.mult), [h])
            recip_free[0] = h
            yield
            tx = transposed(x3, 0, [prm], [hT_read], hT[0])
            ta = []
            for q, (lo, hi) in enumerate(((0, 4), (4, NBB))):
                for k in range(lo, hi):
                    tp = add("pe", lambda e, k=k, q=q, lo=lo, a3=a3: e.transpose(bank[2 + q][:, (k - lo) * P:(k - lo + 1) * P],
                                                                                a3[:, k, :], ident[:, :]), [h, aggT_read, b2_read])
                ta.append(add("act", lambda e, q=q, lo=lo, hi=hi: e.copy(aggT[:, lo * P:hi * P], bank[2 + q][:, 0:(hi - lo) * P]),
                              [tp, aggT_read]))
            evs, mms = [], []
            for q, (lo, hi) in enumerate(((0, 4), (4, NBB))):
                for k in range(lo, hi):
                    o = bank[4 + q][:, (k - lo) * P:(k - lo + 1) * P]
                    add("pe", lambda e, k=k, o=o: e.matmul(o, hT[0][:, k * P:(k + 1) * P], wcol(0), start=True, stop=False),
                        [tx, ta, prm, ps_read[q]])
                    mm = add("pe", lambda e, k=k, o=o: e.matmul(o, aggT[:, k * P:(k + 1) * P], wcol(1), start=False, stop=True), [])
                mms.append(mm)
            hT_read[0] = aggT_read[0] = mm
            b2_copied[0] = ta
            yield
            for q, (lo, hi) in enumerate(((0, 4), (4, NBB))):
                evs.append(add("dve", lambda e, q=q, lo=lo, hi=hi, a3=a3: e.tensor_tensor(
                    a3[:, lo:hi, :], bank[4 + q][:, 0:(hi - lo) * P].rearrange("p (k f) -> p k f", f=P),
                    view(wcol(2), [(0, hi - lo), (1, P)]), ALU.add), [mms[q], ta]))
                ps_read[q] = evs[-1]
            ln = layer_norm(a3, [evs, ln_free])
            g1 = add("dve", lambda e, a3=a3: e.tensor_tensor(a3, a3, bias3(3), ALU.mult), [ln])
            g2 = bias_add(a3, a3, 4, [g1])
            g3 = add("dve", lambda e, a3=a3, x3=x3: e.tensor_tensor(a3, a3, x3, ALU.add), [g2])
            ln = layer_norm(a3, [g3])
            ln_free[0] = ln
            sx = dma("sp", lambda e, t=t, a3=a3: e.dma_start(blocks(res[0], t), a3), [ln])
            yield
            tt = transposed(a3, 0, [ln], [hT_read], hT[0])
            for q, (lo, hi) in enumerate(((0, 4), (4, NBB))):
                for k in range(lo, hi):
                    m1 = add("pe", lambda e, k=k, q=q, lo=lo: e.matmul(bank[6 + q][:, (k - lo) * P:(k - lo + 1) * P],
                                                                       hT[0][:, k * P:(k + 1) * P], wcol(5), start=True, stop=True),
                             [tt, sc_read])
            for k in range(NBB):
                m2 = add("pe", lambda e, k=k: e.matmul(bank[2][:, 2 * k:2 * k + 2], hT[0][:, k * P:(k + 1) * P], wcol(7)[:, 0:2],
                                                       start=True, stop=True), [tt, b2_copied, sc_read])
            hT_read[0] = m2
            x_free[t % 2] = [tt, sx]
            e1 = [add("dve", lambda e, q=q, lo=lo, hi=hi, x3=x3: e.tensor_tensor(
                x3[:, lo:hi, :], bank[6 + q][:, 0:(hi - lo) * P].rearrange("p (k f) -> p k f", f=P),
                view(wcol(6), [(0, hi - lo), (1, P)]), ALU.add), [m1, sx, tt]) for q, (lo, hi) in enumerate(((0, 4), (4, NBB)))]
            ps = bank[2][:, 0:2 * NBB].rearrange("p (k s) -> p k s", s=2)
            e2 = add("dve", lambda e, t=t, ps=ps: e.tensor_scalar(dst_side[:, t * NBB:(t + 1) * NBB, 0], ps[:, :, 0], wcol(8)[:, 0:1], None,
                                                                 ALU.add), [m2])
            e3 = add("dve", lambda e, t=t, ps=ps: e.tensor_copy(agg[:, t * NBB:(t + 1) * NBB, P], ps[:, :, 1]), [m2])
            sc_read[0] = [e1, e2, e3]
            b2_read[0] = [e2, e3]
            st = dma("sp", lambda e, t=t: e.dma_start(blocks(gather_s2, t), agg[:, t * NBB:(t + 1) * NBB, 0:P + 1]), [e1, e3])
            tail.extend([st, sx, e1, e2, e3])
        overlapped([batch(t) for t in range(NBT)])
        p3 = edge_pass("L2", gather_s2, 1, False, [tail])

        prog.stage("dense4")
        prm = [transpose_weight(k, a["L2_gnn_w_ih"][k * P:(k + 1) * P, :], 4 + k, [p3], k) for k in range(3)]
        prm += [transpose_weight(3 + k, a["L2_gnn_w_hh"][k * P:(k + 1) * P, :], 7 + k if k < 2 else 3, [p3], 3 + k) for k in range(3)]
        prm += load_rows([(wcol(6, 3), row_bcast(a["L2_gnn_b_ih"], 0, 3 * P)), (lrelu[:, 0, 0:3 * P], row_bcast(a["L2_gnn_b_hh"], 0, 3 * P)),
                          (wcol(9), a["L3_gnn_W_src"]), (wcol(10), a["L3_gnn_W_dst"]),
                          (att[:, :], row_bcast(a["L3_gnn_attn"]))], [p3])
        prm.append(add("dve", lambda e: e.tensor_tensor(wcol(6, 2), wcol(6, 2), lrelu[:, 0, 0:2 * P], ALU.add), [prm]))
        bhn = lrelu[:, 0, 2 * P:3 * P]
        oeT = oh_e[:, :, :].rearrange("p a b -> p (a b)")[:, 0:NBB * P]
        rz = tile3(4), tile3(5)
        tmp3, msk3 = tile3(6), tile3(7)
        exp3 = flat3(oh_t)[:, 0:NBB * P].rearrange("p (b f) -> p b f", b=NBB)
        kept3 = flat3(xw)[:, 64:64 + NBB * P].rearrange("p (b f) -> p b f", b=NBB)
        mask = xw[:, 0, 0:NBB]
        nmask = xw[:, 0, 16:16 + NBB]
        x_free, st_free = [[], []], [[], []]
        entry_free, hT_read, oeT_read, gates_free, bank_free = [None], [None], [None], [None], [[]] * 4
        tail = []

        def batch(t):
            a3 = agg[:, t * NBB:(t + 1) * NBB, 0:P]
            x3 = tile3(t % 2)
            ld = dma("sp", lambda e, t=t, x3=x3: e.dma_start(x3, blocks(res[0], t)), [p3, prm, x_free[t % 2]])
            mk = add("dve", lambda e, t=t: e.tensor_scalar(mask, agg[:, t * NBB:(t + 1) * NBB, P + 1], 0.0, None, ALU.is_gt), [p3, entry_free])
            mk2 = add("dve", lambda e: e.tensor_scalar(nmask, mask, -1.0, 1.0, ALU.mult, ALU.add), [mk])
            h = normalise(t, 1, 0.0, [p3, entry_free], guard=1e-30)
            h1 = add("dve", lambda e, a3=a3: e.tensor_scalar(exp3, a3, 0.0, None, ALU.min), [h, prm, entry_free])
            h2 = add("act", lambda e: e.activation(exp3, exp3, ACT.Exp), [h1])
            h3 = add("dve", lambda e, a3=a3: e.tensor_scalar(a3, a3, 0.0, -1.0, ALU.max, ALU.add), [h1])
            h4 = add("dve", lambda e, a3=a3: e.tensor_tensor(a3, a3, exp3, ALU.add), [h2, h3])
            h5 = add("dve", lambda e, a3=a3: e.tensor_tensor(a3, a3, view(mask, [(1, NBB), (0, P)]), ALU.mult), [h4, mk])
            h6 = add("dve", lambda e, x3=x3: e.tensor_tensor(kept3, x3, view(nmask, [(1, NBB), (0, P)]), ALU.mult), [ld, mk2, entry_free])
            oe = add("dve", lambda e, a3=a3: e.tensor_tensor(a3, a3, kept3, ALU.add), [h5, h6])
            entry_free[0] = oe
            yield
            tx = transposed(x3, 0, [ld, prm], [hT_read], hT[0])
            to = []
            for q, (lo, hi) in enumerate(((0, 4), (4, NBB))):
                for k in range(lo, hi):
                    tp = add("pe", lambda e, k=k, q=q, lo=lo, a3=a3: e.transpose(bank[2 + q][:, (k - lo) * P:(k - lo + 1) * P],
                                                                                a3[:, k, :], ident[:, :]), [oe, oeT_read])
                to.append(add("act", lambda e, q=q, lo=lo, hi=hi: e.copy(oeT[:, lo * P:hi * P], bank[2 + q][:, 0:(hi - lo) * P]),
                              [tp, oeT_read]))
            evs = []
            for k in range(NBB):
                B = bank[4 + k % 4]
                wait = [tx, to, prm, bank_free[k % 4]]
                add("pe", lambda e, k=k, B=B: e.matmul(B[:, 0:2 * P], oeT[:, k * P:(k + 1) * P], wcol(0, 2), start=True, stop=False), wait)
                add("pe", lambda e, k=k, B=B: e.matmul(B[:, 0:2 * P], hT[0][:, k * P:(k + 1) * P], wcol(3, 2), start=False, stop=True), [])
                add("pe", lambda e, k=k, B=B: e.matmul(B[:, 2 * P:3 * P], oeT[:, k * P:(k + 1) * P], wcol(2), start=True, stop=True), [])
                mm = add("pe", lambda e, k=k, B=B: e.matmul(B[:, 3 * P:4 * P], hT[0][:, k * P:(k + 1) * P], wcol(5), start=True, stop=True), [])
                v1 = add("dve", lambda e, k=k, B=B: e.tensor_tensor(view(tile3(4)[:, k, :], [(NBB * P, 2), (1, P)]),
                                                                    B[:, 0:2 * P].rearrange("p (s f) -> p s f", s=2),
                                                                    wcol(6, 2).rearrange("p (s f) -> p s f", s=2), ALU.add), [mm, gates_free])
                v2 = add("dve", lambda e, k=k, B=B: e.tensor_tensor(msk3[:, k, :], B[:, 2 * P:3 * P], wcol(8), ALU.add), [mm, gates_free])
                v3 = add("dve", lambda e, k=k, B=B: e.tensor_tensor(tmp3[:, k, :], B[:, 3 * P:4 * P], bhn, ALU.add), [mm, gates_free])
                bank_free[k % 4] = [v1, v2, v3]
                evs.append([v1, v2, v3])
            hT_read[0] = oeT_read[0] = mm
            yield
            r1 = add("act", lambda e: e.activation(view(node_tile(4), [(1, 2 * NBB * P)]), view(node_tile(4), [(1, 2 * NBB * P)]),
                                                   ACT.Tanh, scale=0.5), [evs])
            r2 = add("dve", lambda e: e.tensor_scalar(view(node_tile(4), [(1, 2 * NBB * P)]), view(node_tile(4), [(1, 2 * NBB * P)]),
                                                      0.5, 0.5, ALU.mult, ALU.add), [r1])
            n1 = add("dve", lambda e: e.tensor_tensor(tmp3, tmp3, rz[0], ALU.mult), [r2])
            n2 = add("dve", lambda e: e.tensor_tensor(tmp3, tmp3, msk3, ALU.add), [n1])
            n3 = add("act", lambda e: e.activation(tmp3, tmp3, ACT.Tanh), [n2])
            o1 = add("dve", lambda e: e.tensor_scalar(rz[0], rz[1], -1.0, 1.0, ALU.mult, ALU.add), [n1, r2])
            o2 = add("dve", lambda e: e.tensor_tensor(tmp3, tmp3, rz[0], ALU.mult), [n3, o1])
            o3 = add("dve", lambda e, x3=x3: e.tensor_tensor(rz[1], rz[1], x3, ALU.mult), [o1])
            o4 = add("dve", lambda e: e.tensor_tensor(tmp3, tmp3, rz[1], ALU.add), [o2, o3])
            o5 = add("dve", lambda e, a3=a3, x3=x3: e.tensor_tensor(a3, tmp3, x3, ALU.add), [o4, to])
            gates_free[0] = o5
            ln = layer_norm(a3, [o5])
            sx = dma("sp", lambda e, t=t, a3=a3: e.dma_start(blocks(res[1], t), a3), [ln])
            yield
            tt = transposed(a3, 0, [ln], [hT_read], hT[0])
            ev, st = two_sided(t, 9, None, None, [tt, prm], list(bank_free), tile3(2 + t % 2), [st_free[t % 2], prm], gather_c, hT[0])
            bank_free[:] = ev
            hT_read[0] = ev
            st_free[t % 2] = [st]
            x_free[t % 2] = [o5, tx, h6]
            tail.extend([st, sx, ev])
        overlapped([batch(t) for t in range(NBT)])
        p4 = edge_pass("L3", gather_c, 8, True, [tail])

        prog.stage("dense5")
        prm = load_rows([(wcol(0), a["L3_gnn_W_out"]), (wcol(1), row_bcast(a["L3_gnn_b_out"])),
                         (wcol(2), row_bcast(a["L3_gnn_gamma"])), (wcol(3), row_bcast(a["L3_gnn_beta"]))], [p4])
        x_free, n_free = [[], []], [[], []]
        recip_free, ps_read, ht_read, ln_free = [None], [[], []], [None], [None]
        tail = []

        def batch(t):
            a3 = agg[:, t * NBB:(t + 1) * NBB, 0:P]
            x3, n3_ = tile3(t % 2), tile3(2 + t % 2)
            ld = dma("sp", lambda e, t=t, x3=x3: e.dma_start(x3, blocks(res[1], t)), [p4, x_free[t % 2]])
            h = normalise(t, 8, 1e-8, [p4, recip_free])
            hw = P // 8
            muls = []
            for k in range(NBB):
                muls.append(add("dve", lambda e, k=k, t=t, n3_=n3_: e.tensor_tensor(
                    n3_[:, k, :].rearrange("p (h d) -> p h d", h=8), view(agg[:, t * NBB + k, :], [(hw + 1, 8), (1, hw)]),
                    view(recip[:, k * 8:], [(1, 8), (0, hw)]), ALU.mult), [h, n_free[t % 2]]))
            recip_free[0] = muls
            yield
            tt = transposed(n3_, 0, [muls, prm], [ht_read], hT[0])
            n_free[t % 2] = tt
            evs, mms = [], []
            for q, (lo, hi) in enumerate(((0, 4), (4, NBB))):
                for k in range(lo, hi):
                    mm = add("pe", lambda e, k=k, q=q, lo=lo: e.matmul(bank[4 + q][:, (k - lo) * P:(k - lo + 1) * P],
                                                                       hT[0][:, k * P:(k + 1) * P], wcol(0), start=True, stop=True),
                             [tt, prm, ps_read[q]])
                mms.append(mm)
            ht_read[0] = mm
            yield
            for q, (lo, hi) in enumerate(((0, 4), (4, NBB))):
                evs.append(add("dve", lambda e, q=q, lo=lo, hi=hi, a3=a3: e.tensor_tensor(
                    a3[:, lo:hi, :], bank[4 + q][:, 0:(hi - lo) * P].rearrange("p (k f) -> p k f", f=P),
                    view(wcol(1), [(0, hi - lo), (1, P)]), ALU.add), [mms[q], muls]))
                ps_read[q] = evs[-1]
            h = add("dve", lambda e, a3=a3, x3=x3: e.tensor_tensor(a3, a3, x3, ALU.add), [evs, ld])
            ln = layer_norm(a3, [h, ln_free])
            h = add("dve", lambda e, a3=a3: e.tensor_tensor(a3, a3, bias3(2), ALU.mult), [ln])
            h = bias_add(a3, a3, 3, [h])
            h = add("dve", lambda e, a3=a3, x3=x3: e.tensor_tensor(a3, a3, x3, ALU.add), [h])
            x_free[t % 2] = h
            ln = layer_norm(a3, [h])
            ln_free[0] = ln
            lo, hi = t * NBB * P, (t + 1) * NBB * P
            if hi <= N:
                tail.append(dma("sp", lambda e, a3=a3, lo=lo, hi=hi: e.dma_start(out[lo:hi, :].rearrange("(b p) f -> p b f", p=P), a3), [ln]))
            else:
                full = (N - lo) // P
                rem = N - lo - full * P
                if full:
                    tail.append(dma("sp", lambda e, a3=a3, lo=lo, full=full: e.dma_start(
                        out[lo:lo + full * P, :].rearrange("(b p) f -> p b f", p=P), a3[:, 0:full, :]), [ln]))
                if rem:
                    tail.append(dma("sp", lambda e, a3=a3, lo=lo, full=full, rem=rem: e.dma_start(
                        out[lo + full * P:N, :], a3[0:rem, full, :]), [ln]))
        overlapped([batch(t) for t in range(NBT)])
        prog.queue["sp"].append(lambda eng, last, w=list(flat(tail)): [eng.wait_ge(x.sem, x.value) for x in w])

        block = ctx.enter_context(nc.Block())

        @block.sync
        def _(eng):
            prog.play("sp", eng)

        @block.gpsimd
        def _(eng):
            prog.play("pool", eng)

        @block.scalar
        def _(eng):
            prog.play("act", eng)

        @block.vector
        def _(eng):
            prog.play("dve", eng)

        @block.tensor
        def _(eng):
            prog.play("pe", eng)


def kernel(**inputs):
    import numpy as _np
    import concourse.bacc as _bacc
    from concourse import mybir as _mybir
    from concourse.bass_utils import run_bass_kernel_spmd as _run

    x = _np.ascontiguousarray(inputs["x"])
    n_nodes, n_edges = x.shape[0], inputs["src"].shape[0]
    nb = -(-n_nodes // P)
    t_real = -(-n_edges // P)
    sc = -(-(t_real + nb) // P)
    pad = sc * P * P - n_edges
    src = _np.concatenate([_np.asarray(inputs["src"]), _np.full(pad, nb * P - 1, _np.int32)]).reshape(sc * P, P)
    dst = _np.concatenate([_np.asarray(inputs["dst"]), _np.full(pad, nb * P - 1, _np.int32)]).reshape(sc * P, P)
    arrays = {name: _np.ascontiguousarray(v) for name, v in inputs.items() if name not in ("x", "src", "dst")}
    arrays.update(x=x, src=src, dst=dst)
    k = _np.arange(P)
    arrays["c_ident"] = _np.eye(P, dtype=_np.float32)
    arrays["c_iota"] = _np.tile(k.astype(_np.float32), (P, 1))
    arrays["c_ohw"] = _np.stack([k * 0 + 1, k * 0 + 1, -2 * k, (k * k) // 256 * 256, (k * k) % 256]).astype(_mybir.dt.np(BF16))
    arrays["c_ohs"] = _np.concatenate([_np.stack([k * 0 + 1, k * 0 + 1, -2 * k, k * 0, (k * k) // 256 * 256, (k * k) % 256]),
                                       _np.repeat(_np.array([[0], [0], [1], [1], [0], [0]]), P, 1)], 1).astype(_mybir.dt.np(BF16))
    arrays["c_dump"] = (nb * P + k[:, None]).astype(_np.float32)
    arrays["c_tril"] = (k[None, :] < k[:, None]).astype(_np.float32)
    arrays["c_steps"] = (_np.arange(sc)[None, :] * P + k[:, None]).astype(_np.float32)

    nc = _bacc.Bacc("TRN2", target_bir_lowering=False, num_devices=1)
    feed, args = {}, {"t_real": t_real}
    for name, v in arrays.items():
        feed[f"in_{name}_dram"] = v
        args[name] = nc.dram_tensor(f"in_{name}_dram", v.shape, _mybir.dt.from_np(v.dtype), kind="ExternalInput").ap()
    out = nc.dram_tensor("out_0_dram", x.shape, F32, kind="ExternalOutput").ap()
    build(nc, args, out)
    r = _run(nc, [feed], core_ids=[0])
    return r.results[0]["out_0_dram"]
```
